# Optimizing a Trainium2 kernel written in Bass

```python
import numpy as np
import jax
import jax.numpy as jnp

def _softmax(x, axis=-1):
    return jax.nn.softmax(x, axis=axis)

def _gelu(x):
    return jax.nn.gelu(x, approximate=True)

def _silu(x):
    return jax.nn.silu(x)

def _sigmoid(x):
    return jax.nn.sigmoid(x)

def _layernorm(x, axis=-1, eps=1e-05):
    m = jnp.mean(x, axis=axis, keepdims=True)
    v = jnp.var(x, axis=axis, keepdims=True)
    return (x - m) / jnp.sqrt(v + eps)

def _scatter_add(tgt, idx, src, axis=0):
    return tgt.at[idx].add(src)

def _segment_sum(src, seg, n):
    return jax.ops.segment_sum(src, seg, n)
kernel_name = 'mk_decoder_postln_d1_seqx_r4_f37494'

def setup_inputs(seed: int=0):
    np.random.seed(seed)
    _w = jnp.asarray

    def _rec_inputs():
        import jax
        import jax.numpy as jnp
        _rk = jax.random.key(seed)
        x = -0.0002928 + 1 * jax.random.normal(jax.random.fold_in(_rk, 1), (16, 256, 256), jnp.float32)
        _lenS = 256 - jax.random.randint(jax.random.fold_in(_rk, 7), (16,), 0, max(1, 256 // 4) + 1, jnp.int32)
        _lenS2 = 77 - jax.random.randint(jax.random.fold_in(_rk, 8), (16,), 0, max(1, 77 // 4) + 1, jnp.int32)
        _ctx_1024P = jax.random.normal(jax.random.fold_in(_rk, 11), (16, 16, 256), jnp.float32)
        _ctx_1024c = jax.random.dirichlet(jax.random.fold_in(_rk, 511), 0.3 * jnp.ones((16,), jnp.float32), (16, 77))
        _ctx_1024t = jnp.einsum('bsk,bkd->bsd', _ctx_1024c, _ctx_1024P)
        _ctx_1024t = _ctx_1024t * jax.lax.rsqrt(jnp.mean(jnp.square(_ctx_1024t)) + 1e-12) * 0.953939
        ctx_1024 = -1.39393e-06 + 0.999914 * (_ctx_1024t + 0.3 * jax.random.normal(jax.random.fold_in(_rk, 611), (16, 77, 256), jnp.float32))
        _validS = jnp.arange(256)[None, :] < _lenS[:, None]
        _validS2 = jnp.arange(77)[None, :] < _lenS2[:, None]
        _causal = jnp.tril(jnp.ones((256, 256), dtype=bool))
        mask_BxS2_bk0 = jnp.logical_not(jnp.broadcast_to(_validS2[:, :], (16, 77)))
        return (x, ctx_1024, mask_BxS2_bk0)
    x, ctx_1024, mask_BxS2_bk0 = _rec_inputs()

    def _L0_attn_setup():
        import jax, jax.numpy as jnp
        import numpy as np
        D_MODEL = 256
        D_STATE = 16
        D_CONV = 4
        EXPAND = 2
        D_INNER = D_MODEL * EXPAND
        LN_EPS = 1e-05

        def _selective_scan(xc, deltaA, Bm, Cm):
            b, _, di = xc.shape
            n = Bm.shape[-1]
            h0 = jnp.zeros((b, di, n), xc.dtype)

            def step(h, inp):
                xt, bt, ct = inp
                h = deltaA[None] * h + xt[:, :, None] * bt[:, None, :]
                y = jnp.einsum('bin,bn->bi', h, ct)
                return (h, y)
            xs = (jnp.swapaxes(xc, 0, 1), jnp.swapaxes(Bm, 0, 1), jnp.swapaxes(Cm, 0, 1))
            _, ys = jax.lax.scan(step, h0, xs)
            return jnp.swapaxes(ys, 0, 1)
        key = jax.random.key(seed)
        ks = jax.random.split(key, 12)
        s = lambda fan_in: 1.0 / np.sqrt(fan_in)
        return {'x': jax.random.normal(ks[0], (4, 512, D_MODEL), dtype=jnp.float32), 'ln_w': jnp.ones((D_MODEL,), jnp.float32), 'ln_b': jnp.zeros((D_MODEL,), jnp.float32), 'W_in': jax.random.uniform(ks[1], (D_MODEL, 2 * D_INNER), jnp.float32, -s(D_MODEL), s(D_MODEL)), 'b_in': jax.random.uniform(ks[2], (2 * D_INNER,), jnp.float32, -s(D_MODEL), s(D_MODEL)), 'conv_w': jax.random.uniform(ks[3], (D_INNER, 1, D_CONV), jnp.float32, -s(D_CONV), s(D_CONV)), 'conv_b': jax.random.uniform(ks[4], (D_INNER,), jnp.float32, -s(D_CONV), s(D_CONV)), 'A_log': jax.random.normal(ks[5], (D_INNER, D_STATE), jnp.float32), 'D': jax.random.normal(ks[6], (D_INNER,), jnp.float32), 'W_x': jax.random.uniform(ks[7], (D_INNER, 2 * D_STATE), jnp.float32, -s(D_INNER), s(D_INNER)), 'b_x': jax.random.uniform(ks[8], (2 * D_STATE,), jnp.float32, -s(D_INNER), s(D_INNER)), 'W_out': jax.random.uniform(ks[9], (D_INNER, D_MODEL), jnp.float32, -s(D_INNER), s(D_INNER)), 'b_out': jax.random.uniform(ks[10], (D_MODEL,), jnp.float32, -s(D_INNER), s(D_INNER))}
    _L0_attn_all = _L0_attn_setup()
    _L0_attn_in = {k: v for k, v in _L0_attn_all.items() if k in ('ln_w', 'ln_b', 'W_in', 'b_in', 'conv_w', 'conv_b', 'A_log', 'D', 'W_x', 'b_x', 'W_out', 'b_out')}
    del _L0_attn_all

    def _L0_xattn_setup():
        import jax, jax.numpy as jnp
        import numpy as np
        HEADS = 16
        DIM_HEAD = 64
        QUERY_DIM = 256
        CONTEXT_DIM = 256
        INNER = HEADS * DIM_HEAD
        key = jax.random.key(seed)
        k1, k2, k3, k4, k5, k6, k7 = jax.random.split(key, 7)
        b, nq, nk = (2, 512, 512)
        q = jax.random.normal(k1, (b, nq, QUERY_DIM), dtype=jnp.float32)
        context = jax.random.normal(k2, (b, nk, CONTEXT_DIM), dtype=jnp.float32)
        mask = jax.random.randint(k3, (b, nk), 0, 2).astype(bool) & jax.random.randint(k7, (b, nk), 0, 2).astype(bool)
        s = 0.02
        Wq = jax.random.normal(k4, (QUERY_DIM, INNER), dtype=jnp.float32) * s
        Wkv = jax.random.normal(k5, (CONTEXT_DIM, 2 * INNER), dtype=jnp.float32) * s
        Wout = jax.random.normal(k6, (INNER, QUERY_DIM), dtype=jnp.float32) * s
        b_out = jnp.zeros((QUERY_DIM,), dtype=jnp.float32)
        return {'q': q, 'context': context, 'mask': mask, 'Wq': Wq, 'Wkv': Wkv, 'Wout': Wout, 'b_out': b_out}
    _L0_xattn_all = _L0_xattn_setup()
    _L0_xattn_in = {k: v for k, v in _L0_xattn_all.items() if k in ('Wq', 'Wkv', 'Wout', 'b_out')}
    del _L0_xattn_all

    def _L0_ffn_setup():
        import jax, jax.numpy as jnp
        import numpy as np
        DIM, E, K, H = (256, 8, 2, 1024)
        key = jax.random.key(seed)
        ks = jax.random.split(key, 5)
        s_in = 1.0 / np.sqrt(DIM)
        s_h = 1.0 / np.sqrt(H)
        return {'x': jax.random.normal(ks[0], (4, 512, DIM), dtype=jnp.float32), 'Wr': jax.random.normal(ks[1], (DIM, E), dtype=jnp.float32) * s_in, 'W1': jax.random.normal(ks[2], (E, DIM, H), dtype=jnp.float32) * s_in, 'b1': jnp.zeros((E, H), dtype=jnp.float32), 'W2': jax.random.normal(ks[3], (E, H, DIM), dtype=jnp.float32) * s_h, 'b2': jnp.zeros((E, DIM), dtype=jnp.float32)}
    _L0_ffn_all = _L0_ffn_setup()
    _L0_ffn_in = {k: v for k, v in _L0_ffn_all.items() if k in ('Wr', 'W1', 'b1', 'W2', 'b2')}
    del _L0_ffn_all
    return {'x': x, 'ctx_1024': ctx_1024, 'mask_BxS2_bk0': mask_BxS2_bk0, 'L0_attn_ln_w': _L0_attn_in['ln_w'], 'L0_attn_ln_b': _L0_attn_in['ln_b'], 'L0_attn_W_in': _L0_attn_in['W_in'], 'L0_attn_b_in': _L0_attn_in['b_in'], 'L0_attn_conv_w': _L0_attn_in['conv_w'], 'L0_attn_conv_b': _L0_attn_in['conv_b'], 'L0_attn_A_log': _L0_attn_in['A_log'], 'L0_attn_D': _L0_attn_in['D'], 'L0_attn_W_x': _L0_attn_in['W_x'], 'L0_attn_b_x': _L0_attn_in['b_x'], 'L0_attn_W_out': _L0_attn_in['W_out'], 'L0_attn_b_out': _L0_attn_in['b_out'], 'L0_xattn_Wq': _L0_xattn_in['Wq'], 'L0_xattn_Wkv': _L0_xattn_in['Wkv'], 'L0_xattn_Wout': _L0_xattn_in['Wout'], 'L0_xattn_b_out': _L0_xattn_in['b_out'], 'L0_ffn_Wr': _L0_ffn_in['Wr'], 'L0_ffn_W1': _L0_ffn_in['W1'], 'L0_ffn_b1': _L0_ffn_in['b1'], 'L0_ffn_W2': _L0_ffn_in['W2'], 'L0_ffn_b2': _L0_ffn_in['b2']}

def reference(x, ctx_1024, mask_BxS2_bk0, L0_attn_ln_w, L0_attn_ln_b, L0_attn_W_in, L0_attn_b_in, L0_attn_conv_w, L0_attn_conv_b, L0_attn_A_log, L0_attn_D, L0_attn_W_x, L0_attn_b_x, L0_attn_W_out, L0_attn_b_out, L0_xattn_Wq, L0_xattn_Wkv, L0_xattn_Wout, L0_xattn_b_out, L0_ffn_Wr, L0_ffn_W1, L0_ffn_b1, L0_ffn_W2, L0_ffn_b2):
    import jax
    import jax.numpy as jnp

    def _L0_attn_ref(x, ln_w, ln_b, W_in, b_in, conv_w, conv_b, A_log, D, W_x, b_x, W_out, b_out):
        import jax, jax.numpy as jnp
        import numpy as np
        D_MODEL = 256
        D_STATE = 16
        D_CONV = 4
        EXPAND = 2
        D_INNER = D_MODEL * EXPAND
        LN_EPS = 1e-05

        def _selective_scan(xc, deltaA, Bm, Cm):
            b, _, di = xc.shape
            n = Bm.shape[-1]
            h0 = jnp.zeros((b, di, n), xc.dtype)

            def step(h, inp):
                xt, bt, ct = inp
                h = deltaA[None] * h + xt[:, :, None] * bt[:, None, :]
                y = jnp.einsum('bin,bn->bi', h, ct)
                return (h, y)
            xs = (jnp.swapaxes(xc, 0, 1), jnp.swapaxes(Bm, 0, 1), jnp.swapaxes(Cm, 0, 1))
            _, ys = jax.lax.scan(step, h0, xs)
            return jnp.swapaxes(ys, 0, 1)
        residual = x
        mu = jnp.mean(x, -1, keepdims=True)
        var = jnp.mean((x - mu) ** 2, -1, keepdims=True)
        xn = (x - mu) * jax.lax.rsqrt(var + LN_EPS) * ln_w + ln_b
        xg = xn @ W_in + b_in
        x_main, gate = jnp.split(xg, 2, axis=-1)
        xt = jnp.swapaxes(x_main, 1, 2)
        xc = jax.lax.conv_general_dilated(xt, conv_w, window_strides=(1,), padding=[(D_CONV - 1, 0)], feature_group_count=D_INNER, dimension_numbers=('NCH', 'OIH', 'NCH'))
        xc = xc + conv_b[None, :, None]
        x_conv = jax.nn.silu(jnp.swapaxes(xc, 1, 2))
        ssm = x_conv @ W_x + b_x
        Bm, Cm = jnp.split(ssm, 2, axis=-1)
        deltaA = jnp.exp(-jnp.exp(A_log))
        y = _selective_scan(x_conv, deltaA, Bm, Cm)
        y = y + x_conv * D[None, None, :]
        y = y * jax.nn.silu(gate)
        out = y @ W_out + b_out
        return out + residual

    def _L0_xattn_ref(q, context, mask, Wq, Wkv, Wout, b_out):
        import jax, jax.numpy as jnp
        import numpy as np
        HEADS = 16
        DIM_HEAD = 64
        QUERY_DIM = 256
        CONTEXT_DIM = 256
        INNER = HEADS * DIM_HEAD
        b, nq, _ = q.shape
        nk = context.shape[1]
        h, dh = (HEADS, DIM_HEAD)
        scale = dh ** (-0.5)
        qp = q @ Wq
        k, v = jnp.split(context @ Wkv, 2, -1)
        qh = qp.reshape(b, nq, h, dh).transpose(0, 2, 1, 3)
        kh = k.reshape(b, nk, h, dh).transpose(0, 2, 1, 3)
        vh = v.reshape(b, nk, h, dh).transpose(0, 2, 1, 3)
        attn = jnp.einsum('bhid,bhjd->bhij', qh, kh) * scale
        attn = jnp.where(mask[:, None, None, :], -jnp.inf, attn)
        attn = jax.nn.softmax(attn, axis=-1)
        out = jnp.einsum('bhij,bhjd->bhid', attn, vh)
        out = out.transpose(0, 2, 1, 3).reshape(b, nq, h * dh)
        return out @ Wout + b_out

    def _L0_ffn_ref(x, Wr, W1, b1, W2, b2):
        import jax, jax.numpy as jnp
        import numpy as np
        DIM, E, K, H = (256, 8, 2, 1024)
        batch, seq, dim = x.shape
        x_flat = x.reshape(-1, dim)
        logits = x_flat @ Wr
        w, ind = jax.lax.top_k(logits, K)
        w = jax.nn.softmax(w, axis=-1)
        combine = jnp.einsum('tke,tk->te', jax.nn.one_hot(ind, E, dtype=x.dtype), w)

        def body(acc, params):
            W1e, b1e, W2e, b2e, ce = params
            h = jax.nn.gelu(x_flat @ W1e + b1e, approximate=False)
            y = h @ W2e + b2e
            return (acc + ce[:, None] * y, None)
        out0 = jnp.zeros_like(x_flat)
        out, _ = jax.lax.scan(body, out0, (W1, b1, W2, b2, combine.T))
        return out.reshape(batch, seq, dim)
    x = _layernorm(x + _L0_attn_ref(x, L0_attn_ln_w, L0_attn_ln_b, L0_attn_W_in, L0_attn_b_in, L0_attn_conv_w, L0_attn_conv_b, L0_attn_A_log, L0_attn_D, L0_attn_W_x, L0_attn_b_x, L0_attn_W_out, L0_attn_b_out), axis=-1)
    x = _layernorm(x + _L0_xattn_ref(x, ctx_1024, mask_BxS2_bk0, L0_xattn_Wq, L0_xattn_Wkv, L0_xattn_Wout, L0_xattn_b_out), axis=-1)
    x = _layernorm(x + _L0_ffn_ref(x, L0_ffn_Wr, L0_ffn_W1, L0_ffn_b1, L0_ffn_W2, L0_ffn_b2), axis=-1)
    return x

_drawn_inputs = setup_inputs


def setup_inputs(seed=0):
    import zlib

    import numpy as np

    out = dict(_drawn_inputs(seed))
    spreads = {'L0_attn_ln_w': (1.0, 0.537),
     'L0_attn_ln_b': (0.0, 0.377),
     'L0_xattn_b_out': (0.0, 0.1),
     'L0_ffn_b1': (0.0, 0.1),
     'L0_ffn_b2': (0.0, 0.1)}
    factors = {'L0_attn_b_in': 5.896,
     'L0_attn_A_log': 4.187,
     'L0_attn_W_x': 4.161,
     'L0_attn_b_x': 6.591,
     'L0_xattn_Wq': 3.216}
    for name, (base, spread) in spreads.items():
        noise = np.random.default_rng([zlib.crc32(name.encode()), seed]).standard_normal(out[name].shape)
        drawn = base * np.exp(spread * noise) if base else spread * noise
        out[name] = jnp.asarray(drawn.astype(out[name].dtype))
    for name, factor in factors.items():
        out[name] = (out[name] * factor).astype(out[name].dtype)
    return out
```

```python
import concourse.bass as bass
from concourse import mybir
from contextlib import ExitStack
import numpy as np

fp32 = mybir.dt.float32
bf16 = mybir.dt.bfloat16
u32 = mybir.dt.uint32
ALU = mybir.AluOpType
ACT = mybir.ActivationFunctionType
AX = mybir.AxisListType

B, S, D = 16, 256, 256
P = 128
NT = B * S // P
DK = D // P
EPS = 1e-5

DI, NS, TAPS = 512, 16, 4
CT = DI // P
NPAIR = B // 2
TP = 2 * S
TT = TP // P
PADW = S + TAPS - 1
NBC = 2 * NS
U_XT, U_WIN, U_CONV, U_WX, U_FRONT = 0, DK, DK + 2 * CT, DK + 3 * CT, DK + 3 * CT + 1
U_OUT = 2
BLEAD, BRING, URING = 3, 4, 4

def front_unit(q, k):
    if isinstance(q, int) and q == 0:
        return k
    return q * (U_FRONT + U_OUT) - U_OUT + k

def out_unit(p, k):
    last = isinstance(p, int) and p == NPAIR - 1
    return (p + 1) * (U_FRONT + U_OUT) + (0 if last else U_FRONT) - U_OUT + k

def mixer(nc, ctx, t):
    def sb(name, shape, dt=fp32):
        return ctx.enter_context(nc.sbuf_tensor(name, shape, dt))

    def sem(name):
        return ctx.enter_context(nc.semaphore(name))

    xs, ident, mv0, mv1, rstd, nbias, tmpv = t["xs"], t["ident"], t["mv0"], t["mv1"], t["rstd"], t["nbias"], t["tmpv"]
    win = sb("win", [P, DK, 2 * DI])
    wout = sb("wout", [P, CT, D])
    wx3 = sb("wx3", [P, CT, 3 * NBC])
    bx3 = sb("bx3", [3 * NBC, 1])
    bin_ = sb("bin", [P, 2 * CT])
    lnw = sb("lnw", [P, DK])
    lnb = sb("lnb", [P, DK])
    cw = sb("cw", [P, CT, TAPS])
    cb = sb("cb", [P, CT])
    dsk = sb("dsk", [P, CT])
    alog = sb("alog", [P, CT, NS])
    bob = sb("bob", [P, D])
    cdiag = sb("cdiag", [P, CT, TAPS, P])
    ddiag = sb("ddiag", [P, CT, P])
    sel0 = sb("sel0", [3 * NBC, NBC], bf16)
    sel = sb("sel", [3 * NBC, NBC, P], bf16)
    xn = sb("xn", [P, TT, D])
    xnT = sb("xnT", [P, DK, TP])
    xm = sb("xm", [P, CT, 2, PADW])
    gs = sb("gs", [P, 2, CT, TP])
    xc = sb("xc", [P, 2, CT, TP])
    ssm = sb("ssm", [3 * NBC, TP])
    rest = sb("rest", [3 * NBC, TP])
    parts = sb("parts", [3 * NBC, 2, TP], bf16)
    bring = sb("bring", [P, BRING, TP])
    u = sb("u", [P, URING, CT, TP])
    h = sb("h", [P, 2, CT, TP])
    hc = sb("hc", [P, 2, CT, TP])
    yg = sb("yg", [P, CT, TP])
    otmp = sb("otmp", [P, TT, D])
    bst = sb("bst", [P, TT, 6])
    mvt = sb("mvt", [P, TT, 2])

    y = ctx.enter_context(nc.psum_tensor("y", [P, CT, TP], fp32))
    fb = [ctx.enter_context(nc.psum_tensor(f"fb{i}", [P, TP], fp32)) for i in range(2)]
    bbank = ctx.enter_context(nc.psum_tensor("bbank", [P, TP], fp32))
    cbank = ctx.enter_context(nc.psum_tensor("cbank", [P, TP], fp32))

    loaded = sem("m_loaded")
    xloaded = [sem(f"m_xloaded{i}") for i in range(2)]
    made = sem("m_made")
    tables = sem("m_tables")
    adecay = sem("m_adecay")
    stats = sem("m_stats")
    rooted = sem("m_rooted")
    xn_ready = sem("m_xn")
    fb_full = sem("m_fb_full")
    fb_free = sem("m_fb_free")
    split1 = sem("m_split1")
    split2 = sem("m_split2")
    b_sent = sem("m_b_sent")
    b_kept = sem("m_b_kept")
    u_ready = sem("m_u")
    h_ready = sem("m_h")
    c_sent = sem("m_c_sent")
    hc_ready = sem("m_hc")
    summed = sem("m_summed")
    gated = sem("m_gated")
    z_steps = sem("m_z")

    z_seen = sem("m_z_seen")
    mv_kept = sem("m_mv_kept")
    zero_made = sem("m_zero_made")
    zero_sent = sem("m_zero_sent")
    zero = sb("zero", [P, D])

    N_LOADS = 16
    block = ctx.enter_context(nc.Block())

    @block.sync
    def _(sp):
        with nc.allow_non_contiguous_dma(reason="short vectors and tables"):
            xd = t["x"].rearrange("b (h p) d -> p (b h) d", p=P)
            for i in range(2):
                half = slice(i * NT // 2, (i + 1) * NT // 2)
                sp.dma_start(xs[:, half, :], xd[:, half, :]).then_inc(xloaded[i], 16)
            loads = [
                (win[:, :, :], t["W_in"].rearrange("(k p) n -> p k n", p=P)),
                (wout[:, :, :], t["W_out"].rearrange("(k p) n -> p k n", p=P)),
                (bin_[:, :], t["b_in"].rearrange("(m p) -> p m", p=P)),
                (lnw[:, :], t["ln_w"].rearrange("(k p) -> p k", p=P)),
                (lnb[:, :], t["ln_b"].rearrange("(k p) -> p k", p=P)),
                (cw[:, :, :], t["conv_w"].rearrange("(c p) o k -> p c (o k)", p=P)),
                (cb[:, :], t["conv_b"].rearrange("(c p) -> p c", p=P)),
                (dsk[:, :], t["D"].rearrange("(c p) -> p c", p=P)),
                (alog[:, :, :], t["A_log"].rearrange("(c p) n -> p c n", p=P)),
                (bob[:, :], t["b_out"].rearrange("(a n) -> a n", a=1).to_broadcast([P, D])),
            ]
            for g in range(3):
                loads.append((wx3[:, :, g * NBC:(g + 1) * NBC], t["W_x"].rearrange("(c p) n -> p c n", p=P)))
                loads.append((bx3[g * NBC:(g + 1) * NBC, :], t["b_x"].rearrange("(n a) -> n a", a=1)))
            assert len(loads) == N_LOADS
            for dst, src in loads:
                sp.dma_start(dst, src).then_inc(loaded, 16)
        sp.wait_ge(zero_made, 1)
        zeroed = t["xsort"].rearrange("(n p) d -> p n d", p=P)
        sp.dma_start(zeroed, zero[:, :].rearrange("p (a d) -> p a d", a=1).to_broadcast([P, zeroed.shape[1], D])).then_inc(zero_sent, 16)
        sp.wait_ge(zero_sent, 16)

    @block.gpsimd
    def _(pool):
        pool.memset(zero[:, :], 0.0).then_inc(zero_made, 1)
        pool.memset(ident[:, :], 0.0).then_inc(made, 1)
        pool.memset(sel0[:, :], 0.0).then_inc(made, 1)
        pool.memset(xm[:, :, :, :], 0.0).then_inc(made, 1)
        pool.wait_ge(made, 3)
        pool.affine_select(out=ident[:, :], in_=ident[:, :], compare_op=ALU.not_equal, fill=1.0,
                           base=0, pattern=[[-1, P]], channel_multiplier=1).then_inc(made, 1)
        for g in range(3):
            pool.affine_select(out=sel0[:, :], in_=sel0[:, :], compare_op=ALU.not_equal, fill=1.0,
                               base=-g * NBC, pattern=[[-1, NBC]], channel_multiplier=1).then_inc(made, 1)
            pool.wait_ge(made, 5 + g)

        def pair(p, par):
            for n in range(NS):
                i = p * NS + n
                slot = n % BRING
                pool.wait_ge(b_kept, i + 1)
                if not isinstance(i, int) or i >= URING:
                    pool.wait_ge(h_ready, i - URING + 1)
                pool.tensor_tensor(out=u[:, n % URING, :, :], in0=xc[:, par, :, :],
                                   in1=bring[:, slot:slot + 1, :].to_broadcast([P, CT, TP]),
                                   op=ALU.mult).then_inc(u_ready, 1)

        pair(0, 0)
        with pool.Fori(0, NPAIR // 2 - 1) as it:
            pair(it * 2 + 1, 1)
            pair(it * 2 + 2, 0)
        pair(NPAIR - 1, 1)

    @block.vector
    def _(dve):
        dve.sem_inc(z_steps, 4)
        for i in range(NT):
            if i % (NT // 2) == 0:
                dve.wait_ge(xloaded[i // (NT // 2)], 16)
            if i >= TT:
                dve.wait_ge(stats, 2 * (i - TT) + 2)
            dve.bn_stats(bst[:, i % TT, :], xs[:, i, :]).then_inc(stats, 1)
            dve.wait_ge(stats, 2 * i + 1)
            dve.bn_aggr(mv0[:, i, :], bst[:, i % TT, :]).then_inc(stats, 1)
        n = 2 * NT
        dve.wait_ge(stats, n)
        n = rstd_vector(dve, mv0, rstd, nbias, tmpv, stats, rooted, n)
        dve.wait_ge(loaded, 16 * N_LOADS)
        dve.wait_ge(made, 7)
        for c in range(CT):
            for k in range(TAPS):
                dve.tensor_scalar(cdiag[:, c, k, :], ident[:, :], cw[:, c, k:k + 1], None, ALU.mult)
            dve.tensor_scalar(ddiag[:, c, :], ident[:, :], dsk[:, c:c + 1], None, ALU.mult)
        dve.tensor_copy(sel[:, :, :], sel0[:, :].rearrange("p (n a) -> p n a", a=1).to_broadcast([3 * NBC, NBC, P])).then_inc(tables, 1)

        def split(q, par, step):
            if step == 0:
                dve.wait_ge(split2, q * 4 + 2)
                dve.tensor_tensor(out=rest[:, :], in0=ssm[:, :], in1=parts[:, par, :],
                                  op=ALU.subtract).then_inc(split1, 1)
            else:
                dve.wait_ge(split2, q * 4 + 3)
                lo = slice(2 * NBC, 3 * NBC)
                dve.tensor_tensor(out=rest[lo, :], in0=rest[lo, :], in1=parts[lo, par, :],
                                  op=ALU.subtract).then_inc(split1, 1)

        def residual(p, step):
            tiles = bass.ds(p * TT, TT)
            if step == 0:
                dve.wait_ge(fb_free, out_unit(p, 1) + 1)
                dve.scalar_tensor_tensor(out=xs[:, tiles, :], in0=xs[:, tiles, :], scalar=2.0,
                                         in1=otmp[:, :, :], op0=ALU.mult, op1=ALU.add).then_inc(z_steps, 1)
            elif step == 1:
                dve.wait_ge(z_steps, (p + 1) * 4 + 1)
                dve.tensor_tensor(out=xs[:, tiles, :], in0=xs[:, tiles, :],
                                  in1=bob[:, :].rearrange("p (a n) -> p a n", a=1).to_broadcast([P, TT, D]),
                                  op=ALU.add).then_inc(z_steps, 1)
            elif step == 2:
                dve.wait_ge(z_steps, (p + 1) * 4 + 2)
                dve.sem_inc(z_seen, 1)
                for j in range(TT):
                    ins = dve.bn_stats(bst[:, j, :], xs[:, bass.ds(p * TT + j, 1), :])
                ins.then_inc(z_steps, 1)
            elif step == 3:
                dve.wait_ge(z_steps, (p + 1) * 4 + 3)
                if not (isinstance(p, int) and p == 0):
                    dve.wait_ge(mv_kept, p)
                dve.sem_inc(z_seen, 1)
                for j in range(TT):
                    ins = dve.bn_aggr(mvt[:, j, :], bst[:, j, :])
                ins.then_inc(z_steps, 1)
            else:
                dve.wait_ge(z_steps, (p + 1) * 4 + 4)
                dve.tensor_copy(mv1[:, tiles, :], mvt[:, :, :]).then_inc(mv_kept, 1)

        def scan(p, n, par):
            i = p * NS + n
            dve.wait_ge(u_ready, i + 1)
            if not isinstance(i, int) or i >= 2:
                dve.wait_ge(hc_ready, i - 1)
            for c in range(CT):
                for b in range(2):
                    ins = dve.tensor_tensor_scan(
                        out=h[:, n % 2, c, b * S:(b + 1) * S],
                        data0=alog[:, c, n:n + 1].to_broadcast([P, S]),
                        data1=u[:, n % URING, c, b * S:(b + 1) * S],
                        initial=0.0, op0=ALU.mult, op1=ALU.add)
            ins.then_inc(h_ready, 1)

        def times_c(p, n):
            i = p * NS + n
            dve.wait_ge(h_ready, i + 1)
            dve.wait_ge(c_sent, i + 1)
            if not isinstance(i, int) or i >= 2:
                dve.wait_ge(summed, i - 1)
            dve.tensor_tensor(out=hc[:, n % 2, :, :], in0=h[:, n % 2, :, :],
                              in1=cbank[:, :].rearrange("p (a n) -> p a n", a=1).to_broadcast([P, CT, TP]),
                              op=ALU.mult).then_inc(hc_ready, 1)

        def gate(p, par):
            dve.wait_ge(summed, p * NS + NS)
            dve.tensor_tensor(out=yg[:, :, :], in0=y[:, :, :], in1=gs[:, par, :, :],
                              op=ALU.mult).then_inc(gated, 1)

        def pair(p, par, last, before, after):
            for n in range(NS):
                scan(p, n, par)
                if n:
                    times_c(p, n - 1)
                if before and 3 <= n < 8:
                    residual(p - 1, n - 3)
                if after and n == 11:
                    split(p + 1, 1 - par, 0)
                if after and n == 12:
                    split(p + 1, 1 - par, 1)
            times_c(p, NS - 1)
            gate(p, par)

        dve.wait_ge(adecay, 2)
        split(0, 0, 0)
        split(0, 0, 1)
        pair(0, 0, False, False, True)
        with dve.Fori(0, NPAIR // 2 - 1) as it:
            pair(it * 2 + 1, 1, False, True, True)
            pair(it * 2 + 2, 0, False, True, True)
        pair(NPAIR - 1, 1, True, True, False)
        for step in range(5):
            residual(NPAIR - 1, step)

    @block.scalar
    def _(act):
        act.wait_ge(loaded, 16 * N_LOADS)
        act.activation(alog[:, :, :], alog[:, :, :], ACT.Exp).then_inc(adecay, 1)
        act.wait_ge(adecay, 1)
        act.activation(alog[:, :, :], alog[:, :, :], ACT.Exp, scale=-1.0).then_inc(adecay, 1)
        rstd_scalar(act, tmpv, stats, rooted, 2 * NT)
        act.wait_ge(stats, 2 * NT + RSTD_STEPS)
        act.wait_ge(made, 3)

        def take(unit, out, fn, rows=P, **kw):
            bank = unit[1]
            act.wait_ge(fb_full, unit[0] + 1)
            act.activation(out, fb[bank][0:rows, :], fn, **kw).then_inc(fb_free, 1)

        def fu(q, par, k):
            return front_unit(q, k), bank_of(q, par, k)

        def normalise(q):
            for j in range(TT):
                tile = bass.ds(q * TT + j, 1)
                ins = act.activation(xn[:, j, :], xs[:, tile, :], ACT.Identity,
                                     scale=rstd[:, tile], bias=nbias[:, tile])
            ins.then_inc(xn_ready, 1)

        def keep_b(p, n):
            i = p * NS + n
            act.wait_ge(b_sent, i + 1)
            if not isinstance(i, int) or i >= BRING:
                act.wait_ge(u_ready, i - BRING + 1)
            act.activation(bring[:, n % BRING, :], bbank[:, :], ACT.Copy).then_inc(b_kept, 1)

        def front(q, par, step):
            if step == 0:
                normalise(q)
                for k in range(DK):
                    take(fu(q, par, U_XT + k), xnT[:, k, :], ACT.Identity, scale=lnw[:, k:k + 1], bias=lnb[:, k:k + 1])
            elif step <= 2:
                for m in (2 * step - 2, 2 * step - 1):
                    act.wait_ge(fb_full, front_unit(q, U_WIN + m) + 1)
                    act.activation(xm[:, m, :, TAPS - 1:PADW], fb[bank_of(q, par, U_WIN + m)][:, :].rearrange("p (b s) -> p b s", b=2),
                                   ACT.Identity, bias=bin_[:, m:m + 1]).then_inc(fb_free, 1)
            elif step <= 4:
                if not (isinstance(q, int) and q < 2):
                    act.wait_ge(gated, q - 1)
                for m in (2 * step - 2, 2 * step - 1):
                    take(fu(q, par, U_WIN + m), gs[:, par, m - CT, :], ACT.Silu, bias=bin_[:, m:m + 1])
            elif step <= 8:
                c = step - 5
                take(fu(q, par, U_CONV + c), xc[:, par, c, :], ACT.Silu, bias=cb[:, c:c + 1])
            elif step == 9:
                if not (isinstance(q, int) and q == 0):
                    act.wait_ge(split1, q * 2)
                act.wait_ge(fb_full, front_unit(q, U_WX) + 1)
                act.activation(ssm[:, :], fb[bank_of(q, par, U_WX)][0:3 * NBC, :], ACT.Identity,
                               bias=bx3[:, :]).then_inc(split2, 1)
                act.activation(parts[:, par, :], fb[bank_of(q, par, U_WX)][0:3 * NBC, :], ACT.Identity,
                               bias=bx3[:, :]).then_inc(split2, 1)
                act.wait_ge(split2, q * 4 + 2)
                act.sem_inc(fb_free, 1)
            elif step == 10:
                act.wait_ge(split1, q * 2 + 1)
                mid, lo = slice(NBC, 2 * NBC), slice(2 * NBC, 3 * NBC)
                act.activation(parts[mid, par, :], rest[mid, :], ACT.Copy)
                act.activation(parts[lo, par, :], rest[lo, :], ACT.Copy).then_inc(split2, 1)
            else:
                lo = slice(2 * NBC, 3 * NBC)
                act.wait_ge(split1, q * 2 + 2)
                act.activation(parts[lo, par, :], rest[lo, :], ACT.Copy).then_inc(split2, 1)

        def project_out(p, par):
            act.wait_ge(z_steps, p * 4 + 1)
            for k in range(U_OUT):
                act.wait_ge(fb_full, out_unit(p, k) + 1)
                act.activation(otmp[:, 2 * k:2 * k + 2, :],
                               fb[out_bank(p, par, k)][:, :].rearrange("p (a n) -> p a n", a=2),
                               ACT.Copy).then_inc(fb_free, 1)

        def pair(p, par, before, after):
            for n in range(NS):
                if n + BLEAD < NS:
                    keep_b(p, n + BLEAD)
                elif after:
                    keep_b(p + 1, n + BLEAD - NS)
                if before and n == 0:
                    project_out(p - 1, 1 - par)
                if after and 1 <= n < 13:
                    front(p + 1, 1 - par, n - 1)

        for step in range(12):
            front(0, 0, step)
        for n in range(BLEAD):
            keep_b(0, n)
        pair(0, 0, False, True)
        with act.Fori(0, NPAIR // 2 - 1) as it:
            pair(it * 2 + 1, 1, True, True)
            pair(it * 2 + 2, 0, True, True)
        pair(NPAIR - 1, 1, True, False)
        project_out(NPAIR - 1, 1)

    @block.tensor
    def _(pe):
        pe.wait_ge(made, 7)
        pe.wait_ge(tables, 1)
        pe.wait_ge(loaded, 16 * N_LOADS)

        def free_bank(unit):
            if not isinstance(unit, int) or unit >= 2:
                pe.wait_ge(fb_free, unit - 1)

        def front(q, par, step):
            if step == 0:
                pe.wait_ge(xn_ready, q + 1)
                for k in range(DK):
                    free_bank(front_unit(q, U_XT + k))
                    bank = fb[bank_of(q, par, U_XT + k)]
                    for j in range(TT):
                        ins = pe.transpose(bank[:, j * P:(j + 1) * P], xn[:, j, k * P:(k + 1) * P], ident[:, :])
                    ins.then_inc(fb_full, 1)
            elif step <= 4:
                pe.wait_ge(fb_free, front_unit(q, U_XT + DK - 1) + 1)
                for m in (2 * step - 2, 2 * step - 1):
                    free_bank(front_unit(q, U_WIN + m))
                    for k in range(DK):
                        ins = pe.matmul(fb[bank_of(q, par, U_WIN + m)][:, :], win[:, k, m * P:(m + 1) * P],
                                        xnT[:, k, :], start=(k == 0), stop=(k == DK - 1))
                    ins.then_inc(fb_full, 1)
            elif step <= 8:
                c = step - 5
                free_bank(front_unit(q, U_CONV + c))
                for k in range(TAPS):
                    ins = pe.matmul(fb[bank_of(q, par, U_CONV + c)][:, :].rearrange("p (b s) -> p b s", b=2),
                                    cdiag[:, c, k, :], xm[:, c, :, k:k + S],
                                    start=(k == 0), stop=(k == TAPS - 1))
                ins.then_inc(fb_full, 1)
            elif step == 9:
                pe.wait_ge(fb_free, front_unit(q, U_CONV + CT - 1) + 1)
                for c in range(CT):
                    ins = pe.matmul(fb[bank_of(q, par, U_WX)][0:3 * NBC, :], wx3[:, c, :], xc[:, par, c, :],
                                    start=(c == 0), stop=(c == CT - 1))
                ins.then_inc(fb_full, 1)

        def project_out(p, par):
            pe.wait_ge(gated, p + 1)
            for k in range(U_OUT):
                free_bank(out_unit(p, k))
                for a in range(2):
                    j = 2 * k + a
                    for c in range(CT):
                        ins = pe.matmul(fb[out_bank(p, par, k)][:, a * D:(a + 1) * D], yg[:, c, j * P:(j + 1) * P],
                                        wout[:, c, :], start=(c == 0), stop=(c == CT - 1))
                ins.then_inc(fb_full, 1)

        def send_b(p, par, n):
            i = p * NS + n
            if n == 0:
                pe.wait_ge(split2, p * 4 + 4)
            if not isinstance(i, int) or i >= 1:
                pe.wait_ge(b_kept, i)
            pe.matmul(bbank[:, :], sel[:, n, :], parts[:, par, :], start=True, stop=True).then_inc(b_sent, 1)

        def send_c(p, par, n):
            i = p * NS + n
            if not isinstance(i, int) or i >= 1:
                pe.wait_ge(hc_ready, i)
            pe.matmul(cbank[:, :], sel[:, NS + n, :], parts[:, par, :], start=True, stop=True).then_inc(c_sent, 1)

        def add_up(p, n):
            pe.wait_ge(hc_ready, p * NS + n + 1)
            for c in range(CT):
                ins = pe.matmul(y[:, c, :], ident[:, :], hc[:, n % 2, c, :], start=False, stop=(n == NS - 1))
            ins.then_inc(summed, 1)

        def skip(p, par):
            if not (isinstance(p, int) and p == 0):
                pe.wait_ge(gated, p)
            for c in range(CT):
                pe.matmul(y[:, c, :], ddiag[:, c, :], xc[:, par, c, :], start=True, stop=False)

        def pair(p, par, before, after):
            for n in range(NS):
                send_c(p, par, n)
                if n == 0:
                    skip(p, par)
                else:
                    add_up(p, n - 1)
                if n + BLEAD < NS:
                    send_b(p, par, n + BLEAD)
                elif after:
                    send_b(p + 1, 1 - par, n + BLEAD - NS)
                if before and n == 0:
                    project_out(p - 1, 1 - par)
                if after and 1 <= n < 13:
                    front(p + 1, 1 - par, n - 1)
            add_up(p, NS - 1)

        for step in range(10):
            front(0, 0, step)
        for n in range(BLEAD):
            send_b(0, 0, n)
        pair(0, 0, False, True)
        with pe.Fori(0, NPAIR // 2 - 1) as it:
            pair(it * 2 + 1, 1, True, True)
            pair(it * 2 + 2, 0, True, True)
        pair(NPAIR - 1, 1, True, False)
        project_out(NPAIR - 1, 1)

def bank_of(q, par, k):
    if isinstance(q, int):
        return front_unit(q, k) % 2
    return (par * (U_FRONT + U_OUT) - U_OUT + k) % 2

def out_bank(p, par, k):
    if isinstance(p, int):
        return out_unit(p, k) % 2
    return ((par + 1) * (U_FRONT + U_OUT) + U_FRONT - U_OUT + k) % 2

RSTD_STEPS = 8

def rstd_scalar(act, tmpv, stats, rooted, n, cols=slice(0, NT)):
    act.wait_ge(stats, n + 1)
    act.activation(tmpv[:, 1, cols], tmpv[:, 0, cols], ACT.Sqrt).then_inc(rooted, 1)

def rstd_vector(dve, mv, rstd, nbias, tmpv, stats, rooted, n, cols=slice(0, NT), turn=1):
    var, root, a, b = (tmpv[:, k, cols] for k in range(4))
    at = n

    def link(ins):
        nonlocal at
        at += 1
        ins.then_inc(stats, 1)
        dve.wait_ge(stats, at)

    link(dve.tensor_scalar(var, mv[:, cols, 1], EPS, None, ALU.add))
    dve.wait_ge(rooted, turn)
    link(dve.reciprocal(a, root))
    link(dve.tensor_tensor(out=b, in0=a, in1=a, op=ALU.mult))
    link(dve.tensor_tensor(out=b, in0=b, in1=var, op=ALU.mult))
    link(dve.tensor_scalar(b, b, -0.5, 1.5, ALU.mult, ALU.add))
    link(dve.tensor_tensor(out=rstd[:, cols], in0=a, in1=b, op=ALU.mult))
    link(dve.tensor_tensor(out=nbias[:, cols], in0=rstd[:, cols], in1=mv[:, cols, 0], op=ALU.mult))
    link(dve.tensor_scalar(nbias[:, cols], nbias[:, cols], -1.0, None, ALU.mult))
    return at

HEADS, DH, KEYS = 16, 64, 77
INNER = HEADS * DH
MT = INNER // P
JT = S // P
SBANKS = [(0, 6), (6, 11), (11, 16)]
KCHUNK = 6
TH = 4
NTB = HEADS // TH
GB = 3
G_O, G_OUT, G_XT, G_Q, G_V = MT // 2, 1, 1, MT // 2, INNER // 512
G_BACK, G_FRONT = G_O + G_OUT, G_XT + G_Q + G_V
G_ALL = G_BACK + G_FRONT
MASKED = -1e30

def gfront(b, k):
    if isinstance(b, int) and b == 0:
        return k
    return G_FRONT + (b - 1) * G_ALL + k

def gback(b, k):
    last = isinstance(b, int) and b == B - 1
    return (b + 1) * G_ALL + G_FRONT - G_BACK + k - (G_FRONT if last else 0)

def gfront_bank(b, k):
    return (gfront(b, k) if isinstance(b, int) else G_FRONT + k) % GB

def gback_bank(b, k):
    return (gback(b, k) if isinstance(b, int) else G_FRONT - G_BACK + k) % GB

assert G_ALL % GB == 0

def attention(nc, ctx, t):
    def sb(name, shape, dt=fp32):
        return ctx.enter_context(nc.sbuf_tensor(name, shape, dt))

    def sem(name):
        return ctx.enter_context(nc.semaphore(name))

    xs, ident, mv0, mv1, rstd, nbias, tmpv = t["xs"], t["ident"], t["mv0"], t["mv1"], t["rstd"], t["nbias"], t["tmpv"]
    wq = sb("wq", [P, DK, INNER])
    wv = sb("wv", [P, DK, INNER])
    wo = sb("wo", [P, MT, D])
    bo = sb("bo", [P, D])
    cxT = sb("cxT", [P, DK, B * KEYS])
    kT = sb("kT", [P, MT, B * KEYS])
    v = sb("v", [KEYS, 2, INNER])
    x1 = sb("x1", [P, 2, JT, D])
    cxb = sb("cxb", [P, 2, DK, KEYS])
    xT = sb("xT", [P, DK, S])
    q = sb("q", [P, 2, 2, MT, S])
    mrow8 = sb("mrow8", [1, B * KEYS // 4], u32)
    mrow = sb("mrow", [P, B * KEYS])
    first = sb("first", [P, P])
    nmax = sb("nmax", [P, JT, HEADS])
    rsum = sb("rsum", [P, JT, HEADS])
    rinv = sb("rinv", [P, JT, HEADS])
    pr = sb("pr", [P, JT, HEADS, KEYS])
    pn = sb("pn", [P, JT, HEADS, KEYS])
    pT = sb("pT", [KEYS, HEADS, S])
    oT = sb("oT", [P, MT, S])
    bst = sb("bst2", [P, JT, 6])
    mvt = sb("mvt2", [P, JT, 2])
    assert (B, D) == (HEADS, S) and MT * S == DK * INNER
    cx = pT[:, :, :]
    wk = oT[:, :, :].rearrange("p (k m) s -> p k (m s)", k=DK)
    sc = ctx.enter_context(nc.psum_tensor("sc", [P, len(SBANKS), 512], fp32))
    tb = [ctx.enter_context(nc.psum_tensor(f"tb{i}", [P, TH * P], fp32)) for i in range(2)]
    g = [ctx.enter_context(nc.psum_tensor(f"g{i}", [P, 512], fp32)) for i in range(GB)]

    loaded = [sem(f"a_loaded{i}") for i in range(4)]
    stats = sem("a_stats")
    rooted = sem("a_rooted")
    const = sem("a_const")
    maskrow = sem("a_maskrow")
    p_full = sem("a_p_full")
    p_free = sem("a_p_free")
    x1_ready = sem("a_x1")
    g_full = sem("a_g_full")
    g_free = sem("a_g_free")
    s_full = sem("a_s_full")
    maxed = sem("a_maxed")
    exped = sem("a_exped")
    inverted = sem("a_inverted")
    pn_ready = sem("a_pn")
    t_full = sem("a_t_full")
    t_free = sem("a_t_free")
    z_steps = sem("a_z")
    z_seen = sem("a_z_seen")
    mv_kept = sem("a_mv_kept")
    cx_ready = sem("a_cx")

    KB = [(a, min(a + KCHUNK, B)) for a in range(0, B, KCHUNK)]
    XPB = 3
    XB = [(a, min(a + XPB, B)) for a in range(0, B, XPB)]
    NX = len(XB)

    with nc.Block() as block:
        @block.sync
        def _(sp):
            sp.dma_start(cx, t["ctx"].rearrange("b k d -> k b d")).then_inc(loaded[0], 16)
            wkv = t["Wkv"].rearrange("(k p) n -> p k n", p=P)
            sp.dma_start(wk, wkv[:, :, 0:INNER]).then_inc(loaded[1], 16)
            sp.dma_start(wv[:, :, :], wkv[:, :, INNER:2 * INNER]).then_inc(loaded[3], 16)
            sp.dma_start(wq[:, :, :], t["Wq"].rearrange("(k p) n -> p k n", p=P)).then_inc(loaded[2], 16)
            sp.dma_start(mrow8[:, :], t["mask"].rearrange("(a n) -> a n", a=1)).then_inc(loaded[2], 16)
            sp.dma_start(wo[:, :, :], t["Wout"].rearrange("(k p) n -> p k n", p=P)).then_inc(loaded[3], 16)
            sp.dma_start(bo[:, :], t["b_out"].rearrange("(a n) -> a n", a=1).to_broadcast([P, D])).then_inc(loaded[3], 16)

        @block.gpsimd
        def _(pool):
            pool.memset(first[:, :], 0.0).then_inc(const, 1)
            pool.memset(mrow[:, :], 0.0).then_inc(const, 1)
            pool.wait_ge(const, 1)
            pool.memset(first[0:1, :], 1.0).then_inc(const, 1)
            pool.memset(q[:, :, :, :, :], 0.0).then_inc(const, 1)

        @block.vector
        def _(dve):
            rstd_vector(dve, mv1, rstd, nbias, tmpv, stats, rooted, 0)
            dve.wait_ge(loaded[2], 32)
            dve.wait_ge(const, 2)
            dve.tensor_scalar(mrow[0:1, :], mrow8[:, :].bitcast(mybir.dt.uint8), MASKED, None, ALU.mult).then_inc(maskrow, 1)

        @block.scalar
        def _(act):
            rstd_scalar(act, tmpv, stats, rooted, 0)
            unit = 0
            for a, e in XB:
                for k in range(DK):
                    act.wait_ge(p_full, unit + 1)
                    act.activation(cxT[:, k, a * KEYS:e * KEYS], g[unit % 2][:, 0:(e - a) * KEYS], ACT.Copy).then_inc(p_free, 1)
                    unit += 1
            for m in range(MT):
                for a, e in KB:
                    act.wait_ge(p_full, unit + 1)
                    act.activation(kT[:, m, a * KEYS:e * KEYS], g[unit % 2][:, 0:(e - a) * KEYS], ACT.Copy).then_inc(p_free, 1)
                    unit += 1

        @block.tensor
        def _(pe):
            pe.wait_ge(loaded[0], 16)
            unit = 0
            for a, e in XB:
                for k in range(DK):
                    if unit >= 2:
                        pe.wait_ge(p_free, unit - 1)
                    for b in range(a, e):
                        ins = pe.transpose(g[unit % 2][:, (b - a) * KEYS:(b - a + 1) * KEYS],
                                           cx[:, b, k * P:(k + 1) * P], ident[0:KEYS, 0:KEYS])
                    ins.then_inc(p_full, 1)
                    unit += 1
            pe.wait_ge(loaded[1], 16)
            pe.wait_ge(p_free, NX * DK)
            for m in range(MT):
                for a, e in KB:
                    pe.wait_ge(p_free, unit - 1)
                    for k in range(DK):
                        ins = pe.matmul(g[unit % 2][:, 0:(e - a) * KEYS], wk[:, k, m * P:(m + 1) * P],
                                        cxT[:, k, a * KEYS:e * KEYS], start=(k == 0), stop=(k == DK - 1))
                    ins.then_inc(p_full, 1)
                    unit += 1

    block = ctx.enter_context(nc.Block())

    def batches(eng, body):
        body(0, 0, False, True)
        with eng.Fori(0, B // 2 - 1) as it:
            body(it * 2 + 1, 1, True, True)
            body(it * 2 + 2, 0, True, True)
        body(B - 1, 1, True, False)

    @block.gpsimd
    def _(pool):
        def keep_context(b, par):
            pool.tensor_copy(cxb[:, par, :, :], cxT[:, :, bass.ds(b * KEYS, KEYS)]).then_inc(cx_ready, 1)

        def norm_p(b, j):
            pool.wait_ge(inverted, 2 * b + j + 1)
            if not (isinstance(b, int) and b == 0):
                pool.wait_ge(t_full, (b - 1) * JT * NTB + (j + 1) * NTB)
            pool.tensor_tensor(out=pn[:, j, :, :], in0=pr[:, j, :, :],
                               in1=rinv[:, j, :].rearrange("p (h a) -> p h a", a=1).to_broadcast([P, HEADS, KEYS]),
                               op=ALU.mult).then_inc(pn_ready, 1)

        def batch(b, par, before, after):
            if after:
                keep_context(b + 1, 1 - par)
            norm_p(b, 0)
            norm_p(b, 1)

        keep_context(0, 0)
        batches(pool, batch)

    @block.vector
    def _(dve):
        def maxima(b, j):
            dve.wait_ge(s_full, 2 * b + j + 1)
            for i, (a, e) in enumerate(SBANKS):
                ins = dve.tensor_reduce(nmax[:, j, a:e], sc[:, i, 0:(e - a) * KEYS].rearrange("p (h k) -> p h k", k=KEYS),
                                        axis=AX.X, op=ALU.max, negate=True)
            ins.then_inc(maxed, 1)

        def invert(b, j):
            dve.wait_ge(exped, 2 * b + j + 1)
            dve.reciprocal(rinv[:, j, :], rsum[:, j, :]).then_inc(inverted, 1)

        def front_x(b):
            dve.wait_ge(g_full, gfront(b, 0) + 1)
            dve.tensor_copy(xT[:, :, :], g[gfront_bank(b, 0)][:, :].rearrange("p (k s) -> p k s", k=DK)).then_inc(g_free, 1)

        def front_q(b, par):
            for i in range(G_Q):
                bank = g[gfront_bank(b, G_XT + i)]
                dve.wait_ge(g_full, gfront(b, G_XT + i) + 1)
                for o in range(2):
                    rows = slice(o * DH, (o + 1) * DH)
                    ins = dve.tensor_scalar(q[rows, par, o, 2 * i:2 * i + 2, :], bank[rows, :].rearrange("p (m s) -> p m s", m=2),
                                            DH ** -0.5, None, ALU.mult)
                ins.then_inc(g_free, 1)

        def front_v(b, par):
            for i in range(G_V):
                dve.wait_ge(g_full, gfront(b, G_XT + G_Q + i) + 1)
                dve.tensor_copy(v[:, par, i * 512:(i + 1) * 512], g[gfront_bank(b, G_XT + G_Q + i)][0:KEYS, :]).then_inc(g_free, 1)

        def back(b, par):
            for i in range(G_O):
                dve.wait_ge(g_full, gback(b, i) + 1)
                dve.tensor_copy(oT[:, 2 * i:2 * i + 2, :], g[gback_bank(b, i)][:, :].rearrange("p (m s) -> p m s", m=2)).then_inc(g_free, 1)
            tiles = bass.ds(b * JT, JT)
            dve.wait_ge(g_full, gback(b, G_O) + 1)
            dve.tensor_tensor(out=xs[:, tiles, :], in0=x1[:, par, :, :],
                              in1=g[gback_bank(b, G_O)][:, :].rearrange("p (j d) -> p j d", j=JT), op=ALU.add).then_inc(g_free, 1)
            dve.wait_ge(g_free, gback(b, G_O) + 1)
            dve.tensor_tensor(out=xs[:, tiles, :], in0=xs[:, tiles, :],
                              in1=bo[:, :].rearrange("p (a n) -> p a n", a=1).to_broadcast([P, JT, D]),
                              op=ALU.add).then_inc(z_steps, 1)
            dve.wait_ge(z_steps, 3 * b + 1)
            dve.sem_inc(z_seen, 1)
            for j in range(JT):
                ins = dve.bn_stats(bst[:, j, :], xs[:, bass.ds(b * JT + j, 1), :])
            ins.then_inc(z_steps, 1)
            dve.wait_ge(z_steps, 3 * b + 2)
            if not (isinstance(b, int) and b == 0):
                dve.wait_ge(mv_kept, b)
            dve.sem_inc(z_seen, 1)
            for j in range(JT):
                ins = dve.bn_aggr(mvt[:, j, :], bst[:, j, :])
            ins.then_inc(z_steps, 1)
            dve.wait_ge(z_steps, 3 * b + 3)
            dve.tensor_copy(mv0[:, tiles, :], mvt[:, :, :]).then_inc(mv_kept, 1)

        def batch(b, par, before, after):
            maxima(b, 0)
            if before:
                back(b - 1, 1 - par)
            invert(b, 0)
            maxima(b, 1)
            if after:
                front_x(b + 1)
                front_q(b + 1, 1 - par)
                invert(b, 1)
                front_v(b + 1, 1 - par)
            else:
                invert(b, 1)

        dve.wait_ge(loaded[3], 48)
        front_x(0)
        front_q(0, 0)
        front_v(0, 0)
        batches(dve, batch)
        back(B - 1, 1)

    @block.scalar
    def _(act):
        def exps(b, j):
            act.wait_ge(maxed, 2 * b + j + 1)
            if not (isinstance(b, int) and b == 0):
                act.wait_ge(pn_ready, 2 * (b - 1) + j + 1)
            for i, (a, e) in enumerate(SBANKS):
                for hd in range(a, e):
                    ins = act.activation(pr[:, j, hd, :], sc[:, i, (hd - a) * KEYS:(hd - a + 1) * KEYS], ACT.Exp,
                                         bias=nmax[:, j, hd:hd + 1], accum_out=rsum[:, j, hd:hd + 1])
            ins.then_inc(exped, 1)

        def transposed(b, j):
            for k in range(NTB):
                act.wait_ge(t_full, b * JT * NTB + j * NTB + k + 1)
                act.activation(pT[:, k * TH:(k + 1) * TH, j * P:(j + 1) * P],
                               tb[k % 2][0:KEYS, :].rearrange("p (h s) -> p h s", h=TH), ACT.Copy).then_inc(t_free, 1)

        def norm_x(b, par):
            if not (isinstance(b, int) and b < 2):
                act.wait_ge(z_steps, 3 * (b - 2) + 1)
            for j in range(JT):
                tile = bass.ds(b * JT + j, 1)
                ins = act.activation(x1[:, par, j, :], xs[:, tile, :], ACT.Identity, scale=rstd[:, tile], bias=nbias[:, tile])
            ins.then_inc(x1_ready, 1)

        def batch(b, par, before, after):
            exps(b, 0)
            if after:
                norm_x(b + 1, 1 - par)
            exps(b, 1)
            transposed(b, 0)
            transposed(b, 1)

        norm_x(0, 0)
        batches(act, batch)

    @block.tensor
    def _(pe):
        def free_bank(unit):
            if not isinstance(unit, int) or unit >= GB:
                pe.wait_ge(g_free, unit - GB + 1)

        def scores(b, j, par):
            if j == 0:
                pe.wait_ge(g_free, gfront(b, G_XT + G_Q - 1) + 1)
            if not (isinstance(b, int) and b == 0 and j == 0):
                pe.wait_ge(exped, 2 * b + j)
            keys = bass.ds(b * KEYS, KEYS)
            for i, (a, e) in enumerate(SBANKS):
                mask = mrow[:, keys].rearrange("p (a k) -> p a k", a=1).to_broadcast([P, e - a, KEYS])
                pe.matmul(sc[:, i, 0:(e - a) * KEYS].rearrange("p (h k) -> p h k", k=KEYS), first[:, :], mask, start=True, stop=False)
                for hd in range(a, e):
                    ins = pe.matmul(sc[:, i, (hd - a) * KEYS:(hd - a + 1) * KEYS], q[:, par, hd % 2, hd // 2, j * P:(j + 1) * P],
                                    kT[:, hd // 2, keys], start=False, stop=(hd == e - 1))
            ins.then_inc(s_full, 1)

        def transposes(b, j):
            pe.wait_ge(pn_ready, 2 * b + j + 1)
            for k in range(NTB):
                unit = b * JT * NTB + j * NTB + k
                if not isinstance(unit, int) or unit >= 2:
                    pe.wait_ge(t_free, unit - 1)
                for hd in range(TH):
                    ins = pe.transpose(tb[k % 2][0:KEYS, hd * P:(hd + 1) * P], pn[:, j, k * TH + hd, :], ident[:, :])
                ins.then_inc(t_full, 1)

        def front(b, par):
            free_bank(gfront(b, 0))
            pe.wait_ge(x1_ready, b + 1)
            for k in range(DK):
                for j in range(JT):
                    ins = pe.transpose(g[gfront_bank(b, 0)][:, k * S + j * P:k * S + (j + 1) * P],
                                       x1[:, par, j, k * P:(k + 1) * P], ident[:, :])
            ins.then_inc(g_full, 1)
            for i in range(G_Q):
                free_bank(gfront(b, G_XT + i))
                if i == 0:
                    pe.wait_ge(g_free, gfront(b, 0) + 1)
                for a in range(2):
                    m = 2 * i + a
                    for k in range(DK):
                        ins = pe.matmul(g[gfront_bank(b, G_XT + i)][:, a * S:(a + 1) * S], wq[:, k, m * P:(m + 1) * P],
                                        xT[:, k, :], start=(k == 0), stop=(k == DK - 1))
                ins.then_inc(g_full, 1)
            pe.wait_ge(cx_ready, b + 1)
            for i in range(G_V):
                free_bank(gfront(b, G_XT + G_Q + i))
                for k in range(DK):
                    ins = pe.matmul(g[gfront_bank(b, G_XT + G_Q + i)][0:KEYS, :], cxb[:, par, k, :],
                                    wv[:, k, i * 512:(i + 1) * 512], start=(k == 0), stop=(k == DK - 1))
                ins.then_inc(g_full, 1)

        def back(b, par):
            pe.wait_ge(t_free, (b + 1) * JT * NTB)
            for i in range(G_O):
                free_bank(gback(b, i))
                for hd in range(4 * i, 4 * i + 4):
                    m, o = hd // 2 - 2 * i, hd % 2
                    ins = pe.matmul(g[gback_bank(b, i)][o * DH:(o + 1) * DH, m * S:(m + 1) * S],
                                    v[:, par, hd * DH:(hd + 1) * DH], pT[:, hd, :], start=True, stop=True)
                ins.then_inc(g_full, 1)
            pe.wait_ge(g_free, gback(b, G_O - 1) + 1)
            for j in range(JT):
                for m in range(MT):
                    ins = pe.matmul(g[gback_bank(b, G_O)][:, j * D:(j + 1) * D], oT[:, m, j * P:(j + 1) * P],
                                    wo[:, m, :], start=(m == 0), stop=(m == MT - 1))
            ins.then_inc(g_full, 1)

        def batch(b, par, before, after):
            scores(b, 0, par)
            if before:
                back(b - 1, 1 - par)
            scores(b, 1, par)
            if after:
                front(b + 1, 1 - par)
            transposes(b, 0)
            transposes(b, 1)

        pe.wait_ge(loaded[3], 48)
        front(0, 0)
        batches(pe, batch)
        back(B - 1, 1)

fp16 = mybir.dt.float16
i32 = mybir.dt.int32

E, TOPK, H = 8, 2, 1024
HM = H // P
TS_LOG = 8
TS = 1 << TS_LOG
SJ = TS // P
NTILES = (TOPK * B * S + E * (TS - 1)) // TS
NSLOT = NTILES * TS
WSCALE = 16.0
RG = 4
HU = 2

def router(nc, ctx, t):
    def sb(name, shape, dt=fp32):
        return ctx.enter_context(nc.sbuf_tensor(name, shape, dt))

    def sem(name):
        return ctx.enter_context(nc.semaphore(name))

    xs, ident, mv0, rstd, nbias, tmpv = (t[k] for k in ("xs", "ident", "mv0", "rstd", "nbias", "tmpv"))
    w1h, w1l, w2h, w2l, b1s, b2s = (t[k] for k in ("w1h", "w1l", "w2h", "w2l", "b1s", "b2s"))
    slots, gates, expert_of = t["slots"], t["gates"], t["expert_of"]
    stage = sb("stage", [P, 2, 2 * H])
    b2f, b2r = (stage[0:1, i, :].rearrange("p (e d) -> p e d", e=E) for i in range(2))
    wr = sb("wr", [P, DK, E])
    x2 = sb("x2", [P, 2, RG, D])
    x2T = sb("x2T", [P, DK, RG * P])
    lg = sb("lg", [P, NT, E])
    rev = sb("rev", [P, NT, E])
    tid = sb("tid", [1, NTILES, E])
    ones = sb("ones", [P, NT])
    lower = sb("lower", [P, P], bf16)
    allone = sb("allone", [P, P], bf16)
    hit = sb("hit", [P, TOPK, NT, E])
    w = [sb(f"w{i}", [P, NT, E]) for i in range(3)]
    chosen = sb("chosen", [P, NT, E], bf16)
    best = sb("best", [P, TOPK, NT])
    at = sb("at", [P, NT])
    small = sb("small", [P, 4, E])
    cnt = sb("cnt", [P, E], i32)
    over = sb("over", [1, NTILES, E])
    fexp = sb("fexp", [1, NTILES])
    tp = [ctx.enter_context(nc.psum_tensor(f"tp{i}", [P, RG * P], fp32)) for i in range(2)]
    lp = [ctx.enter_context(nc.psum_tensor(f"lp{i}", [P, RG, E], fp32)) for i in range(2)]
    ranks = ctx.enter_context(nc.psum_tensor("ranks", [P, NT, E], fp32))
    totals = ctx.enter_context(nc.psum_tensor("totals", [P, NT, E], fp32))

    loaded = sem("r_loaded")
    wstage = [sem(f"r_wstage{i}") for i in range(2)]
    whi = sem("r_whi")
    wlo = sem("r_wlo")
    stats = sem("r_stats")
    rooted = sem("r_rooted")
    const = sem("r_const")
    x2_ready = sem("r_x2")
    xs_ready = sem("r_xs")
    t_full, t_free = sem("r_t_full"), sem("r_t_free")
    l_full, l_free = sem("r_l_full"), sem("r_l_free")
    steps = sem("r_steps")
    ranked = sem("r_ranked")
    chosen_ready = sem("r_chosen")
    gap = sem("r_gap")
    egap = sem("r_egap")
    placed = sem("r_placed")
    b2_zero = sem("r_b2_zero")
    b2_steps = sem("r_b2")
    sent = sem("r_sent")

    NG = NT // RG
    wviews = []
    for e in range(E):
        wviews.append((t["W1"][e].rearrange("(k p) n -> p k n", p=P), w1h[:, e, :, :], w1l[:, e, :, :], DK))
        wviews.append((t["W2"][e].rearrange("(m p) n -> p m n", p=P), w2h[:, e, :, :], w2l[:, e, :, :], HM))

    block = ctx.enter_context(nc.Block())

    @block.sync
    def _(sp):
        with nc.allow_non_contiguous_dma(reason="biases"):
            sp.dma_start(wr[:, :, :], t["Wr"].rearrange("(k p) n -> p k n", p=P)).then_inc(loaded, 16)
            sp.dma_start(b1s[:, :, :], t["b1"].rearrange("e (m p) -> p e m", p=P)).then_inc(loaded, 16)
            sp.dma_start(b2f, t["b2"].rearrange("(a e) n -> a e n", a=1)).then_inc(loaded, 16)
        sp.wait_ge(b2_steps, 3)
        for i, (src, _, _, k) in enumerate(wviews):
            if i >= 2:
                sp.wait_ge(wlo, i - 1)
                sp.wait_ge(whi, i - 1)
            sp.dma_start(stage[:, i % 2, :].rearrange("p (k n) -> p k n", k=k), src).then_inc(wstage[i % 2], 16)

    @block.gpsimd
    def _(pool):
        pool.memset(b2s[:, :, :], 0.0).then_inc(b2_zero, 1)
        pool.iota(rev[:, :, :], pattern=[[0, NT], [-1, E]], base=E, channel_multiplier=0,
                  allow_small_or_imprecise_dtypes=True).then_inc(const, 1)
        pool.iota(tid[:, :, :], pattern=[[1, NTILES], [0, E]], base=0, channel_multiplier=0,
                  allow_small_or_imprecise_dtypes=True).then_inc(const, 1)
        pool.memset(ones[:, :], 1.0).then_inc(const, 1)
        pool.memset(lower[:, :], 0.0).then_inc(const, 1)
        pool.memset(allone[:, :], 1.0).then_inc(const, 1)
        pool.wait_ge(const, 5)
        pool.affine_select(out=lower[:, :], in_=lower[:, :], compare_op=ALU.is_ge, fill=1.0,
                           base=0, pattern=[[-1, P]], channel_multiplier=1).then_inc(const, 1)

        def copy_back(g, par):
            pool.wait_ge(x2_ready, g + 1)
            pool.tensor_copy(xs[:, bass.ds(g * RG, RG), :], x2[:, par, :, :]).then_inc(xs_ready, 1)

        with pool.Fori(0, NG // 2) as it:
            copy_back(it * 2, 0)
            copy_back(it * 2 + 1, 1)
        pool.wait_ge(placed, 1)
        pool.wait_ge(xs_ready, NG)
        for k in range(TOPK):
            for j in range(NT):
                pool.indirect_dma_start(t["xsort"], bass.IndirectOffsetOnAxis(ap=slots[:, k, j:j + 1], axis=0),
                                        xs[:, j, :], None).then_inc(sent, 16)
        pool.wait_ge(sent, 16 * TOPK * NT)

    @block.scalar
    def _(act):
        rstd_scalar(act, tmpv, stats, rooted, 0)
        act.wait_ge(stats, RSTD_STEPS)

        def normalise(g, par):
            if not (isinstance(g, int) and g < 2):
                act.wait_ge(xs_ready, g - 1)
                act.wait_ge(t_full, 2 * (g - 1))
            for j in range(RG):
                tile = bass.ds(g * RG + j, 1)
                ins = act.activation(x2[:, par, j, :], xs[:, tile, :], ACT.Identity, scale=rstd[:, tile], bias=nbias[:, tile])
            ins.then_inc(x2_ready, 1)

        normalise(0, 0)
        normalise(1, 1)
        with act.Fori(1, NG // 2) as it:
            normalise(it * 2, 0)
            normalise(it * 2 + 1, 1)
        act.wait_ge(gap, 1)
        act.activation(at[:, :], best[:, 0, :], ACT.Exp).then_inc(egap, 1)
        for i, (src, hi, lo, k) in enumerate(wviews):
            act.wait_ge(wstage[i % 2], 16 * (i // 2 + 1))
            act.activation(hi, stage[:, i % 2, :].rearrange("p (k n) -> p k n", k=k), ACT.Copy, scale=WSCALE).then_inc(whi, 1)

    @block.tensor
    def _(pe):
        pe.wait_ge(loaded, 48)

        def group(g, par):
            pe.wait_ge(x2_ready, g + 1)
            for k in range(DK):
                if not (isinstance(g, int) and g == 0):
                    pe.wait_ge(t_free, 2 * g + k - 1)
                for j in range(RG):
                    ins = pe.transpose(tp[k][:, j * P:(j + 1) * P], x2[:, par, j, k * P:(k + 1) * P], ident[:, :])
                ins.then_inc(t_full, 1)
            pe.wait_ge(t_free, 2 * g + 2)
            if not (isinstance(g, int) and g < 2):
                pe.wait_ge(l_free, g - 1)
            for j in range(RG):
                for k in range(DK):
                    ins = pe.matmul(lp[par][:, j, :], x2T[:, k, j * P:(j + 1) * P], wr[:, k, :],
                                    start=(k == 0), stop=(k == DK - 1))
            ins.then_inc(l_full, 1)

        group(0, 0)
        group(1, 1)
        with pe.Fori(1, NG // 2) as it:
            group(it * 2, 0)
            group(it * 2 + 1, 1)
        pe.wait_ge(const, 6)
        pe.wait_ge(chosen_ready, 1)
        pe.matmul(ranks[:, :, :], lower[:, :], chosen[:, :, :], start=True, stop=True)
        pe.matmul(totals[:, :, :], allone[:, :], chosen[:, :, :], start=True, stop=True).then_inc(ranked, 1)

    @block.vector
    def _(dve):
        dve.wait_ge(loaded, 48)
        dve.wait_ge(b2_zero, 1)
        dve.tensor_scalar(b2s[0:1, :, :], b2f, WSCALE, None, ALU.mult).then_inc(b2_steps, 1)
        dve.wait_ge(b2_steps, 1)
        dve.scalar_tensor_tensor(out=b2r, in0=b2f, scalar=WSCALE, in1=b2s[0:1, :, :],
                                 op0=ALU.mult, op1=ALU.subtract).then_inc(b2_steps, 1)
        dve.wait_ge(b2_steps, 2)
        dve.tensor_copy(b2s[32:33, :, :], b2r).then_inc(b2_steps, 1)
        rstd_vector(dve, mv0, rstd, nbias, tmpv, stats, rooted, 0)

        def group(g, par):
            for k in range(DK):
                dve.wait_ge(t_full, 2 * g + k + 1)
                dve.tensor_copy(x2T[:, k, :], tp[k][:, :]).then_inc(t_free, 1)
            dve.wait_ge(l_full, g + 1)
            dve.tensor_copy(lg[:, bass.ds(g * RG, RG), :], lp[par][:, :, :]).then_inc(l_free, 1)

        with dve.Fori(0, NG // 2) as it:
            group(it * 2, 0)
            group(it * 2 + 1, 1)
        dve.wait_ge(const, 6)
        dve.wait_ge(l_free, NG)
        n = 0

        def link(ins):
            nonlocal n
            n += 1
            ins.then_inc(steps, 1)
            dve.wait_ge(steps, n)

        def over_experts(v):
            return v.rearrange("p (j a) -> p j a", a=1).to_broadcast([P, NT, E])

        logits = lg
        for k in range(TOPK):
            link(dve.tensor_reduce(best[:, k, :], logits[:, :, :], axis=AX.X, op=ALU.max))
            link(dve.tensor_tensor(out=w[1][:, :, :], in0=logits[:, :, :], in1=over_experts(best[:, k, :]), op=ALU.is_equal))
            link(dve.tensor_tensor(out=w[1][:, :, :], in0=w[1][:, :, :], in1=rev[:, :, :], op=ALU.mult))
            link(dve.tensor_reduce(at[:, :], w[1][:, :, :], axis=AX.X, op=ALU.max))
            link(dve.tensor_tensor(out=hit[:, k, :, :], in0=rev[:, :, :], in1=over_experts(at[:, :]), op=ALU.is_equal))
            if k == 0:
                link(dve.scalar_tensor_tensor(out=w[0][:, :, :], in0=hit[:, 0, :, :], scalar=-3e38, in1=lg[:, :, :],
                                              op0=ALU.mult, op1=ALU.add))
                logits = w[0]
        dve.tensor_tensor(out=chosen[:, :, :], in0=hit[:, 0, :, :], in1=hit[:, 1, :, :], op=ALU.add).then_inc(chosen_ready, 1)
        link(dve.tensor_tensor(out=best[:, 0, :], in0=best[:, 1, :], in1=best[:, 0, :], op=ALU.subtract))
        dve.sem_inc(gap, 1)
        dve.wait_ge(egap, 1)
        link(dve.tensor_scalar(best[:, 1, :], at[:, :], 1.0, None, ALU.add))
        link(dve.reciprocal(gates[:, 0, :], best[:, 1, :]))
        link(dve.tensor_tensor(out=gates[:, 1, :], in0=gates[:, 0, :], in1=at[:, :], op=ALU.mult))
        dve.wait_ge(ranked, 1)
        upto = w[0][:, :, :].rearrange("p j e -> p (j e)").rearrange("p (e j) -> p e j", e=E)
        for e in range(E):
            ins = dve.tensor_tensor_scan(out=upto[:, e, :], data0=ones[:, :], data1=totals[:, :, e], initial=0.0,
                                         op0=ALU.mult, op1=ALU.add)
        link(ins)
        count, tiles, ends, base = (small[:, i, :] for i in range(4))
        link(dve.tensor_scalar(cnt[:, :], upto[:, :, NT - 1], float(TS - 1), None, ALU.add))
        link(dve.tensor_scalar(cnt[:, :], cnt[:, :], TS_LOG, None, ALU.logical_shift_right))
        link(dve.tensor_copy(tiles, cnt[:, :]))
        link(dve.tensor_tensor_scan(out=ends, data0=ones[:, 0:E], data1=tiles, initial=0.0, op0=ALU.mult, op1=ALU.add))
        link(dve.tensor_tensor(out=base, in0=ends, in1=tiles, op=ALU.subtract))
        link(dve.tensor_scalar(base, base, float(TS), None, ALU.mult))
        link(dve.tensor_tensor(out=w[1][:, :, :], in0=upto.rearrange("p e j -> p j e"), in1=totals[:, :, :], op=ALU.subtract))
        link(dve.tensor_tensor(out=w[2][:, :, :], in0=w[1][:, :, :], in1=ranks[:, :, :], op=ALU.add))
        link(dve.tensor_tensor(out=w[1][:, :, :], in0=w[2][:, :, :],
                               in1=base.rearrange("p (a e) -> p a e", a=1).to_broadcast([P, NT, E]), op=ALU.add))
        for k in range(TOPK):
            link(dve.tensor_tensor(out=w[2][:, :, :], in0=w[1][:, :, :], in1=hit[:, k, :, :], op=ALU.mult))
            link(dve.tensor_reduce(best[:, k, :], w[2][:, :, :], axis=AX.X, op=ALU.add))
            link(dve.tensor_copy(slots[:, k, :], best[:, k, :]))
        dve.sem_inc(placed, 1)
        link(dve.tensor_tensor(out=over[:, :, :], in0=tid[:, :, :],
                               in1=ends[0:1, :].rearrange("p (a e) -> p a e", a=1).to_broadcast([1, NTILES, E]), op=ALU.is_ge))
        link(dve.tensor_reduce(fexp[:, :], over[:, :, :], axis=AX.X, op=ALU.add))
        link(dve.tensor_scalar(expert_of[:, :], fexp[:, :], float(E - 1), None, ALU.min))
        for i, (src, hi, lo, k) in enumerate(wviews):
            dve.wait_ge(whi, i + 1)
            dve.scalar_tensor_tensor(out=lo, in0=stage[:, i % 2, :].rearrange("p (k n) -> p k n", k=k), scalar=WSCALE,
                                     in1=hi, op0=ALU.mult, op1=ALU.subtract).then_inc(wlo, 1)
        dve.wait_ge(wlo, len(wviews))

def experts(nc, ctx, t):
    def sb(name, shape, dt=fp32):
        return ctx.enter_context(nc.sbuf_tensor(name, shape, dt))

    def sem(name):
        return ctx.enter_context(nc.semaphore(name))

    ident, w1h, w1l, w2h, w2l, b1s, b2s, expert_of = (t[k] for k in ("ident", "w1h", "w1l", "w2h", "w2l", "b1s", "b2s", "expert_of"))
    NHU = HM // HU
    STORE_LAG = 4
    xt = sb("xt", [P, 2, SJ, D])
    xh = sb("xh", [P, 2, DK, TS], fp16)
    xl = sb("xl", [P, 2, DK, TS], fp16)
    act32 = sb("act32", [P, 2, HU, TS])
    hh = sb("hh", [P, 2, HM, TS], fp16)
    hl = sb("hl", [P, 2, HM, TS], fp16)
    ys = sb("ys", [P, 2, SJ, D])
    brow = sb("brow", [P, P], fp16)
    hp = [ctx.enter_context(nc.psum_tensor(f"hp{i}", [P, HU * TS], fp32)) for i in range(4)]
    xp = ctx.enter_context(nc.psum_tensor("xp", [P, DK * TS], fp32))
    yp = [ctx.enter_context(nc.psum_tensor(f"yp{i}", [P, SJ * D], fp32)) for i in range(2)]

    x_in = [sem(f"e_x_in{i}") for i in range(2)]
    const = sem("e_const")
    xp_full = sem("e_xp_full")
    xh_ready, xl_ready = sem("e_xh"), sem("e_xl")
    h_full = sem("e_h_full")
    g_ready = sem("e_g")
    hh_ready = sem("e_hh")
    hl_ready = sem("e_hl")
    y_full = sem("e_y_full")
    y_ready = sem("e_y")
    y_out = [sem(f"e_y_out{i}") for i in range(2)]

    xv = t["xsort"].rearrange("(t j p) d -> p t j d", j=SJ, p=P)
    yv = t["ysort"].rearrange("(t j p) d -> p t j d", j=SJ, p=P)
    block = ctx.enter_context(nc.Block())

    def tiles(eng, body, apart=2):
        for t in range(apart):
            body(t, t % 2, t // 2)
        with eng.Fori(apart // 2, NTILES // 2) as it:
            body(it * 2, 0, it)
            body(it * 2 + 1, 1, it)
        if NTILES % 2:
            body(NTILES - 1, 0, NTILES // 2)

    def late(t, n=1):
        return not isinstance(t, int) or t >= n

    @block.sync
    def _(sp):
        def store(t, par):
            sp.wait_ge(y_ready, t + 1)
            sp.dma_start(yv[:, bass.ds(t, 1), :, :], ys[:, par, :, :]).then_inc(y_out[par], 16)

        def tile(t, par, uses):
            if late(t, 2):
                sp.wait_ge(xp_full, t - 1)
            sp.dma_start(xt[:, par, :, :], xv[:, bass.ds(t, 1), :, :]).then_inc(x_in[par], 16)
            if late(t, STORE_LAG):
                store(t - STORE_LAG, par)

        tiles(sp, tile, STORE_LAG)
        for t in range(NTILES - STORE_LAG, NTILES):
            store(t, t % 2)
        for par in range(2):
            sp.wait_ge(y_out[par], 16 * ((NTILES + 1 - par) // 2))

    @block.gpsimd
    def _(pool):
        pool.memset(brow[:, :], 0.0).then_inc(const, 1)
        pool.wait_ge(const, 1)
        pool.memset(brow[0:1, :], 1.0).then_inc(const, 1)
        pool.memset(brow[32:33, :], 1.0).then_inc(const, 1)

    @block.scalar
    def _(act):
        def take_x(t, par):
            act.wait_ge(xp_full, t + 1)
            if late(t, 2):
                act.wait_ge(h_full, (t - 1) * NHU)
            act.activation(xh[:, par, :, :], xp[:, :].rearrange("p (k s) -> p k s", k=DK), ACT.Copy).then_inc(xh_ready, 1)

        def hidden(t, par):
            e = act.value_load(expert_of[0:1, bass.ds(t, 1)] , min_val=0, max_val=E - 1)
            for i in range(NHU):
                act.wait_ge(h_full, t * NHU + i + 1)
                if late(t * NHU + i, 2) if isinstance(t, int) else True:
                    act.wait_ge(hl_ready, t * NHU + i - 1)
                if late(t, 2):
                    act.wait_ge(y_full, t - 1)
                for a in range(HU):
                    m = i * HU + a
                    bias = b1s[:, bass.ds(e, 1), m]
                    pre = hp[i % 4][:, a * TS:(a + 1) * TS]
                    ins = act.activation(act32[:, i % 2, a, :], pre, ACT.Gelu, bias=bias, scale=1 / WSCALE)
                ins.then_inc(g_ready, 1)
                for a in range(HU):
                    m = i * HU + a
                    bias = b1s[:, bass.ds(e, 1), m]
                    pre = hp[i % 4][:, a * TS:(a + 1) * TS]
                    ins = act.activation(hh[:, par, m, :], pre, ACT.Gelu, bias=bias, scale=1 / WSCALE)
                ins.then_inc(hh_ready, 1)

        def tile(t, par, uses):
            hidden(t, par)
            if not (isinstance(t, int) and t == NTILES - 1):
                take_x(t + 1, 1 - par)

        take_x(0, 0)
        tiles(act, tile)

    @block.vector
    def _(dve):
        def take_x(t, par):
            dve.wait_ge(xh_ready, t + 1)
            if late(t, 2):
                dve.wait_ge(h_full, (t - 1) * NHU)
            dve.tensor_tensor(out=xl[:, par, :, :], in0=xp[:, :].rearrange("p (k s) -> p k s", k=DK),
                              in1=xh[:, par, :, :], op=ALU.subtract).then_inc(xl_ready, 1)

        def hidden(t, par):
            for i in range(NHU):
                dve.wait_ge(hh_ready, t * NHU + i + 1)
                if late(t, 2):
                    dve.wait_ge(y_full, t - 1)
                dve.tensor_tensor(out=hl[:, par, i * HU:(i + 1) * HU, :], in0=act32[:, i % 2, :, :],
                                  in1=hh[:, par, i * HU:(i + 1) * HU, :], op=ALU.subtract).then_inc(hl_ready, 1)

        def output(t, par, uses):
            dve.wait_ge(y_full, t + 1)
            if late(t, 2):
                dve.wait_ge(y_out[par], uses * 16)
            dve.tensor_scalar(ys[:, par, :, :], yp[par][:, :].rearrange("p (j d) -> p j d", j=SJ), 1 / WSCALE, None,
                              ALU.mult).then_inc(y_ready, 1)

        def tile(t, par, uses):
            hidden(t, par)
            if not (isinstance(t, int) and t == NTILES - 1):
                take_x(t + 1, 1 - par)
            if late(t):
                output(t - 1, 1 - par, uses - 1 + par)

        take_x(0, 0)
        tiles(dve, tile)
        output(NTILES - 1, (NTILES - 1) % 2, (NTILES - 1) // 2)

    @block.tensor
    def _(pe):
        def transpose(t, par, uses):
            pe.wait_ge(x_in[par], uses * 16 + 16)
            if late(t):
                pe.wait_ge(xl_ready, t)
            for k in range(DK):
                for j in range(SJ):
                    ins = pe.transpose(xp[:, k * TS + j * P:k * TS + (j + 1) * P], xt[:, par, j, k * P:(k + 1) * P], ident[:, :])
            ins.then_inc(xp_full, 1)

        def hidden(t, par):
            e = pe.value_load(expert_of[0:1, bass.ds(t, 1)], min_val=0, max_val=E - 1)
            pe.wait_ge(xl_ready, t + 1)
            for i in range(NHU):
                if late(t * NHU + i, 4) if isinstance(t, int) else True:
                    pe.wait_ge(hh_ready, t * NHU + i - 3)
                for a in range(HU):
                    m = i * HU + a
                    n = 0
                    for k in range(DK):
                        for wt, xx in ((w1h, xh), (w1h, xl), (w1l, xh)):
                            ins = pe.matmul(hp[i % 4][:, a * TS:(a + 1) * TS],
                                            wt[:, bass.ds(e, 1), k, m * P:(m + 1) * P], xx[:, par, k, :],
                                            start=(n == 0), stop=(n == 3 * DK - 1))
                            n += 1
                ins.then_inc(h_full, 1)

        def output(t, par):
            e = pe.value_load(expert_of[0:1, bass.ds(t, 1)], min_val=0, max_val=E - 1)
            pe.wait_ge(hl_ready, (t + 1) * NHU)
            if late(t, 2):
                pe.wait_ge(y_ready, t - 1)
            for j in range(SJ):
                out = yp[par][:, j * D:(j + 1) * D]
                pe.matmul(out, brow[:, :], b2s[:, bass.ds(e, 1), :], start=True, stop=False)
                for m in range(HM):
                    for hx, wt in ((hh, w2h), (hh, w2l), (hl, w2h)):
                        ins = pe.matmul(out, hx[:, par, m, j * P:(j + 1) * P], wt[:, bass.ds(e, 1), m, :], start=False,
                                        stop=(m == HM - 1 and hx is hl))
            ins.then_inc(y_full, 1)

        def tile(t, par, uses):
            hidden(t, par)
            if not (isinstance(t, int) and t == NTILES - 1):
                transpose(t + 1, 1 - par, uses + par)
            if late(t):
                output(t - 1, 1 - par)

        pe.wait_ge(const, 3)
        transpose(0, 0, 0)
        tiles(pe, tile)
        output(NTILES - 1, (NTILES - 1) % 2)

CG = 8

def combine(nc, ctx, t):
    def sb(name, shape, dt=fp32):
        return ctx.enter_context(nc.sbuf_tensor(name, shape, dt))

    def sem(name):
        return ctx.enter_context(nc.semaphore(name))

    xs, mv, rstd, nbias, tmpv, slots, gates = (t[k] for k in ("xs", "mv0", "rstd", "nbias", "tmpv", "slots", "gates"))
    NG = NT // CG
    yk = sb("yk", [P, NT, TOPK, D])
    res = sb("res", [P, NT, D])
    bst = sb("bst3", [P, NT, 6])
    got = [sem(f"c_got{i}") for i in range(NG)]
    steps = sem("c_steps")
    rooted = sem("c_rooted")
    done = sem("c_done")
    out_sent = sem("c_out_sent")
    PER = 4 + RSTD_STEPS
    block = ctx.enter_context(nc.Block())

    @block.gpsimd
    def _(pool):
        for j in range(NT):
            for k in range(TOPK):
                pool.indirect_dma_start(yk[:, j, k, :], None, t["ysort"],
                                        bass.IndirectOffsetOnAxis(ap=slots[:, k, j:j + 1], axis=0)).then_inc(got[j // CG], 16)

    @block.vector
    def _(dve):
        for g in range(NG):
            cols = slice(g * CG, (g + 1) * CG)
            dve.wait_ge(got[g], 16 * CG * TOPK)
            for k in range(TOPK):
                for j in range(g * CG, (g + 1) * CG):
                    ins = dve.scalar_tensor_tensor(out=xs[:, j, :], in0=yk[:, j, k, :], scalar=gates[:, k, j:j + 1],
                                                   in1=xs[:, j, :], op0=ALU.mult, op1=ALU.add)
                ins.then_inc(steps, 1)
                dve.wait_ge(steps, g * PER + k + 1)
            for j in range(g * CG, (g + 1) * CG):
                ins = dve.bn_stats(bst[:, j, :], xs[:, j, :])
            ins.then_inc(steps, 1)
            dve.wait_ge(steps, g * PER + 3)
            for j in range(g * CG, (g + 1) * CG):
                ins = dve.bn_aggr(mv[:, j, :], bst[:, j, :])
            ins.then_inc(steps, 1)
            dve.wait_ge(steps, g * PER + 4)
            rstd_vector(dve, mv, rstd, nbias, tmpv, steps, rooted, g * PER + 4, cols, g + 1)

    @block.scalar
    def _(act):
        for g in range(NG):
            rstd_scalar(act, tmpv, steps, rooted, g * PER + 4, slice(g * CG, (g + 1) * CG))
            act.wait_ge(steps, (g + 1) * PER)
            for j in range(g * CG, (g + 1) * CG):
                ins = act.activation(res[:, j, :], xs[:, j, :], ACT.Identity, scale=rstd[:, j:j + 1], bias=nbias[:, j:j + 1])
            ins.then_inc(done, 1)

    @block.sync
    def _(sp):
        ov = t["out"].rearrange("b (h p) d -> p (b h) d", p=P)
        for g in range(NG):
            sp.wait_ge(done, g + 1)
            sp.dma_start(ov[:, g * CG:(g + 1) * CG, :], res[:, g * CG:(g + 1) * CG, :]).then_inc(out_sent, 16)
        sp.wait_ge(out_sent, 16 * NG)

def decoder_layer(nc, a, out):
    def part(prefix):
        return {k[len(prefix):]: v for k, v in a.items() if k.startswith(prefix)}

    with ExitStack() as ctx:
        def sb(name, shape, dt=fp32):
            return ctx.enter_context(nc.sbuf_tensor(name, shape, dt))

        t = {
            "xs": sb("xs", [P, NT, D]),
            "ident": sb("ident", [P, P]),
            "mv0": sb("mv0", [P, NT, 2]),
            "mv1": sb("mv1", [P, NT, 2]),
            "rstd": sb("rstd", [P, NT]),
            "nbias": sb("nbias", [P, NT]),
            "tmpv": sb("tmpv", [P, 4, NT]),
            "slots": sb("slots", [P, TOPK, NT], i32),
            "gates": sb("gates", [P, TOPK, NT]),
            "expert_of": sb("expert_of", [1, NTILES], i32),
            "xsort": nc.dram_tensor("xsort", [NSLOT, D], fp32, kind="Internal").ap(),
            "ysort": nc.dram_tensor("ysort", [NSLOT, D], fp32, kind="Internal").ap(),
            "out": out,
        }
        with ExitStack() as stage:
            mixer(nc, stage, t | part("L0_attn_") | {"x": a["x"]})
        with ExitStack() as stage:
            attention(nc, stage, t | part("L0_xattn_") | {"ctx": a["ctx_1024"], "mask": a["mask_BxS2_bk0"]})
        with ExitStack() as weights:
            def wsb(name, shape, dt=fp16):
                return weights.enter_context(nc.sbuf_tensor(name, shape, dt))

            tw = t | part("L0_ffn_") | {
                "w1h": wsb("w1h", [P, E, DK, H]), "w1l": wsb("w1l", [P, E, DK, H]),
                "w2h": wsb("w2h", [P, E, HM, D]), "w2l": wsb("w2l", [P, E, HM, D]),
                "b1s": wsb("b1s", [P, E, HM], fp32), "b2s": wsb("b2s", [P, E, D]),
            }
            with ExitStack() as stage:
                router(nc, stage, tw)
            with ExitStack() as stage:
                experts(nc, stage, tw)
        with ExitStack() as stage:
            combine(nc, stage, t)

_INS = ["x", "ctx_1024", "mask_BxS2_bk0"] + [
    "L0_attn_" + n for n in ("ln_w", "ln_b", "W_in", "b_in", "conv_w", "conv_b", "A_log", "D", "W_x", "b_x", "W_out", "b_out")
] + ["L0_xattn_" + n for n in ("Wq", "Wkv", "Wout", "b_out")] + ["L0_ffn_" + n for n in ("Wr", "W1", "b1", "W2", "b2")]

def kernel(**inputs):
    import numpy as _np
    import concourse.bacc as _bacc
    from concourse import mybir as _mybir
    from concourse.bass_utils import run_bass_kernel_spmd as _run

    nc = _bacc.Bacc("TRN2", target_bir_lowering=False, num_devices=1)
    arrays, aps = {}, {}
    for name in _INS:
        a = _np.ascontiguousarray(inputs[name])
        if a.dtype.kind == "b":
            a = a.reshape(-1).view(_np.uint32)
        arrays[f"in_{name}"] = a
        aps[name] = nc.dram_tensor(f"in_{name}", a.shape, _mybir.dt.from_np(a.dtype), kind="ExternalInput").ap()
    out = nc.dram_tensor("out_0", (B, S, D), fp32, kind="ExternalOutput").ap()
    decoder_layer(nc, aps, out)
    r = _run(nc, [arrays], core_ids=[0])
    return _np.asarray(r.results[0]["out_0"])
```

```python
import concourse.bass as bass
from concourse import mybir
from contextlib import ExitStack
import numpy as np

fp32 = mybir.dt.float32
bf16 = mybir.dt.bfloat16
u32 = mybir.dt.uint32
ALU = mybir.AluOpType
ACT = mybir.ActivationFunctionType
AX = mybir.AxisListType

B, S, D = 16, 256, 256
P = 128
NT = B * S // P
DK = D // P
EPS = 1e-5

DI, NS, TAPS = 512, 16, 4
CT = DI // P
NPAIR = B // 2
TP = 2 * S
TT = TP // P
PADW = S + TAPS - 1
NBC = 2 * NS
U_XT, U_WIN, U_CONV, U_WX, U_FRONT = 0, DK, DK + CT, DK + 2 * CT, DK + 2 * CT + 1
U_GATE = CT
U_OUT = 2
U_ALL = U_OUT + U_GATE + U_FRONT
BLEAD, BRING = 3, 4
HRING = 8
ADDED = (0, 3, 6, 9)
ADD_LAG = 4
SUM_LAG, PAIR_LAG = 1, 4
SUM_STEP = []
for _n in range(NS):
    SUM_STEP.append(max(_n + (PAIR_LAG if _n in ADDED else SUM_LAG), SUM_STEP[-1] if _n else 0))
CRING = 2

def front_unit(q, k):
    if isinstance(q, int) and q == 0:
        return k
    return q * U_ALL - (U_ALL - U_FRONT - U_GATE) + k

def gate_unit(p, k):
    return p * U_ALL + U_FRONT + k

def out_unit(p, k):
    last = isinstance(p, int) and p == NPAIR - 1
    return (p + 1) * U_ALL + (0 if last else U_FRONT) - U_OUT + k

def mixer(nc, ctx, t):
    def sb(name, shape, dt=fp32):
        return ctx.enter_context(nc.sbuf_tensor(name, shape, dt))

    def sem(name):
        return ctx.enter_context(nc.semaphore(name))

    xs, ident, mv0, mv1, rstd, nbias, tmpv = t["xs"], t["ident"], t["mv0"], t["mv1"], t["rstd"], t["nbias"], t["tmpv"]
    win = sb("win", [P, DK, 2 * DI])
    wout = sb("wout", [P, CT, D])
    wx3 = sb("wx3", [P, CT, 3 * NBC])
    bx3 = sb("bx3", [3 * NBC, 1])
    bin_ = sb("bin", [P, 2 * CT])
    lnw = sb("lnw", [P, DK])
    lnb = sb("lnb", [P, DK])
    cw = sb("cw", [P, CT, TAPS])
    cb = sb("cb", [P, CT])
    dsk = sb("dsk", [P, CT])
    alog = sb("alog", [P, CT, NS])
    bob = sb("bob", [P, D])
    cdiag = sb("cdiag", [P, CT, TAPS, P])
    ddiag = sb("ddiag", [P, CT, P])
    sel0 = sb("sel0", [3 * NBC, NBC], bf16)
    sel = sb("sel", [3 * NBC, NBC, P], bf16)
    xn = sb("xn", [P, TT, D])
    xnT = sb("xnT", [P, DK, TP])
    xm = sb("xm", [P, CT, 2, PADW])
    gs = sb("gs", [P, CT, TP])
    xc = sb("xc", [P, 2, CT, TP])
    rest = sb("rest", [3 * NBC, TP])
    parts = sb("parts", [3 * NBC, 2, TP], bf16)
    bring = sb("bring", [P, BRING, TP])
    cring = sb("cring", [P, CRING, TP])
    h = sb("h", [P, HRING, CT, TP])
    otmp = sb("otmp", [P, TT, D])
    bst = sb("bst", [P, TT, 6])
    mvt = sb("mvt", [P, TT, 2])

    y = ctx.enter_context(nc.psum_tensor("y", [P, CT, TP], fp32))
    fb = [ctx.enter_context(nc.psum_tensor(f"fb{i}", [P, TP], fp32)) for i in range(2)]
    bbank = ctx.enter_context(nc.psum_tensor("bbank", [P, TP], fp32))
    cbank = ctx.enter_context(nc.psum_tensor("cbank", [P, TP], fp32))

    loaded = sem("m_loaded")
    xloaded = [sem(f"m_xloaded{i}") for i in range(2)]
    made = sem("m_made")
    tables = sem("m_tables")
    adecay = sem("m_adecay")
    stats = sem("m_stats")
    rooted = sem("m_rooted")
    xn_ready = sem("m_xn")
    fb_full = sem("m_fb_full")
    fb_free = sem("m_fb_free")
    split1 = sem("m_split1")
    split2 = sem("m_split2")
    b_sent = sem("m_b_sent")
    b_kept = sem("m_b_kept")
    u_ready = sem("m_u")
    h_ready = sem("m_h")
    c_sent = sem("m_c_sent")
    c_kept = sem("m_c_kept")
    hc_ready = sem("m_hc")
    added = sem("m_added")
    summed = sem("m_summed")
    gated = sem("m_gated")
    z_steps = sem("m_z")

    z_seen = sem("m_z_seen")
    mv_kept = sem("m_mv_kept")

    N_LOADS = 16
    block = ctx.enter_context(nc.Block())

    @block.sync
    def _(sp):
        with nc.allow_non_contiguous_dma(reason="short vectors and tables"):
            xd = t["x"].rearrange("b (h p) d -> p (b h) d", p=P)
            for i in range(2):
                half = slice(i * NT // 2, (i + 1) * NT // 2)
                sp.dma_start(xs[:, half, :], xd[:, half, :]).then_inc(xloaded[i], 16)
            loads = [
                (win[:, :, :], t["W_in"].rearrange("(k p) n -> p k n", p=P)),
                (wout[:, :, :], t["W_out"].rearrange("(k p) n -> p k n", p=P)),
                (bin_[:, :], t["b_in"].rearrange("(m p) -> p m", p=P)),
                (lnw[:, :], t["ln_w"].rearrange("(k p) -> p k", p=P)),
                (lnb[:, :], t["ln_b"].rearrange("(k p) -> p k", p=P)),
                (cw[:, :, :], t["conv_w"].rearrange("(c p) o k -> p c (o k)", p=P)),
                (cb[:, :], t["conv_b"].rearrange("(c p) -> p c", p=P)),
                (dsk[:, :], t["D"].rearrange("(c p) -> p c", p=P)),
                (alog[:, :, :], t["A_log"].rearrange("(c p) n -> p c n", p=P)),
                (bob[:, :], t["b_out"].rearrange("(a n) -> a n", a=1).to_broadcast([P, D])),
            ]
            for g in range(3):
                loads.append((wx3[:, :, g * NBC:(g + 1) * NBC], t["W_x"].rearrange("(c p) n -> p c n", p=P)))
                loads.append((bx3[g * NBC:(g + 1) * NBC, :], t["b_x"].rearrange("(n a) -> n a", a=1)))
            assert len(loads) == N_LOADS
            for dst, src in loads:
                sp.dma_start(dst, src).then_inc(loaded, 16)

    @block.gpsimd
    def _(pool):
        pool.memset(ident[:, :], 0.0).then_inc(made, 1)
        pool.memset(sel0[:, :], 0.0).then_inc(made, 1)
        pool.memset(xm[:, :, :, :], 0.0).then_inc(made, 1)
        pool.wait_ge(made, 3)
        pool.affine_select(out=ident[:, :], in_=ident[:, :], compare_op=ALU.not_equal, fill=1.0,
                           base=0, pattern=[[-1, P]], channel_multiplier=1).then_inc(made, 1)
        for g in range(3):
            pool.affine_select(out=sel0[:, :], in_=sel0[:, :], compare_op=ALU.not_equal, fill=1.0,
                               base=-g * NBC, pattern=[[-1, NBC]], channel_multiplier=1).then_inc(made, 1)
            pool.wait_ge(made, 5 + g)

        def add(p, n):
            pool.wait_ge(hc_ready, p * NS + n + 2)
            pool.tensor_tensor(out=h[:, n % HRING, :, :], in0=h[:, n % HRING, :, :], in1=h[:, (n + 1) % HRING, :, :],
                               op=ALU.add).then_inc(added, 1)

        def pair(p, par):
            for n in range(NS):
                i = p * NS + n
                slot = n % BRING
                pool.wait_ge(b_kept, i + 1)
                if not isinstance(i, int) or i >= HRING:
                    pool.wait_ge(summed, i - HRING + 1)
                pool.tensor_tensor(out=h[:, n % HRING, :, :], in0=xc[:, par, :, :],
                                   in1=bring[:, slot:slot + 1, :].to_broadcast([P, CT, TP]),
                                   op=ALU.mult).then_inc(u_ready, 1)
                if n - ADD_LAG in ADDED:
                    add(p, n - ADD_LAG)

        pair(0, 0)
        with pool.Fori(0, NPAIR // 2 - 1) as it:
            pair(it * 2 + 1, 1)
            pair(it * 2 + 2, 0)
        pair(NPAIR - 1, 1)

    @block.vector
    def _(dve):
        dve.sem_inc(z_steps, 4)
        for i in range(NT):
            if i % (NT // 2) == 0:
                dve.wait_ge(xloaded[i // (NT // 2)], 16)
            if i >= TT:
                dve.wait_ge(stats, 2 * (i - TT) + 2)
            dve.bn_stats(bst[:, i % TT, :], xs[:, i, :]).then_inc(stats, 1)
            dve.wait_ge(stats, 2 * i + 1)
            dve.bn_aggr(mv0[:, i, :], bst[:, i % TT, :]).then_inc(stats, 1)
        n = 2 * NT
        dve.wait_ge(stats, n)
        n = rstd_vector(dve, mv0, rstd, nbias, tmpv, stats, rooted, n)
        dve.wait_ge(loaded, 16 * N_LOADS)
        dve.wait_ge(made, 7)
        for c in range(CT):
            for k in range(TAPS):
                dve.tensor_scalar(cdiag[:, c, k, :], ident[:, :], cw[:, c, k:k + 1], None, ALU.mult)
            dve.tensor_scalar(ddiag[:, c, :], ident[:, :], dsk[:, c:c + 1], None, ALU.mult)
        dve.tensor_copy(sel[:, :, :], sel0[:, :].rearrange("p (n a) -> p n a", a=1).to_broadcast([3 * NBC, NBC, P])).then_inc(tables, 1)

        def split(q, par, step):
            if step == 0:
                dve.wait_ge(split2, q * 4 + 2)
                dve.tensor_tensor(out=rest[:, :], in0=rest[:, :], in1=parts[:, par, :],
                                  op=ALU.subtract).then_inc(split1, 1)
            else:
                dve.wait_ge(split2, q * 4 + 3)
                lo = slice(2 * NBC, 3 * NBC)
                dve.tensor_tensor(out=rest[lo, :], in0=rest[lo, :], in1=parts[lo, par, :],
                                  op=ALU.subtract).then_inc(split1, 1)

        def residual(p, step):
            tiles = bass.ds(p * TT, TT)
            if step == 0:
                dve.wait_ge(fb_free, out_unit(p, 1) + 1)
                dve.scalar_tensor_tensor(out=xs[:, tiles, :], in0=xs[:, tiles, :], scalar=2.0,
                                         in1=otmp[:, :, :], op0=ALU.mult, op1=ALU.add).then_inc(z_steps, 1)
            elif step == 1:
                dve.wait_ge(z_steps, (p + 1) * 4 + 1)
                dve.tensor_tensor(out=xs[:, tiles, :], in0=xs[:, tiles, :],
                                  in1=bob[:, :].rearrange("p (a n) -> p a n", a=1).to_broadcast([P, TT, D]),
                                  op=ALU.add).then_inc(z_steps, 1)
            elif step == 2:
                dve.wait_ge(z_steps, (p + 1) * 4 + 2)
                dve.sem_inc(z_seen, 1)
                for j in range(TT):
                    ins = dve.bn_stats(bst[:, j, :], xs[:, bass.ds(p * TT + j, 1), :])
                ins.then_inc(z_steps, 1)
            elif step == 3:
                dve.wait_ge(z_steps, (p + 1) * 4 + 3)
                if not (isinstance(p, int) and p == 0):
                    dve.wait_ge(mv_kept, p)
                dve.sem_inc(z_seen, 1)
                for j in range(TT):
                    ins = dve.bn_aggr(mvt[:, j, :], bst[:, j, :])
                ins.then_inc(z_steps, 1)
            else:
                dve.wait_ge(z_steps, (p + 1) * 4 + 4)
                dve.tensor_copy(mv1[:, tiles, :], mvt[:, :, :]).then_inc(mv_kept, 1)

        def scan(p, n, par):
            i = p * NS + n
            dve.wait_ge(u_ready, i + 1)
            for c in range(CT):
                for b in range(2):
                    ins = dve.tensor_tensor_scan(
                        out=h[:, n % HRING, c, b * S:(b + 1) * S],
                        data0=alog[:, c, n:n + 1].to_broadcast([P, S]),
                        data1=h[:, n % HRING, c, b * S:(b + 1) * S],
                        initial=0.0, op0=ALU.mult, op1=ALU.add)
            ins.then_inc(h_ready, 1)

        def times_c(p, n):
            i = p * NS + n
            dve.wait_ge(h_ready, i + 1)
            dve.wait_ge(c_kept, i + 1)
            dve.tensor_tensor(out=h[:, n % HRING, :, :], in0=h[:, n % HRING, :, :],
                              in1=cring[:, n % CRING:n % CRING + 1, :].to_broadcast([P, CT, TP]),
                              op=ALU.mult).then_inc(hc_ready, 1)

        def gate(p):
            dve.wait_ge(fb_free, gate_unit(p, CT - 1) + 1)
            dve.wait_ge(summed, p * NS + NS)
            dve.tensor_tensor(out=gs[:, :, :], in0=y[:, :, :], in1=gs[:, :, :],
                              op=ALU.mult).then_inc(gated, 1)

        def pair(p, par, last, before, after):
            for n in range(NS):
                scan(p, n, par)
                if n == 1 and before:
                    gate(p - 1)
                if n:
                    times_c(p, n - 1)
                if before and 3 <= n < 8:
                    residual(p - 1, n - 3)
                if after and n == 11:
                    split(p + 1, 1 - par, 0)
                if after and n == 12:
                    split(p + 1, 1 - par, 1)
            times_c(p, NS - 1)

        dve.wait_ge(adecay, 2)
        split(0, 0, 0)
        split(0, 0, 1)
        pair(0, 0, False, False, True)
        with dve.Fori(0, NPAIR // 2 - 1) as it:
            pair(it * 2 + 1, 1, False, True, True)
            pair(it * 2 + 2, 0, False, True, True)
        pair(NPAIR - 1, 1, True, True, False)
        gate(NPAIR - 1)
        for step in range(5):
            residual(NPAIR - 1, step)

    @block.scalar
    def _(act):
        act.wait_ge(loaded, 16 * N_LOADS)
        act.activation(alog[:, :, :], alog[:, :, :], ACT.Exp).then_inc(adecay, 1)
        act.wait_ge(adecay, 1)
        act.activation(alog[:, :, :], alog[:, :, :], ACT.Exp, scale=-1.0).then_inc(adecay, 1)
        rstd_scalar(act, tmpv, stats, rooted, 2 * NT)
        act.wait_ge(stats, 2 * NT + RSTD_STEPS)
        act.wait_ge(made, 3)

        def take(unit, out, fn, rows=P, **kw):
            bank = unit[1]
            act.wait_ge(fb_full, unit[0] + 1)
            act.activation(out, fb[bank][0:rows, :], fn, **kw).then_inc(fb_free, 1)

        def fu(q, par, k):
            return front_unit(q, k), bank_of(q, par, k)

        def normalise(q):
            for j in range(TT):
                tile = bass.ds(q * TT + j, 1)
                ins = act.activation(xn[:, j, :], xs[:, tile, :], ACT.Identity,
                                     scale=rstd[:, tile], bias=nbias[:, tile])
            ins.then_inc(xn_ready, 1)

        def keep_b(p, n):
            i = p * NS + n
            act.wait_ge(b_sent, i + 1)
            if not isinstance(i, int) or i >= BRING:
                act.wait_ge(u_ready, i - BRING + 1)
            act.activation(bring[:, n % BRING, :], bbank[:, :], ACT.Copy).then_inc(b_kept, 1)

        def keep_c(p, n):
            i = p * NS + n
            act.wait_ge(c_sent, i + 1)
            if not isinstance(i, int) or i >= CRING:
                act.wait_ge(hc_ready, i - CRING + 1)
            act.activation(cring[:, n % CRING, :], cbank[:, :], ACT.Copy).then_inc(c_kept, 1)

        def front(q, par, step):
            if step == 0:
                normalise(q)
                for k in range(DK):
                    take(fu(q, par, U_XT + k), xnT[:, k, :], ACT.Identity, scale=lnw[:, k:k + 1], bias=lnb[:, k:k + 1])
            elif step <= 2:
                for m in (2 * step - 2, 2 * step - 1):
                    act.wait_ge(fb_full, front_unit(q, U_WIN + m) + 1)
                    act.activation(xm[:, m, :, TAPS - 1:PADW], fb[bank_of(q, par, U_WIN + m)][:, :].rearrange("p (b s) -> p b s", b=2),
                                   ACT.Identity, bias=bin_[:, m:m + 1]).then_inc(fb_free, 1)
            elif step <= 6:
                if step == 3 and not (isinstance(q, int) and q < 2):
                    act.wait_ge(gated, q - 1)
                c = step - 3
                take(fu(q, par, U_CONV + c), xc[:, par, c, :], ACT.Silu, bias=cb[:, c:c + 1])
            elif step == 7:
                if not (isinstance(q, int) and q == 0):
                    act.wait_ge(split2, q * 4)
                act.wait_ge(fb_full, front_unit(q, U_WX) + 1)
                act.activation(rest[:, :], fb[bank_of(q, par, U_WX)][0:3 * NBC, :], ACT.Identity,
                               bias=bx3[:, :]).then_inc(split2, 1)
                act.activation(parts[:, par, :], fb[bank_of(q, par, U_WX)][0:3 * NBC, :], ACT.Identity,
                               bias=bx3[:, :]).then_inc(split2, 1)
                act.wait_ge(split2, q * 4 + 2)
                act.sem_inc(fb_free, 1)
            elif step == 8:
                act.wait_ge(split1, q * 2 + 1)
                mid, lo = slice(NBC, 2 * NBC), slice(2 * NBC, 3 * NBC)
                act.activation(parts[mid, par, :], rest[mid, :], ACT.Copy)
                act.activation(parts[lo, par, :], rest[lo, :], ACT.Copy).then_inc(split2, 1)
            else:
                lo = slice(2 * NBC, 3 * NBC)
                act.wait_ge(split1, q * 2 + 2)
                act.activation(parts[lo, par, :], rest[lo, :], ACT.Copy).then_inc(split2, 1)

        def gate(p, par, half):
            for m in (2 * half, 2 * half + 1):
                take((gate_unit(p, m), gate_bank(p, par, m)), gs[:, m, :], ACT.Silu, bias=bin_[:, CT + m:CT + m + 1])

        def project_out(p, par):
            act.wait_ge(z_steps, p * 4 + 1)
            for k in range(U_OUT):
                act.wait_ge(fb_full, out_unit(p, k) + 1)
                act.activation(otmp[:, 2 * k:2 * k + 2, :],
                               fb[out_bank(p, par, k)][:, :].rearrange("p (a n) -> p a n", a=2),
                               ACT.Copy).then_inc(fb_free, 1)

        def pair(p, par, before, after):
            for n in range(NS):
                if n + BLEAD < NS:
                    keep_b(p, n + BLEAD)
                elif after:
                    keep_b(p + 1, n + BLEAD - NS)
                if n + 1 < NS:
                    keep_c(p, n + 1)
                elif after:
                    keep_c(p + 1, 0)
                if before and n == 0:
                    project_out(p - 1, 1 - par)
                if 1 <= n < 3:
                    gate(p, par, n - 1)
                if after and 2 <= n < 12:
                    front(p + 1, 1 - par, n - 2)

        for step in range(10):
            front(0, 0, step)
        for n in range(BLEAD):
            keep_b(0, n)
        keep_c(0, 0)
        pair(0, 0, False, True)
        with act.Fori(0, NPAIR // 2 - 1) as it:
            pair(it * 2 + 1, 1, True, True)
            pair(it * 2 + 2, 0, True, True)
        pair(NPAIR - 1, 1, True, False)
        project_out(NPAIR - 1, 1)

    @block.tensor
    def _(pe):
        pe.wait_ge(made, 7)
        pe.wait_ge(tables, 1)
        pe.wait_ge(loaded, 16 * N_LOADS)

        def free_bank(unit):
            if not isinstance(unit, int) or unit >= 2:
                pe.wait_ge(fb_free, unit - 1)

        def front(q, par, step):
            if step == 0:
                pe.wait_ge(xn_ready, q + 1)
                for k in range(DK):
                    free_bank(front_unit(q, U_XT + k))
                    bank = fb[bank_of(q, par, U_XT + k)]
                    for j in range(TT):
                        ins = pe.transpose(bank[:, j * P:(j + 1) * P], xn[:, j, k * P:(k + 1) * P], ident[:, :])
                    ins.then_inc(fb_full, 1)
            elif step <= 2:
                pe.wait_ge(fb_free, front_unit(q, U_XT + DK - 1) + 1)
                for m in (2 * step - 2, 2 * step - 1):
                    free_bank(front_unit(q, U_WIN + m))
                    for k in range(DK):
                        ins = pe.matmul(fb[bank_of(q, par, U_WIN + m)][:, :], win[:, k, m * P:(m + 1) * P],
                                        xnT[:, k, :], start=(k == 0), stop=(k == DK - 1))
                    ins.then_inc(fb_full, 1)
            elif step <= 6:
                c = step - 3
                free_bank(front_unit(q, U_CONV + c))
                for k in range(TAPS):
                    ins = pe.matmul(fb[bank_of(q, par, U_CONV + c)][:, :].rearrange("p (b s) -> p b s", b=2),
                                    cdiag[:, c, k, :], xm[:, c, :, k:k + S],
                                    start=(k == 0), stop=(k == TAPS - 1))
                ins.then_inc(fb_full, 1)
            elif step == 7:
                pe.wait_ge(fb_free, front_unit(q, U_CONV + CT - 1) + 1)
                for c in range(CT):
                    ins = pe.matmul(fb[bank_of(q, par, U_WX)][0:3 * NBC, :], wx3[:, c, :], xc[:, par, c, :],
                                    start=(c == 0), stop=(c == CT - 1))
                ins.then_inc(fb_full, 1)

        def gate(p, par, half):
            for m in (2 * half, 2 * half + 1):
                free_bank(gate_unit(p, m))
                for k in range(DK):
                    ins = pe.matmul(fb[gate_bank(p, par, m)][:, :], win[:, k, (CT + m) * P:(CT + m + 1) * P],
                                    xnT[:, k, :], start=(k == 0), stop=(k == DK - 1))
                ins.then_inc(fb_full, 1)

        def project_out(p, par):
            pe.wait_ge(gated, p + 1)
            for k in range(U_OUT):
                free_bank(out_unit(p, k))
                for a in range(2):
                    j = 2 * k + a
                    for c in range(CT):
                        ins = pe.matmul(fb[out_bank(p, par, k)][:, a * D:(a + 1) * D], gs[:, c, j * P:(j + 1) * P],
                                        wout[:, c, :], start=(c == 0), stop=(c == CT - 1))
                ins.then_inc(fb_full, 1)

        def send_b(p, par, n):
            i = p * NS + n
            if n == 0:
                pe.wait_ge(split2, p * 4 + 4)
            if not isinstance(i, int) or i >= 1:
                pe.wait_ge(b_kept, i)
            pe.matmul(bbank[:, :], sel[:, n, :], parts[:, par, :], start=True, stop=True).then_inc(b_sent, 1)

        def send_c(p, par, n):
            i = p * NS + n
            if not isinstance(i, int) or i >= 1:
                pe.wait_ge(c_kept, i)
            pe.matmul(cbank[:, :], sel[:, NS + n, :], parts[:, par, :], start=True, stop=True).then_inc(c_sent, 1)

        def add_up(p, n):
            if n - 1 in ADDED:
                return
            if n in ADDED:
                pe.wait_ge(added, p * len(ADDED) + ADDED.index(n) + 1)
            else:
                pe.wait_ge(hc_ready, p * NS + n + 1)
            for c in range(CT):
                ins = pe.matmul(y[:, c, :], ident[:, :], h[:, n % HRING, c, :], start=False, stop=(n == NS - 1))
            ins.then_inc(summed, 2 if n in ADDED else 1)

        def skip(p, par):
            if not (isinstance(p, int) and p == 0):
                pe.wait_ge(gated, p)
            for c in range(CT):
                pe.matmul(y[:, c, :], ddiag[:, c, :], xc[:, par, c, :], start=True, stop=False)

        def pair(p, par, before, after):
            for n in range(NS):
                if n + BLEAD < NS:
                    send_b(p, par, n + BLEAD)
                elif after:
                    send_b(p + 1, 1 - par, n + BLEAD - NS)
                if n + 1 < NS:
                    send_c(p, par, n + 1)
                elif after:
                    send_c(p + 1, 1 - par, 0)
                if n == 0:
                    skip(p, par)
                for m in range(NS):
                    if SUM_STEP[m] == n:
                        add_up(p, m)
                if before and n == 0:
                    project_out(p - 1, 1 - par)
                if 1 <= n < 3:
                    gate(p, par, n - 1)
                if after and 2 <= n < 10:
                    front(p + 1, 1 - par, n - 2)
            for m in range(NS):
                if SUM_STEP[m] >= NS:
                    add_up(p, m)

        for step in range(8):
            front(0, 0, step)
        for n in range(BLEAD):
            send_b(0, 0, n)
        send_c(0, 0, 0)
        pair(0, 0, False, True)
        with pe.Fori(0, NPAIR // 2 - 1) as it:
            pair(it * 2 + 1, 1, True, True)
            pair(it * 2 + 2, 0, True, True)
        pair(NPAIR - 1, 1, True, False)
        project_out(NPAIR - 1, 1)

def bank_of(q, par, k):
    return front_unit(q if isinstance(q, int) else par + 2, k) % 2

def gate_bank(p, par, k):
    return gate_unit(p if isinstance(p, int) else par, k) % 2

def out_bank(p, par, k):
    return out_unit(p if isinstance(p, int) else par, k) % 2

RSTD_STEPS = 8

def rstd_scalar(act, tmpv, stats, rooted, n, cols=slice(0, NT)):
    act.wait_ge(stats, n + 1)
    act.activation(tmpv[:, 1, cols], tmpv[:, 0, cols], ACT.Sqrt).then_inc(rooted, 1)

def rstd_vector(dve, mv, rstd, nbias, tmpv, stats, rooted, n, cols=slice(0, NT), turn=1):
    var, root, a, b = (tmpv[:, k, cols] for k in range(4))
    at = n

    def link(ins):
        nonlocal at
        at += 1
        ins.then_inc(stats, 1)
        dve.wait_ge(stats, at)

    link(dve.tensor_scalar(var, mv[:, cols, 1], EPS, None, ALU.add))
    dve.wait_ge(rooted, turn)
    link(dve.reciprocal(a, root))
    link(dve.tensor_tensor(out=b, in0=a, in1=a, op=ALU.mult))
    link(dve.tensor_tensor(out=b, in0=b, in1=var, op=ALU.mult))
    link(dve.tensor_scalar(b, b, -0.5, 1.5, ALU.mult, ALU.add))
    link(dve.tensor_tensor(out=rstd[:, cols], in0=a, in1=b, op=ALU.mult))
    link(dve.tensor_tensor(out=nbias[:, cols], in0=rstd[:, cols], in1=mv[:, cols, 0], op=ALU.mult))
    link(dve.tensor_scalar(nbias[:, cols], nbias[:, cols], -1.0, None, ALU.mult))
    return at

HEADS, DH, KEYS = 16, 64, 77
INNER = HEADS * DH
MT = INNER // P
JT = S // P
SBANKS = [(0, 6), (6, 11), (11, 16)]
NSB = len(SBANKS)
KCHUNK = 6
TH = 4
NTB = HEADS // TH
GB = 3
G_O, G_OUT, G_V, G_Q = MT // 2, JT, INNER // 512, MT // 2
G_BACK, G_FRONT = G_O + G_OUT, G_V + G_Q
G_ALL = G_BACK + G_FRONT
T_ALL = 1 + JT * NTB
MASKED = -1e30

def gfront(b, k):
    if isinstance(b, int) and b == 0:
        return k
    return b * G_ALL - G_BACK + k

def gback(b, k):
    last = isinstance(b, int) and b == B - 1
    return (b + 1) * G_ALL + k - (G_FRONT if last else 0)

def gbank(k):
    return k % GB

def txunit(b):
    return 0 if isinstance(b, int) and b == 0 else (b - 1) * T_ALL + 1

def tpunit(b, k):
    last = isinstance(b, int) and b == B - 1
    return b * T_ALL + k + (1 if last else 2)

def tx_bank(b, par):
    return (txunit(b) if isinstance(b, int) else par) % 2

def tp_bank(b, par, k):
    return (tpunit(b, k) if isinstance(b, int) else par + k) % 2

assert G_FRONT % GB == 0 and G_BACK % GB == 0 and T_ALL % 2 == 1 and B % 2 == 0

def attention(nc, ctx, t):
    def sb(name, shape, dt=fp32):
        return ctx.enter_context(nc.sbuf_tensor(name, shape, dt))

    def sem(name):
        return ctx.enter_context(nc.semaphore(name))

    xs, ident, mv0, mv1, rstd, nbias, tmpv = t["xs"], t["ident"], t["mv0"], t["mv1"], t["rstd"], t["nbias"], t["tmpv"]
    wq = sb("wq", [P, DK, INNER])
    wv = sb("wv", [P, DK, INNER])
    wo = sb("wo", [P, MT, D])
    bo = sb("bo", [P, D])
    cxT = sb("cxT", [P, DK, B * KEYS])
    kT = sb("kT", [P, MT, B * KEYS])
    v = sb("v", [KEYS, 2, INNER])
    x1 = sb("x1", [P, 2, JT, D])
    cxb = sb("cxb", [P, 2, DK, KEYS])
    xT = sb("xT", [P, DK, S])
    q = sb("q", [P, 2, 2, MT, S])
    mrow8 = sb("mrow8", [1, B * KEYS // 4], u32)
    mrow = sb("mrow", [P, B * KEYS], bf16)
    first = sb("first", [P, P], bf16)
    nmax = sb("nmax", [P, JT, HEADS])
    rsum = sb("rsum", [P, JT, HEADS])
    rinv = sb("rinv", [P, JT, HEADS])
    pr = sb("pr", [P, JT, HEADS, KEYS])
    pn = sb("pn", [P, JT, HEADS, KEYS])
    pT = sb("pT", [KEYS, HEADS, S])
    oT = sb("oT", [P, MT, S])
    bst = sb("bst2", [P, JT, 6])
    mvt = sb("mvt2", [P, JT, 2])
    assert (B, D) == (HEADS, S) and MT * S == DK * INNER
    cx = pT[:, :, :]
    wk = oT[:, :, :].rearrange("p (k m) s -> p k (m s)", k=DK)
    sc = ctx.enter_context(nc.psum_tensor("sc", [P, NSB, 512], fp32))
    tb = [ctx.enter_context(nc.psum_tensor(f"tb{i}", [P, TH * P], fp32)) for i in range(2)]
    g = [ctx.enter_context(nc.psum_tensor(f"g{i}", [P, 512], fp32)) for i in range(GB)]

    loaded = [sem(f"a_loaded{i}") for i in range(4)]
    stats = sem("a_stats")
    rooted = sem("a_rooted")
    const = sem("a_const")
    maskrow = sem("a_maskrow")
    p_full = sem("a_p_full")
    p_free = sem("a_p_free")
    x1_ready = sem("a_x1")
    g_full = sem("a_g_full")
    g_free = sem("a_g_free")
    s_full = sem("a_s_full")
    maxed = sem("a_maxed")
    exped = sem("a_exped")
    inverted = sem("a_inverted")
    pn_ready = sem("a_pn")
    t_full = sem("a_t_full")
    t_free = sem("a_t_free")
    z_steps = sem("a_z")
    z_seen = sem("a_z_seen")
    mv_kept = sem("a_mv_kept")
    cx_ready = sem("a_cx")

    zero_made = sem("a_zero_made")
    zero_sent = sem("a_zero_sent")
    zero = sb("zero", [P, D])

    KB = [(a, min(a + KCHUNK, B)) for a in range(0, B, KCHUNK)]
    XPB = 3
    XB = [(a, min(a + XPB, B)) for a in range(0, B, XPB)]
    NX = len(XB)

    with nc.Block() as block:
        @block.sync
        def _(sp):
            sp.dma_start(cx, t["ctx"].rearrange("b k d -> k b d")).then_inc(loaded[0], 16)
            wkv = t["Wkv"].rearrange("(k p) n -> p k n", p=P)
            sp.dma_start(wk, wkv[:, :, 0:INNER]).then_inc(loaded[1], 16)
            sp.dma_start(wv[:, :, :], wkv[:, :, INNER:2 * INNER]).then_inc(loaded[3], 16)
            sp.dma_start(wq[:, :, :], t["Wq"].rearrange("(k p) n -> p k n", p=P)).then_inc(loaded[2], 16)
            sp.dma_start(mrow8[:, :], t["mask"].rearrange("(a n) -> a n", a=1)).then_inc(loaded[2], 16)
            sp.dma_start(wo[:, :, :], t["Wout"].rearrange("(k p) n -> p k n", p=P)).then_inc(loaded[3], 16)
            sp.dma_start(bo[:, :], t["b_out"].rearrange("(a n) -> a n", a=1).to_broadcast([P, D])).then_inc(loaded[3], 16)

        @block.gpsimd
        def _(pool):
            pool.memset(zero[:, :], 0.0).then_inc(zero_made, 1)
            pool.memset(first[:, :], 0.0).then_inc(const, 1)
            pool.memset(mrow[:, :], 0.0).then_inc(const, 1)
            pool.wait_ge(const, 1)
            pool.memset(first[0:1, :], 1.0).then_inc(const, 1)
            pool.memset(q[:, :, :, :, :], 0.0).then_inc(const, 1)

        @block.vector
        def _(dve):
            rstd_vector(dve, mv1, rstd, nbias, tmpv, stats, rooted, 0)
            dve.wait_ge(loaded[2], 32)
            dve.wait_ge(const, 2)
            dve.tensor_scalar(mrow[0:1, :], mrow8[:, :].bitcast(mybir.dt.uint8), MASKED, None, ALU.mult).then_inc(maskrow, 1)

        @block.scalar
        def _(act):
            rstd_scalar(act, tmpv, stats, rooted, 0)
            unit = 0
            for a, e in XB:
                for k in range(DK):
                    act.wait_ge(p_full, unit + 1)
                    act.activation(cxT[:, k, a * KEYS:e * KEYS], g[unit % 2][:, 0:(e - a) * KEYS], ACT.Copy).then_inc(p_free, 1)
                    unit += 1
            for m in range(MT):
                for a, e in KB:
                    act.wait_ge(p_full, unit + 1)
                    act.activation(kT[:, m, a * KEYS:e * KEYS], g[unit % 2][:, 0:(e - a) * KEYS], ACT.Copy).then_inc(p_free, 1)
                    unit += 1

        @block.tensor
        def _(pe):
            pe.wait_ge(loaded[0], 16)
            unit = 0
            for a, e in XB:
                for k in range(DK):
                    if unit >= 2:
                        pe.wait_ge(p_free, unit - 1)
                    for b in range(a, e):
                        ins = pe.transpose(g[unit % 2][:, (b - a) * KEYS:(b - a + 1) * KEYS],
                                           cx[:, b, k * P:(k + 1) * P], ident[0:KEYS, 0:KEYS])
                    ins.then_inc(p_full, 1)
                    unit += 1
            pe.wait_ge(loaded[1], 16)
            pe.wait_ge(p_free, NX * DK)
            for m in range(MT):
                for a, e in KB:
                    pe.wait_ge(p_free, unit - 1)
                    for k in range(DK):
                        ins = pe.matmul(g[unit % 2][:, 0:(e - a) * KEYS], wk[:, k, m * P:(m + 1) * P],
                                        cxT[:, k, a * KEYS:e * KEYS], start=(k == 0), stop=(k == DK - 1))
                    ins.then_inc(p_full, 1)
                    unit += 1

    block = ctx.enter_context(nc.Block())

    def batches(eng, body):
        body(0, 0, False, True)
        with eng.Fori(0, B // 2 - 1) as it:
            body(it * 2 + 1, 1, True, True)
            body(it * 2 + 2, 0, True, True)
        body(B - 1, 1, True, False)

    @block.sync
    def _(sp):
        sp.wait_ge(zero_made, 1)
        zeroed = t["xsort"].rearrange("(n p) d -> p n d", p=P)
        sp.dma_start(zeroed, zero[:, :].rearrange("p (a d) -> p a d", a=1).to_broadcast([P, zeroed.shape[1], D])).then_inc(zero_sent, 16)
        sp.wait_ge(zero_sent, 16)

    @block.gpsimd
    def _(pool):
        def keep_context(b, par):
            pool.tensor_copy(cxb[:, par, :, :], cxT[:, :, bass.ds(b * KEYS, KEYS)]).then_inc(cx_ready, 1)

        def norm_p(b, j):
            pool.wait_ge(inverted, 2 * b + j + 1)
            if not (isinstance(b, int) and b == 0):
                pool.wait_ge(t_full, tpunit(b - 1, (j + 1) * NTB - 1) + 1)
            pool.tensor_tensor(out=pn[:, j, :, :], in0=pr[:, j, :, :],
                               in1=rinv[:, j, :].rearrange("p (h a) -> p h a", a=1).to_broadcast([P, HEADS, KEYS]),
                               op=ALU.mult).then_inc(pn_ready, 1)

        def batch(b, par, before, after):
            if after:
                keep_context(b + 1, 1 - par)
            norm_p(b, 0)
            norm_p(b, 1)

        keep_context(0, 0)
        batches(pool, batch)

    @block.vector
    def _(dve):
        def maxima(b, j):
            for i, (a, e) in enumerate(SBANKS):
                dve.wait_ge(s_full, (2 * b + j) * NSB + i + 1)
                dve.tensor_reduce(nmax[:, j, a:e], sc[:, i, 0:(e - a) * KEYS].rearrange("p (h k) -> p h k", k=KEYS),
                                  axis=AX.X, op=ALU.max, negate=True).then_inc(maxed, 1)

        def invert(b, j):
            dve.wait_ge(exped, (2 * b + j + 1) * NSB)
            dve.reciprocal(rinv[:, j, :], rsum[:, j, :]).then_inc(inverted, 1)

        def front_v(b, par):
            for i in range(G_V):
                dve.wait_ge(g_full, gfront(b, i) + 1)
                dve.tensor_copy(v[:, par, i * 512:(i + 1) * 512], g[gbank(i)][0:KEYS, :]).then_inc(g_free, 1)

        def front_q(b, par):
            for i in range(G_Q):
                bank = g[gbank(G_V + i)]
                dve.wait_ge(g_full, gfront(b, G_V + i) + 1)
                for o in range(2):
                    rows = slice(o * DH, (o + 1) * DH)
                    ins = dve.tensor_scalar(q[rows, par, o, 2 * i:2 * i + 2, :], bank[rows, :].rearrange("p (m s) -> p m s", m=2),
                                            DH ** -0.5, None, ALU.mult)
                ins.then_inc(g_free, 1)

        def outputs(b):
            for i in range(G_O):
                dve.wait_ge(g_full, gback(b, i) + 1)
                dve.tensor_copy(oT[:, 2 * i:2 * i + 2, :], g[gbank(i)][:, :].rearrange("p (m s) -> p m s", m=2)).then_inc(g_free, 1)

        def residual(b, par, j):
            dve.wait_ge(g_full, gback(b, G_O + j) + 1)
            dve.tensor_tensor(out=xs[:, bass.ds(b * JT + j, 1), :], in0=x1[:, par, j:j + 1, :],
                              in1=g[gbank(G_O + j)][:, 0:D].rearrange("p (a d) -> p a d", a=1), op=ALU.add).then_inc(g_free, 1)

        def statistics(b):
            tiles = bass.ds(b * JT, JT)
            dve.wait_ge(g_free, gback(b, G_BACK - 1) + 1)
            dve.tensor_tensor(out=xs[:, tiles, :], in0=xs[:, tiles, :],
                              in1=bo[:, :].rearrange("p (a n) -> p a n", a=1).to_broadcast([P, JT, D]),
                              op=ALU.add).then_inc(z_steps, 1)
            dve.wait_ge(z_steps, 3 * b + 1)
            dve.sem_inc(z_seen, 1)
            for j in range(JT):
                ins = dve.bn_stats(bst[:, j, :], xs[:, bass.ds(b * JT + j, 1), :])
            ins.then_inc(z_steps, 1)
            dve.wait_ge(z_steps, 3 * b + 2)
            if not (isinstance(b, int) and b == 0):
                dve.wait_ge(mv_kept, b)
            dve.sem_inc(z_seen, 1)
            for j in range(JT):
                ins = dve.bn_aggr(mvt[:, j, :], bst[:, j, :])
            ins.then_inc(z_steps, 1)
            dve.wait_ge(z_steps, 3 * b + 3)
            dve.tensor_copy(mv0[:, tiles, :], mvt[:, :, :]).then_inc(mv_kept, 1)

        def batch(b, par, before, after):
            maxima(b, 0)
            if before:
                outputs(b - 1)
            invert(b, 0)
            maxima(b, 1)
            if before:
                residual(b - 1, 1 - par, 0)
            invert(b, 1)
            if before:
                residual(b - 1, 1 - par, 1)
                statistics(b - 1)
            if after:
                front_v(b + 1, 1 - par)
                front_q(b + 1, 1 - par)

        dve.wait_ge(loaded[3], 48)
        front_v(0, 0)
        front_q(0, 0)
        batches(dve, batch)
        outputs(B - 1)
        for j in range(JT):
            residual(B - 1, 1, j)
        statistics(B - 1)

    @block.scalar
    def _(act):
        def exps(b, j):
            if not (isinstance(b, int) and b == 0):
                act.wait_ge(pn_ready, 2 * (b - 1) + j + 1)
            for i, (a, e) in enumerate(SBANKS):
                act.wait_ge(maxed, (2 * b + j) * NSB + i + 1)
                for hd in range(a, e):
                    ins = act.activation(pr[:, j, hd, :], sc[:, i, (hd - a) * KEYS:(hd - a + 1) * KEYS], ACT.Exp,
                                         bias=nmax[:, j, hd:hd + 1], accum_out=rsum[:, j, hd:hd + 1])
                ins.then_inc(exped, 1)

        def probabilities(b, par):
            for k in range(JT * NTB):
                j, kk = divmod(k, NTB)
                act.wait_ge(t_full, tpunit(b, k) + 1)
                act.activation(pT[:, kk * TH:(kk + 1) * TH, j * P:(j + 1) * P],
                               tb[tp_bank(b, par, k)][0:KEYS, :].rearrange("p (h s) -> p h s", h=TH), ACT.Copy).then_inc(t_free, 1)

        def norm_x(b, par):
            if not (isinstance(b, int) and b < 2):
                act.wait_ge(z_steps, 3 * (b - 2) + 1)
            for j in range(JT):
                tile = bass.ds(b * JT + j, 1)
                ins = act.activation(x1[:, par, j, :], xs[:, tile, :], ACT.Identity, scale=rstd[:, tile], bias=nbias[:, tile])
            ins.then_inc(x1_ready, 1)

        def front_x(b, par):
            act.wait_ge(t_full, txunit(b) + 1)
            act.activation(xT[:, :, :], tb[tx_bank(b, par)][:, :].rearrange("p (k s) -> p k s", k=DK), ACT.Copy).then_inc(t_free, 1)

        def batch(b, par, before, after):
            exps(b, 0)
            exps(b, 1)
            if after:
                norm_x(b + 1, 1 - par)
                front_x(b + 1, 1 - par)
            probabilities(b, par)

        norm_x(0, 0)
        front_x(0, 0)
        batches(act, batch)

    @block.tensor
    def _(pe):
        def free_bank(unit):
            if not isinstance(unit, int) or unit >= GB:
                pe.wait_ge(g_free, unit - GB + 1)

        def free_tbank(unit):
            if not isinstance(unit, int) or unit >= 2:
                pe.wait_ge(t_free, unit - 1)

        def scores(b, j, par):
            keys = bass.ds(b * KEYS, KEYS)
            for i, (a, e) in enumerate(SBANKS):
                if j == 0:
                    pe.wait_ge(g_free, gfront(b, G_V + (e - 1) // 4) + 1)
                if not (isinstance(b, int) and b == 0 and j == 0):
                    pe.wait_ge(exped, (2 * b + j - 1) * NSB + i + 1)
                mask = mrow[:, keys].rearrange("p (a k) -> p a k", a=1).to_broadcast([P, e - a, KEYS])
                pe.matmul(sc[:, i, 0:(e - a) * KEYS].rearrange("p (h k) -> p h k", k=KEYS), first[:, :], mask, start=True, stop=False)
                for hd in range(a, e):
                    ins = pe.matmul(sc[:, i, (hd - a) * KEYS:(hd - a + 1) * KEYS], q[:, par, hd % 2, hd // 2, j * P:(j + 1) * P],
                                    kT[:, hd // 2, keys], start=False, stop=(hd == e - 1))
                ins.then_inc(s_full, 1)

        def transposes(b, par, k):
            j, kk = divmod(k, NTB)
            if kk == 0:
                pe.wait_ge(pn_ready, 2 * b + j + 1)
            free_tbank(tpunit(b, k))
            for hd in range(TH):
                ins = pe.transpose(tb[tp_bank(b, par, k)][0:KEYS, hd * P:(hd + 1) * P], pn[:, j, kk * TH + hd, :], ident[:, :])
            ins.then_inc(t_full, 1)

        def front_v(b, par):
            pe.wait_ge(cx_ready, b + 1)
            for i in range(G_V):
                free_bank(gfront(b, i))
                for k in range(DK):
                    ins = pe.matmul(g[gbank(i)][0:KEYS, :], cxb[:, par, k, :],
                                    wv[:, k, i * 512:(i + 1) * 512], start=(k == 0), stop=(k == DK - 1))
                ins.then_inc(g_full, 1)

        def front_x(b, par):
            pe.wait_ge(x1_ready, b + 1)
            free_tbank(txunit(b))
            for k in range(DK):
                for j in range(JT):
                    ins = pe.transpose(tb[tx_bank(b, par)][:, k * S + j * P:k * S + (j + 1) * P],
                                       x1[:, par, j, k * P:(k + 1) * P], ident[:, :])
            ins.then_inc(t_full, 1)

        def front_q(b, i):
            free_bank(gfront(b, G_V + i))
            if i == 0:
                pe.wait_ge(t_free, txunit(b) + 1)
            for a in range(2):
                m = 2 * i + a
                for k in range(DK):
                    ins = pe.matmul(g[gbank(G_V + i)][:, a * S:(a + 1) * S], wq[:, k, m * P:(m + 1) * P],
                                    xT[:, k, :], start=(k == 0), stop=(k == DK - 1))
            ins.then_inc(g_full, 1)

        def outputs(b, par):
            pe.wait_ge(t_free, tpunit(b, JT * NTB - 1) + 1)
            for i in range(G_O):
                free_bank(gback(b, i))
                for hd in range(4 * i, 4 * i + 4):
                    m, o = hd // 2 - 2 * i, hd % 2
                    ins = pe.matmul(g[gbank(i)][o * DH:(o + 1) * DH, m * S:(m + 1) * S],
                                    v[:, par, hd * DH:(hd + 1) * DH], pT[:, hd, :], start=True, stop=True)
                ins.then_inc(g_full, 1)

        def project_out(b):
            pe.wait_ge(g_free, gback(b, G_O - 1) + 1)
            for j in range(JT):
                free_bank(gback(b, G_O + j))
                for m in range(MT):
                    ins = pe.matmul(g[gbank(G_O + j)][:, 0:D], oT[:, m, j * P:(j + 1) * P],
                                    wo[:, m, :], start=(m == 0), stop=(m == MT - 1))
                ins.then_inc(g_full, 1)

        def batch(b, par, before, after):
            scores(b, 0, par)
            if before:
                outputs(b - 1, 1 - par)
            scores(b, 1, par)
            if before:
                project_out(b - 1)
            if after:
                front_v(b + 1, 1 - par)
                front_x(b + 1, 1 - par)
            for i in range(G_Q):
                transposes(b, par, 2 * i)
                if i < G_Q - 1:
                    transposes(b, par, 2 * i + 1)
                if after:
                    front_q(b + 1, i)
            transposes(b, par, 2 * G_Q - 1)

        assert JT * NTB == 2 * G_Q
        pe.wait_ge(loaded[3], 48)
        front_v(0, 0)
        front_x(0, 0)
        for i in range(G_Q):
            front_q(0, i)
        batches(pe, batch)
        outputs(B - 1, 1)
        project_out(B - 1)

fp16 = mybir.dt.float16
i32 = mybir.dt.int32

E, TOPK, H = 8, 2, 1024
HM = H // P
TS_LOG = 8
TS = 1 << TS_LOG
SJ = TS // P
NTILES = (TOPK * B * S + E * (TS - 1)) // TS
NSLOT = NTILES * TS
WSCALE = 16.0
RG = 4
HU = 2

def router(nc, ctx, t):
    def sb(name, shape, dt=fp32):
        return ctx.enter_context(nc.sbuf_tensor(name, shape, dt))

    def sem(name):
        return ctx.enter_context(nc.semaphore(name))

    xs, ident, mv0, rstd, nbias, tmpv = (t[k] for k in ("xs", "ident", "mv0", "rstd", "nbias", "tmpv"))
    w1h, w1l, w2h, w2l, b1s, b2s = (t[k] for k in ("w1h", "w1l", "w2h", "w2l", "b1s", "b2s"))
    slots, gates, expert_of = t["slots"], t["gates"], t["expert_of"]
    stage = sb("stage", [P, 2, 2 * H])
    b2f, b2r = (stage[0:1, i, :].rearrange("p (e d) -> p e d", e=E) for i in range(2))
    wr = sb("wr", [P, DK, E])
    x2 = sb("x2", [P, 2, RG, D])
    x2T = sb("x2T", [P, DK, RG * P])
    lg = sb("lg", [P, NT, E])
    rev = sb("rev", [P, NT, E])
    tid = sb("tid", [1, NTILES, E])
    ones = sb("ones", [P, NT])
    lower = sb("lower", [P, P], bf16)
    allone = sb("allone", [P, P], bf16)
    hit = sb("hit", [P, TOPK, NT, E])
    w = [sb(f"w{i}", [P, NT, E]) for i in range(3)]
    chosen = sb("chosen", [P, NT, E], bf16)
    best = sb("best", [P, TOPK, NT])
    at = sb("at", [P, NT])
    small = sb("small", [P, 4, E])
    cnt = sb("cnt", [P, E], i32)
    over = sb("over", [1, NTILES, E])
    fexp = sb("fexp", [1, NTILES])
    tp = [ctx.enter_context(nc.psum_tensor(f"tp{i}", [P, RG * P], fp32)) for i in range(2)]
    lp = [ctx.enter_context(nc.psum_tensor(f"lp{i}", [P, RG, E], fp32)) for i in range(2)]
    ranks = ctx.enter_context(nc.psum_tensor("ranks", [P, NT, E], fp32))
    totals = ctx.enter_context(nc.psum_tensor("totals", [P, NT, E], fp32))

    loaded = sem("r_loaded")
    wstage = [sem(f"r_wstage{i}") for i in range(2)]
    whi = sem("r_whi")
    wlo = sem("r_wlo")
    stats = sem("r_stats")
    rooted = sem("r_rooted")
    const = sem("r_const")
    x2_ready = sem("r_x2")
    xs_ready = sem("r_xs")
    t_full, t_free = sem("r_t_full"), sem("r_t_free")
    l_full, l_free = sem("r_l_full"), sem("r_l_free")
    steps = sem("r_steps")
    ranked = sem("r_ranked")
    chosen_ready = sem("r_chosen")
    gap = sem("r_gap")
    egap = sem("r_egap")
    placed = sem("r_placed")
    b2_zero = sem("r_b2_zero")
    b2_steps = sem("r_b2")
    sent = sem("r_sent")

    NG = NT // RG
    wviews = []
    for e in range(E):
        wviews.append((t["W1"][e].rearrange("(k p) n -> p k n", p=P), w1h[:, e, :, :], w1l[:, e, :, :], DK))
        wviews.append((t["W2"][e].rearrange("(m p) n -> p m n", p=P), w2h[:, e, :, :], w2l[:, e, :, :], HM))

    block = ctx.enter_context(nc.Block())

    @block.sync
    def _(sp):
        with nc.allow_non_contiguous_dma(reason="biases"):
            sp.dma_start(wr[:, :, :], t["Wr"].rearrange("(k p) n -> p k n", p=P)).then_inc(loaded, 16)
            sp.dma_start(b1s[:, :, :], t["b1"].rearrange("e (m p) -> p e m", p=P)).then_inc(loaded, 16)
            sp.dma_start(b2f, t["b2"].rearrange("(a e) n -> a e n", a=1)).then_inc(loaded, 16)
        sp.wait_ge(b2_steps, 3)
        for i, (src, _, _, k) in enumerate(wviews):
            if i >= 2:
                sp.wait_ge(wlo, i - 1)
                sp.wait_ge(whi, i - 1)
            sp.dma_start(stage[:, i % 2, :].rearrange("p (k n) -> p k n", k=k), src).then_inc(wstage[i % 2], 16)

    @block.gpsimd
    def _(pool):
        pool.memset(b2s[:, :, :], 0.0).then_inc(b2_zero, 1)
        pool.iota(rev[:, :, :], pattern=[[0, NT], [-1, E]], base=E, channel_multiplier=0,
                  allow_small_or_imprecise_dtypes=True).then_inc(const, 1)
        pool.iota(tid[:, :, :], pattern=[[1, NTILES], [0, E]], base=0, channel_multiplier=0,
                  allow_small_or_imprecise_dtypes=True).then_inc(const, 1)
        pool.memset(ones[:, :], 1.0).then_inc(const, 1)
        pool.memset(lower[:, :], 0.0).then_inc(const, 1)
        pool.memset(allone[:, :], 1.0).then_inc(const, 1)
        pool.wait_ge(const, 5)
        pool.affine_select(out=lower[:, :], in_=lower[:, :], compare_op=ALU.is_ge, fill=1.0,
                           base=0, pattern=[[-1, P]], channel_multiplier=1).then_inc(const, 1)

        def copy_back(g, par):
            pool.wait_ge(x2_ready, g + 1)
            pool.tensor_copy(xs[:, bass.ds(g * RG, RG), :], x2[:, par, :, :]).then_inc(xs_ready, 1)

        with pool.Fori(0, NG // 2) as it:
            copy_back(it * 2, 0)
            copy_back(it * 2 + 1, 1)
        pool.wait_ge(placed, 1)
        pool.wait_ge(xs_ready, NG)
        for k in range(TOPK):
            for j in range(NT):
                pool.indirect_dma_start(t["xsort"], bass.IndirectOffsetOnAxis(ap=slots[:, k, j:j + 1], axis=0),
                                        xs[:, j, :], None).then_inc(sent, 16)
        pool.wait_ge(sent, 16 * TOPK * NT)

    @block.scalar
    def _(act):
        rstd_scalar(act, tmpv, stats, rooted, 0)
        act.wait_ge(stats, RSTD_STEPS)

        def normalise(g, par):
            if not (isinstance(g, int) and g < 2):
                act.wait_ge(xs_ready, g - 1)
                act.wait_ge(t_full, 2 * (g - 1))
            for j in range(RG):
                tile = bass.ds(g * RG + j, 1)
                ins = act.activation(x2[:, par, j, :], xs[:, tile, :], ACT.Identity, scale=rstd[:, tile], bias=nbias[:, tile])
            ins.then_inc(x2_ready, 1)

        normalise(0, 0)
        normalise(1, 1)
        with act.Fori(1, NG // 2) as it:
            normalise(it * 2, 0)
            normalise(it * 2 + 1, 1)
        act.wait_ge(gap, 1)
        act.activation(at[:, :], best[:, 0, :], ACT.Exp).then_inc(egap, 1)
        for i, (src, hi, lo, k) in enumerate(wviews):
            act.wait_ge(wstage[i % 2], 16 * (i // 2 + 1))
            act.activation(hi, stage[:, i % 2, :].rearrange("p (k n) -> p k n", k=k), ACT.Copy, scale=WSCALE).then_inc(whi, 1)

    @block.tensor
    def _(pe):
        pe.wait_ge(loaded, 48)

        def group(g, par):
            pe.wait_ge(x2_ready, g + 1)
            for k in range(DK):
                if not (isinstance(g, int) and g == 0):
                    pe.wait_ge(t_free, 2 * g + k - 1)
                for j in range(RG):
                    ins = pe.transpose(tp[k][:, j * P:(j + 1) * P], x2[:, par, j, k * P:(k + 1) * P], ident[:, :])
                ins.then_inc(t_full, 1)
            pe.wait_ge(t_free, 2 * g + 2)
            if not (isinstance(g, int) and g < 2):
                pe.wait_ge(l_free, g - 1)
            for j in range(RG):
                for k in range(DK):
                    ins = pe.matmul(lp[par][:, j, :], x2T[:, k, j * P:(j + 1) * P], wr[:, k, :],
                                    start=(k == 0), stop=(k == DK - 1))
            ins.then_inc(l_full, 1)

        group(0, 0)
        group(1, 1)
        with pe.Fori(1, NG // 2) as it:
            group(it * 2, 0)
            group(it * 2 + 1, 1)
        pe.wait_ge(const, 6)
        pe.wait_ge(chosen_ready, 1)
        pe.matmul(ranks[:, :, :], lower[:, :], chosen[:, :, :], start=True, stop=True)
        pe.matmul(totals[:, :, :], allone[:, :], chosen[:, :, :], start=True, stop=True).then_inc(ranked, 1)

    @block.vector
    def _(dve):
        dve.wait_ge(loaded, 48)
        dve.wait_ge(b2_zero, 1)
        dve.tensor_scalar(b2s[0:1, :, :], b2f, WSCALE, None, ALU.mult).then_inc(b2_steps, 1)
        dve.wait_ge(b2_steps, 1)
        dve.scalar_tensor_tensor(out=b2r, in0=b2f, scalar=WSCALE, in1=b2s[0:1, :, :],
                                 op0=ALU.mult, op1=ALU.subtract).then_inc(b2_steps, 1)
        dve.wait_ge(b2_steps, 2)
        dve.tensor_copy(b2s[32:33, :, :], b2r).then_inc(b2_steps, 1)
        rstd_vector(dve, mv0, rstd, nbias, tmpv, stats, rooted, 0)

        def group(g, par):
            for k in range(DK):
                dve.wait_ge(t_full, 2 * g + k + 1)
                dve.tensor_copy(x2T[:, k, :], tp[k][:, :]).then_inc(t_free, 1)
            dve.wait_ge(l_full, g + 1)
            dve.tensor_copy(lg[:, bass.ds(g * RG, RG), :], lp[par][:, :, :]).then_inc(l_free, 1)

        with dve.Fori(0, NG // 2) as it:
            group(it * 2, 0)
            group(it * 2 + 1, 1)
        dve.wait_ge(const, 6)
        dve.wait_ge(l_free, NG)
        n = 0

        def link(ins):
            nonlocal n
            n += 1
            ins.then_inc(steps, 1)
            dve.wait_ge(steps, n)

        def over_experts(v):
            return v.rearrange("p (j a) -> p j a", a=1).to_broadcast([P, NT, E])

        logits = lg
        for k in range(TOPK):
            link(dve.tensor_reduce(best[:, k, :], logits[:, :, :], axis=AX.X, op=ALU.max))
            link(dve.tensor_tensor(out=w[1][:, :, :], in0=logits[:, :, :], in1=over_experts(best[:, k, :]), op=ALU.is_equal))
            link(dve.tensor_tensor(out=w[1][:, :, :], in0=w[1][:, :, :], in1=rev[:, :, :], op=ALU.mult))
            link(dve.tensor_reduce(at[:, :], w[1][:, :, :], axis=AX.X, op=ALU.max))
            link(dve.tensor_tensor(out=hit[:, k, :, :], in0=rev[:, :, :], in1=over_experts(at[:, :]), op=ALU.is_equal))
            if k == 0:
                link(dve.scalar_tensor_tensor(out=w[0][:, :, :], in0=hit[:, 0, :, :], scalar=-3e38, in1=lg[:, :, :],
                                              op0=ALU.mult, op1=ALU.add))
                logits = w[0]
        dve.tensor_tensor(out=chosen[:, :, :], in0=hit[:, 0, :, :], in1=hit[:, 1, :, :], op=ALU.add).then_inc(chosen_ready, 1)
        link(dve.tensor_tensor(out=best[:, 0, :], in0=best[:, 1, :], in1=best[:, 0, :], op=ALU.subtract))
        dve.sem_inc(gap, 1)
        dve.wait_ge(egap, 1)
        link(dve.tensor_scalar(best[:, 1, :], at[:, :], 1.0, None, ALU.add))
        link(dve.reciprocal(gates[:, 0, :], best[:, 1, :]))
        link(dve.tensor_tensor(out=gates[:, 1, :], in0=gates[:, 0, :], in1=at[:, :], op=ALU.mult))
        dve.wait_ge(ranked, 1)
        upto = w[0][:, :, :].rearrange("p j e -> p (j e)").rearrange("p (e j) -> p e j", e=E)
        for e in range(E):
            ins = dve.tensor_tensor_scan(out=upto[:, e, :], data0=ones[:, :], data1=totals[:, :, e], initial=0.0,
                                         op0=ALU.mult, op1=ALU.add)
        link(ins)
        count, tiles, ends, base = (small[:, i, :] for i in range(4))
        link(dve.tensor_scalar(cnt[:, :], upto[:, :, NT - 1], float(TS - 1), None, ALU.add))
        link(dve.tensor_scalar(cnt[:, :], cnt[:, :], TS_LOG, None, ALU.logical_shift_right))
        link(dve.tensor_copy(tiles, cnt[:, :]))
        link(dve.tensor_tensor_scan(out=ends, data0=ones[:, 0:E], data1=tiles, initial=0.0, op0=ALU.mult, op1=ALU.add))
        link(dve.tensor_tensor(out=base, in0=ends, in1=tiles, op=ALU.subtract))
        link(dve.tensor_scalar(base, base, float(TS), None, ALU.mult))
        link(dve.tensor_tensor(out=w[1][:, :, :], in0=upto.rearrange("p e j -> p j e"), in1=totals[:, :, :], op=ALU.subtract))
        link(dve.tensor_tensor(out=w[2][:, :, :], in0=w[1][:, :, :], in1=ranks[:, :, :], op=ALU.add))
        link(dve.tensor_tensor(out=w[1][:, :, :], in0=w[2][:, :, :],
                               in1=base.rearrange("p (a e) -> p a e", a=1).to_broadcast([P, NT, E]), op=ALU.add))
        for k in range(TOPK):
            link(dve.tensor_tensor(out=w[2][:, :, :], in0=w[1][:, :, :], in1=hit[:, k, :, :], op=ALU.mult))
            link(dve.tensor_reduce(best[:, k, :], w[2][:, :, :], axis=AX.X, op=ALU.add))
            link(dve.tensor_copy(slots[:, k, :], best[:, k, :]))
        dve.sem_inc(placed, 1)
        link(dve.tensor_tensor(out=over[:, :, :], in0=tid[:, :, :],
                               in1=ends[0:1, :].rearrange("p (a e) -> p a e", a=1).to_broadcast([1, NTILES, E]), op=ALU.is_ge))
        link(dve.tensor_reduce(fexp[:, :], over[:, :, :], axis=AX.X, op=ALU.add))
        link(dve.tensor_scalar(expert_of[:, :], fexp[:, :], float(E - 1), None, ALU.min))
        for i, (src, hi, lo, k) in enumerate(wviews):
            dve.wait_ge(whi, i + 1)
            dve.scalar_tensor_tensor(out=lo, in0=stage[:, i % 2, :].rearrange("p (k n) -> p k n", k=k), scalar=WSCALE,
                                     in1=hi, op0=ALU.mult, op1=ALU.subtract).then_inc(wlo, 1)
        dve.wait_ge(wlo, len(wviews))

def experts(nc, ctx, t):
    def sb(name, shape, dt=fp32):
        return ctx.enter_context(nc.sbuf_tensor(name, shape, dt))

    def sem(name):
        return ctx.enter_context(nc.semaphore(name))

    ident, w1h, w1l, w2h, w2l, b1s, b2s, expert_of = (t[k] for k in ("ident", "w1h", "w1l", "w2h", "w2l", "b1s", "b2s", "expert_of"))
    NHU = HM // HU
    STORE_LAG = 4
    xt = sb("xt", [P, 2, SJ, D])
    xh = sb("xh", [P, 2, DK, TS], fp16)
    xl = sb("xl", [P, 2, DK, TS], fp16)
    act32 = sb("act32", [P, 2, HU, TS])
    hh = sb("hh", [P, 2, HM, TS], fp16)
    hl = sb("hl", [P, 2, HM, TS], fp16)
    ys = sb("ys", [P, 2, SJ, D])
    brow = sb("brow", [P, P], fp16)
    hp = [ctx.enter_context(nc.psum_tensor(f"hp{i}", [P, HU * TS], fp32)) for i in range(4)]
    xp = ctx.enter_context(nc.psum_tensor("xp", [P, DK * TS], fp32))
    yp = [ctx.enter_context(nc.psum_tensor(f"yp{i}", [P, SJ * D], fp32)) for i in range(2)]

    x_in = [sem(f"e_x_in{i}") for i in range(2)]
    const = sem("e_const")
    xp_full = sem("e_xp_full")
    xh_ready, xl_ready = sem("e_xh"), sem("e_xl")
    h_full = sem("e_h_full")
    g_ready = sem("e_g")
    hh_ready = sem("e_hh")
    hl_ready = sem("e_hl")
    y_full = sem("e_y_full")
    y_ready = sem("e_y")
    y_out = [sem(f"e_y_out{i}") for i in range(2)]

    xv = t["xsort"].rearrange("(t j p) d -> p t j d", j=SJ, p=P)
    yv = t["ysort"].rearrange("(t j p) d -> p t j d", j=SJ, p=P)
    block = ctx.enter_context(nc.Block())

    def tiles(eng, body, apart=2):
        for t in range(apart):
            body(t, t % 2, t // 2)
        with eng.Fori(apart // 2, NTILES // 2) as it:
            body(it * 2, 0, it)
            body(it * 2 + 1, 1, it)
        if NTILES % 2:
            body(NTILES - 1, 0, NTILES // 2)

    def late(t, n=1):
        return not isinstance(t, int) or t >= n

    @block.sync
    def _(sp):
        def store(t, par):
            sp.wait_ge(y_ready, t + 1)
            sp.dma_start(yv[:, bass.ds(t, 1), :, :], ys[:, par, :, :]).then_inc(y_out[par], 16)

        def tile(t, par, uses):
            if late(t, 2):
                sp.wait_ge(xp_full, t - 1)
            sp.dma_start(xt[:, par, :, :], xv[:, bass.ds(t, 1), :, :]).then_inc(x_in[par], 16)
            if late(t, STORE_LAG):
                store(t - STORE_LAG, par)

        tiles(sp, tile, STORE_LAG)
        for t in range(NTILES - STORE_LAG, NTILES):
            store(t, t % 2)
        for par in range(2):
            sp.wait_ge(y_out[par], 16 * ((NTILES + 1 - par) // 2))

    @block.gpsimd
    def _(pool):
        pool.memset(brow[:, :], 0.0).then_inc(const, 1)
        pool.wait_ge(const, 1)
        pool.memset(brow[0:1, :], 1.0).then_inc(const, 1)
        pool.memset(brow[32:33, :], 1.0).then_inc(const, 1)

    @block.scalar
    def _(act):
        def take_x(t, par):
            act.wait_ge(xp_full, t + 1)
            if late(t, 2):
                act.wait_ge(h_full, (t - 1) * NHU)
            act.activation(xh[:, par, :, :], xp[:, :].rearrange("p (k s) -> p k s", k=DK), ACT.Copy).then_inc(xh_ready, 1)

        def hidden(t, par):
            e = act.value_load(expert_of[0:1, bass.ds(t, 1)] , min_val=0, max_val=E - 1)
            for i in range(NHU):
                act.wait_ge(h_full, t * NHU + i + 1)
                if late(t * NHU + i, 2) if isinstance(t, int) else True:
                    act.wait_ge(hl_ready, t * NHU + i - 1)
                if late(t, 2):
                    act.wait_ge(y_full, t - 1)
                for a in range(HU):
                    m = i * HU + a
                    bias = b1s[:, bass.ds(e, 1), m]
                    pre = hp[i % 4][:, a * TS:(a + 1) * TS]
                    ins = act.activation(act32[:, i % 2, a, :], pre, ACT.Gelu, bias=bias, scale=1 / WSCALE)
                ins.then_inc(g_ready, 1)
                for a in range(HU):
                    m = i * HU + a
                    bias = b1s[:, bass.ds(e, 1), m]
                    pre = hp[i % 4][:, a * TS:(a + 1) * TS]
                    ins = act.activation(hh[:, par, m, :], pre, ACT.Gelu, bias=bias, scale=1 / WSCALE)
                ins.then_inc(hh_ready, 1)

        def tile(t, par, uses):
            hidden(t, par)
            if not (isinstance(t, int) and t == NTILES - 1):
                take_x(t + 1, 1 - par)

        take_x(0, 0)
        tiles(act, tile)

    @block.vector
    def _(dve):
        def take_x(t, par):
            dve.wait_ge(xh_ready, t + 1)
            if late(t, 2):
                dve.wait_ge(h_full, (t - 1) * NHU)
            dve.tensor_tensor(out=xl[:, par, :, :], in0=xp[:, :].rearrange("p (k s) -> p k s", k=DK),
                              in1=xh[:, par, :, :], op=ALU.subtract).then_inc(xl_ready, 1)

        def hidden(t, par):
            for i in range(NHU):
                dve.wait_ge(hh_ready, t * NHU + i + 1)
                if late(t, 2):
                    dve.wait_ge(y_full, t - 1)
                dve.tensor_tensor(out=hl[:, par, i * HU:(i + 1) * HU, :], in0=act32[:, i % 2, :, :],
                                  in1=hh[:, par, i * HU:(i + 1) * HU, :], op=ALU.subtract).then_inc(hl_ready, 1)

        def output(t, par, uses):
            dve.wait_ge(y_full, t + 1)
            if late(t, 2):
                dve.wait_ge(y_out[par], uses * 16)
            dve.tensor_scalar(ys[:, par, :, :], yp[par][:, :].rearrange("p (j d) -> p j d", j=SJ), 1 / WSCALE, None,
                              ALU.mult).then_inc(y_ready, 1)

        def tile(t, par, uses):
            hidden(t, par)
            if not (isinstance(t, int) and t == NTILES - 1):
                take_x(t + 1, 1 - par)
            if late(t):
                output(t - 1, 1 - par, uses - 1 + par)

        take_x(0, 0)
        tiles(dve, tile)
        output(NTILES - 1, (NTILES - 1) % 2, (NTILES - 1) // 2)

    @block.tensor
    def _(pe):
        def transpose(t, par, uses):
            pe.wait_ge(x_in[par], uses * 16 + 16)
            if late(t):
                pe.wait_ge(xl_ready, t)
            for k in range(DK):
                for j in range(SJ):
                    ins = pe.transpose(xp[:, k * TS + j * P:k * TS + (j + 1) * P], xt[:, par, j, k * P:(k + 1) * P], ident[:, :])
            ins.then_inc(xp_full, 1)

        def hidden(t, par):
            e = pe.value_load(expert_of[0:1, bass.ds(t, 1)], min_val=0, max_val=E - 1)
            pe.wait_ge(xl_ready, t + 1)
            for i in range(NHU):
                if late(t * NHU + i, 4) if isinstance(t, int) else True:
                    pe.wait_ge(hh_ready, t * NHU + i - 3)
                for a in range(HU):
                    m = i * HU + a
                    n = 0
                    for k in range(DK):
                        for wt, xx in ((w1h, xh), (w1h, xl), (w1l, xh)):
                            ins = pe.matmul(hp[i % 4][:, a * TS:(a + 1) * TS],
                                            wt[:, bass.ds(e, 1), k, m * P:(m + 1) * P], xx[:, par, k, :],
                                            start=(n == 0), stop=(n == 3 * DK - 1))
                            n += 1
                ins.then_inc(h_full, 1)

        def output(t, par):
            e = pe.value_load(expert_of[0:1, bass.ds(t, 1)], min_val=0, max_val=E - 1)
            pe.wait_ge(hl_ready, (t + 1) * NHU)
            if late(t, 2):
                pe.wait_ge(y_ready, t - 1)
            for j in range(SJ):
                out = yp[par][:, j * D:(j + 1) * D]
                pe.matmul(out, brow[:, :], b2s[:, bass.ds(e, 1), :], start=True, stop=False)
                for m in range(HM):
                    for hx, wt in ((hh, w2h), (hh, w2l), (hl, w2h)):
                        ins = pe.matmul(out, hx[:, par, m, j * P:(j + 1) * P], wt[:, bass.ds(e, 1), m, :], start=False,
                                        stop=(m == HM - 1 and hx is hl))
            ins.then_inc(y_full, 1)

        def tile(t, par, uses):
            hidden(t, par)
            if not (isinstance(t, int) and t == NTILES - 1):
                transpose(t + 1, 1 - par, uses + par)
            if late(t):
                output(t - 1, 1 - par)

        pe.wait_ge(const, 3)
        transpose(0, 0, 0)
        tiles(pe, tile)
        output(NTILES - 1, (NTILES - 1) % 2)

CG = 8

def combine(nc, ctx, t):
    def sb(name, shape, dt=fp32):
        return ctx.enter_context(nc.sbuf_tensor(name, shape, dt))

    def sem(name):
        return ctx.enter_context(nc.semaphore(name))

    xs, mv, rstd, nbias, tmpv, slots, gates = (t[k] for k in ("xs", "mv0", "rstd", "nbias", "tmpv", "slots", "gates"))
    NG = NT // CG
    yk = sb("yk", [P, NT, TOPK, D])
    res = sb("res", [P, NT, D])
    bst = sb("bst3", [P, NT, 6])
    got = [sem(f"c_got{i}") for i in range(NG)]
    steps = sem("c_steps")
    rooted = sem("c_rooted")
    done = sem("c_done")
    out_sent = sem("c_out_sent")
    PER = 4 + RSTD_STEPS
    block = ctx.enter_context(nc.Block())

    @block.gpsimd
    def _(pool):
        for j in range(NT):
            for k in range(TOPK):
                pool.indirect_dma_start(yk[:, j, k, :], None, t["ysort"],
                                        bass.IndirectOffsetOnAxis(ap=slots[:, k, j:j + 1], axis=0)).then_inc(got[j // CG], 16)

    @block.vector
    def _(dve):
        for g in range(NG):
            cols = slice(g * CG, (g + 1) * CG)
            dve.wait_ge(got[g], 16 * CG * TOPK)
            for k in range(TOPK):
                for j in range(g * CG, (g + 1) * CG):
                    ins = dve.scalar_tensor_tensor(out=xs[:, j, :], in0=yk[:, j, k, :], scalar=gates[:, k, j:j + 1],
                                                   in1=xs[:, j, :], op0=ALU.mult, op1=ALU.add)
                ins.then_inc(steps, 1)
                dve.wait_ge(steps, g * PER + k + 1)
            for j in range(g * CG, (g + 1) * CG):
                ins = dve.bn_stats(bst[:, j, :], xs[:, j, :])
            ins.then_inc(steps, 1)
            dve.wait_ge(steps, g * PER + 3)
            for j in range(g * CG, (g + 1) * CG):
                ins = dve.bn_aggr(mv[:, j, :], bst[:, j, :])
            ins.then_inc(steps, 1)
            dve.wait_ge(steps, g * PER + 4)
            rstd_vector(dve, mv, rstd, nbias, tmpv, steps, rooted, g * PER + 4, cols, g + 1)

    @block.scalar
    def _(act):
        for g in range(NG):
            rstd_scalar(act, tmpv, steps, rooted, g * PER + 4, slice(g * CG, (g + 1) * CG))
            act.wait_ge(steps, (g + 1) * PER)
            for j in range(g * CG, (g + 1) * CG):
                ins = act.activation(res[:, j, :], xs[:, j, :], ACT.Identity, scale=rstd[:, j:j + 1], bias=nbias[:, j:j + 1])
            ins.then_inc(done, 1)

    @block.sync
    def _(sp):
        ov = t["out"].rearrange("b (h p) d -> p (b h) d", p=P)
        for g in range(NG):
            sp.wait_ge(done, g + 1)
            sp.dma_start(ov[:, g * CG:(g + 1) * CG, :], res[:, g * CG:(g + 1) * CG, :]).then_inc(out_sent, 16)
        sp.wait_ge(out_sent, 16 * NG)

def decoder_layer(nc, a, out):
    def part(prefix):
        return {k[len(prefix):]: v for k, v in a.items() if k.startswith(prefix)}

    with ExitStack() as ctx:
        def sb(name, shape, dt=fp32):
            return ctx.enter_context(nc.sbuf_tensor(name, shape, dt))

        t = {
            "xs": sb("xs", [P, NT, D]),
            "ident": sb("ident", [P, P]),
            "mv0": sb("mv0", [P, NT, 2]),
            "mv1": sb("mv1", [P, NT, 2]),
            "rstd": sb("rstd", [P, NT]),
            "nbias": sb("nbias", [P, NT]),
            "tmpv": sb("tmpv", [P, 4, NT]),
            "slots": sb("slots", [P, TOPK, NT], i32),
            "gates": sb("gates", [P, TOPK, NT]),
            "expert_of": sb("expert_of", [1, NTILES], i32),
            "xsort": nc.dram_tensor("xsort", [NSLOT, D], fp32, kind="Internal").ap(),
            "ysort": nc.dram_tensor("ysort", [NSLOT, D], fp32, kind="Internal").ap(),
            "out": out,
        }
        with ExitStack() as stage:
            mixer(nc, stage, t | part("L0_attn_") | {"x": a["x"]})
        with ExitStack() as stage:
            attention(nc, stage, t | part("L0_xattn_") | {"ctx": a["ctx_1024"], "mask": a["mask_BxS2_bk0"]})
        with ExitStack() as weights:
            def wsb(name, shape, dt=fp16):
                return weights.enter_context(nc.sbuf_tensor(name, shape, dt))

            tw = t | part("L0_ffn_") | {
                "w1h": wsb("w1h", [P, E, DK, H]), "w1l": wsb("w1l", [P, E, DK, H]),
                "w2h": wsb("w2h", [P, E, HM, D]), "w2l": wsb("w2l", [P, E, HM, D]),
                "b1s": wsb("b1s", [P, E, HM], fp32), "b2s": wsb("b2s", [P, E, D]),
            }
            with ExitStack() as stage:
                router(nc, stage, tw)
            with ExitStack() as stage:
                experts(nc, stage, tw)
        with ExitStack() as stage:
            combine(nc, stage, t)

_INS = ["x", "ctx_1024", "mask_BxS2_bk0"] + [
    "L0_attn_" + n for n in ("ln_w", "ln_b", "W_in", "b_in", "conv_w", "conv_b", "A_log", "D", "W_x", "b_x", "W_out", "b_out")
] + ["L0_xattn_" + n for n in ("Wq", "Wkv", "Wout", "b_out")] + ["L0_ffn_" + n for n in ("Wr", "W1", "b1", "W2", "b2")]

def kernel(**inputs):
    import numpy as _np
    import concourse.bacc as _bacc
    from concourse import mybir as _mybir
    from concourse.bass_utils import run_bass_kernel_spmd as _run

    nc = _bacc.Bacc("TRN2", target_bir_lowering=False, num_devices=1)
    arrays, aps = {}, {}
    for name in _INS:
        a = _np.ascontiguousarray(inputs[name])
        if a.dtype.kind == "b":
            a = a.reshape(-1).view(_np.uint32)
        arrays[f"in_{name}"] = a
        aps[name] = nc.dram_tensor(f"in_{name}", a.shape, _mybir.dt.from_np(a.dtype), kind="ExternalInput").ap()
    out = nc.dram_tensor("out_0", (B, S, D), fp32, kind="ExternalOutput").ap()
    decoder_layer(nc, aps, out)
    r = _run(nc, [arrays], core_ids=[0])
    return _np.asarray(r.results[0]["out_0"])
```

```python
import concourse.bass as bass
from concourse import mybir
from contextlib import ExitStack
import numpy as np

fp32 = mybir.dt.float32
bf16 = mybir.dt.bfloat16
u32 = mybir.dt.uint32
ALU = mybir.AluOpType
ACT = mybir.ActivationFunctionType
AX = mybir.AxisListType

B, S, D = 16, 256, 256
P = 128
NT = B * S // P
DK = D // P
EPS = 1e-5

DI, NS, TAPS = 512, 16, 4
CT = DI // P
NPAIR = B // 2
TP = 2 * S
TT = TP // P
PADW = S + TAPS - 1
NBC = 2 * NS
U_XT, U_WIN, U_CONV, U_WX, U_FRONT = 0, DK, DK + CT, DK + 2 * CT, DK + 2 * CT + 1
U_GATE = CT
U_OUT = 2
U_ALL = U_OUT + U_GATE + U_FRONT
BLEAD, BRING = 4, 8
HRING = 8
ADDED = (0, 3, 6, 9)
ADD_LAG = 4
SUM_LAG, PAIR_LAG = 1, 4
SUM_STEP = []
for _n in range(NS):
    SUM_STEP.append(max(_n + (PAIR_LAG if _n in ADDED else SUM_LAG), SUM_STEP[-1] if _n else 0))
CLEAD, CRING = 2, 4

def front_unit(q, k):
    if isinstance(q, int) and q == 0:
        return k
    return q * U_ALL - (U_ALL - U_FRONT - U_GATE) + k

def gate_unit(p, k):
    return p * U_ALL + U_FRONT + k

def out_unit(p, k):
    last = isinstance(p, int) and p == NPAIR - 1
    return (p + 1) * U_ALL + (0 if last else U_FRONT) - U_OUT + k

def mixer(nc, ctx, t):
    def sb(name, shape, dt=fp32):
        return ctx.enter_context(nc.sbuf_tensor(name, shape, dt))

    def sem(name):
        return ctx.enter_context(nc.semaphore(name))

    xs, ident, mv0, mv1, rstd, nbias, tmpv = t["xs"], t["ident"], t["mv0"], t["mv1"], t["rstd"], t["nbias"], t["tmpv"]
    win = sb("win", [P, DK, 2 * DI])
    wout = sb("wout", [P, CT, D])
    wx3 = sb("wx3", [P, CT, 3 * NBC])
    bx3 = sb("bx3", [3 * NBC, 1])
    bin_ = sb("bin", [P, 2 * CT])
    lnw = sb("lnw", [P, DK])
    lnb = sb("lnb", [P, DK])
    cw = sb("cw", [P, CT, TAPS])
    cb = sb("cb", [P, CT])
    dsk = sb("dsk", [P, CT])
    alog = sb("alog", [P, CT, NS])
    bob = sb("bob", [P, D])
    cdiag = sb("cdiag", [P, CT, TAPS, P])
    ddiag = sb("ddiag", [P, CT, P])
    sel0 = sb("sel0", [3 * NBC, NBC], bf16)
    sel = sb("sel", [3 * NBC, NBC, P], bf16)
    xn = sb("xn", [P, TT, D])
    xnT = sb("xnT", [P, DK, TP])
    xm = sb("xm", [P, CT, 2, PADW])
    gs = sb("gs", [P, CT, TP])
    xc = sb("xc", [P, 2, CT, TP])
    rest = sb("rest", [3 * NBC, TP])
    parts = sb("parts", [3 * NBC, 2, TP], bf16)
    bring = sb("bring", [P, BRING, TP])
    cring = sb("cring", [P, CRING, TP])
    h = sb("h", [P, HRING, CT, TP])
    otmp = sb("otmp", [P, TT, D])
    bst = sb("bst", [P, TT, 6])
    mvt = sb("mvt", [P, TT, 2])

    y = ctx.enter_context(nc.psum_tensor("y", [P, CT, TP], fp32))
    fb = [ctx.enter_context(nc.psum_tensor(f"fb{i}", [P, TP], fp32)) for i in range(2)]
    bbank = ctx.enter_context(nc.psum_tensor("bbank", [P, TP], fp32))
    cbank = ctx.enter_context(nc.psum_tensor("cbank", [P, TP], fp32))

    loaded = sem("m_loaded")
    xloaded = [sem(f"m_xloaded{i}") for i in range(2)]
    made = sem("m_made")
    tables = sem("m_tables")
    adecay = sem("m_adecay")
    stats = sem("m_stats")
    rooted = sem("m_rooted")
    xn_ready = sem("m_xn")
    fb_full = sem("m_fb_full")
    fb_free = sem("m_fb_free")
    split1 = sem("m_split1")
    split2 = sem("m_split2")
    b_sent = sem("m_b_sent")
    b_kept = sem("m_b_kept")
    u_ready = sem("m_u")
    h_ready = sem("m_h")
    c_sent = sem("m_c_sent")
    c_kept = sem("m_c_kept")
    hc_ready = sem("m_hc")
    added = sem("m_added")
    summed = sem("m_summed")
    y_done = sem("m_y_done")
    gated = sem("m_gated")
    z_steps = sem("m_z")

    z_seen = sem("m_z_seen")
    mv_kept = sem("m_mv_kept")

    N_LOADS = 16
    block = ctx.enter_context(nc.Block())

    @block.sync
    def _(sp):
        with nc.allow_non_contiguous_dma(reason="short vectors and tables"):
            xd = t["x"].rearrange("b (h p) d -> p (b h) d", p=P)
            sp.dma_start(xs[:, 0:TT, :], xd[:, 0:TT, :]).then_inc(xloaded[0], 16)
            loads = [
                (win[:, :, :], t["W_in"].rearrange("(k p) n -> p k n", p=P)),
                (wout[:, :, :], t["W_out"].rearrange("(k p) n -> p k n", p=P)),
                (bin_[:, :], t["b_in"].rearrange("(m p) -> p m", p=P)),
                (lnw[:, :], t["ln_w"].rearrange("(k p) -> p k", p=P)),
                (lnb[:, :], t["ln_b"].rearrange("(k p) -> p k", p=P)),
                (cw[:, :, :], t["conv_w"].rearrange("(c p) o k -> p c (o k)", p=P)),
                (cb[:, :], t["conv_b"].rearrange("(c p) -> p c", p=P)),
                (dsk[:, :], t["D"].rearrange("(c p) -> p c", p=P)),
                (alog[:, :, :], t["A_log"].rearrange("(c p) n -> p c n", p=P)),
                (bob[:, :], t["b_out"].rearrange("(a n) -> a n", a=1).to_broadcast([P, D])),
            ]
            for g in range(3):
                loads.append((wx3[:, :, g * NBC:(g + 1) * NBC], t["W_x"].rearrange("(c p) n -> p c n", p=P)))
                loads.append((bx3[g * NBC:(g + 1) * NBC, :], t["b_x"].rearrange("(n a) -> n a", a=1)))
            assert len(loads) == N_LOADS
            for dst, src in loads:
                sp.dma_start(dst, src).then_inc(loaded, 16)
            sp.dma_start(xs[:, TT:NT, :], xd[:, TT:NT, :]).then_inc(xloaded[1], 16)

    @block.gpsimd
    def _(pool):
        pool.memset(ident[:, :], 0.0).then_inc(made, 1)
        pool.memset(sel0[:, :], 0.0).then_inc(made, 1)
        pool.memset(xm[:, :, :, :], 0.0).then_inc(made, 1)
        pool.wait_ge(made, 3)
        pool.affine_select(out=ident[:, :], in_=ident[:, :], compare_op=ALU.not_equal, fill=1.0,
                           base=0, pattern=[[-1, P]], channel_multiplier=1).then_inc(made, 1)
        for g in range(3):
            pool.affine_select(out=sel0[:, :], in_=sel0[:, :], compare_op=ALU.not_equal, fill=1.0,
                               base=-g * NBC, pattern=[[-1, NBC]], channel_multiplier=1).then_inc(made, 1)
            pool.wait_ge(made, 5 + g)

        def add(p, n):
            pool.wait_ge(hc_ready, p * NS + n + 2)
            pool.tensor_tensor(out=h[:, n % HRING, :, :], in0=h[:, n % HRING, :, :], in1=h[:, (n + 1) % HRING, :, :],
                               op=ALU.add).then_inc(added, 1)

        def pair(p, par):
            for n in range(NS):
                i = p * NS + n
                slot = n % BRING
                pool.wait_ge(b_kept, i + 1)
                if not isinstance(i, int) or i >= HRING:
                    pool.wait_ge(summed, i - HRING + 1)
                pool.tensor_tensor(out=h[:, n % HRING, :, :], in0=xc[:, par, :, :],
                                   in1=bring[:, slot:slot + 1, :].to_broadcast([P, CT, TP]),
                                   op=ALU.mult).then_inc(u_ready, 1)
                if n - ADD_LAG in ADDED:
                    add(p, n - ADD_LAG)

        pair(0, 0)
        with pool.Fori(0, NPAIR // 2 - 1) as it:
            pair(it * 2 + 1, 1)
            pair(it * 2 + 2, 0)
        pair(NPAIR - 1, 1)

    @block.vector
    def _(dve):
        dve.sem_inc(z_steps, 4)

        def first_norm(tiles, n):
            at = n
            for i in tiles:
                if i - tiles[0] >= TT:
                    dve.wait_ge(stats, at - 2 * TT + 2)
                dve.bn_stats(bst[:, i % TT, :], xs[:, i, :]).then_inc(stats, 1)
                dve.wait_ge(stats, at + 1)
                dve.bn_aggr(mv0[:, i, :], bst[:, i % TT, :]).then_inc(stats, 1)
                at += 2
            dve.wait_ge(stats, at)
            return rstd_vector(dve, mv0, rstd, nbias, tmpv, stats, rooted, at, slice(tiles[0], tiles[-1] + 1),
                               1 if n == 0 else 2)

        dve.wait_ge(xloaded[0], 16)
        n = first_norm(range(TT), 0)
        dve.wait_ge(loaded, 16 * N_LOADS)
        dve.wait_ge(made, 7)
        for c in range(CT):
            for k in range(TAPS):
                dve.tensor_scalar(cdiag[:, c, k, :], ident[:, :], cw[:, c, k:k + 1], None, ALU.mult)
            dve.tensor_scalar(ddiag[:, c, :], ident[:, :], dsk[:, c:c + 1], None, ALU.mult)
        dve.tensor_copy(sel[:, :, :], sel0[:, :].rearrange("p (n a) -> p n a", a=1).to_broadcast([3 * NBC, NBC, P])).then_inc(tables, 1)

        def split(q, par, step):
            if step == 0:
                dve.wait_ge(split2, q * 4 + 2)
                dve.tensor_tensor(out=rest[:, :], in0=rest[:, :], in1=parts[:, par, :],
                                  op=ALU.subtract).then_inc(split1, 1)
            else:
                dve.wait_ge(split2, q * 4 + 3)
                lo = slice(2 * NBC, 3 * NBC)
                dve.tensor_tensor(out=rest[lo, :], in0=rest[lo, :], in1=parts[lo, par, :],
                                  op=ALU.subtract).then_inc(split1, 1)

        def residual(p, step):
            tiles = bass.ds(p * TT, TT)
            if step == 0:
                dve.wait_ge(fb_free, out_unit(p, 1) + 1)
                dve.scalar_tensor_tensor(out=xs[:, tiles, :], in0=xs[:, tiles, :], scalar=2.0,
                                         in1=otmp[:, :, :], op0=ALU.mult, op1=ALU.add).then_inc(z_steps, 1)
            elif step == 1:
                dve.wait_ge(z_steps, (p + 1) * 4 + 1)
                dve.tensor_tensor(out=xs[:, tiles, :], in0=xs[:, tiles, :],
                                  in1=bob[:, :].rearrange("p (a n) -> p a n", a=1).to_broadcast([P, TT, D]),
                                  op=ALU.add).then_inc(z_steps, 1)
            elif step == 2:
                dve.wait_ge(z_steps, (p + 1) * 4 + 2)
                dve.sem_inc(z_seen, 1)
                for j in range(TT):
                    ins = dve.bn_stats(bst[:, j, :], xs[:, bass.ds(p * TT + j, 1), :])
                ins.then_inc(z_steps, 1)
            elif step == 3:
                dve.wait_ge(z_steps, (p + 1) * 4 + 3)
                if not (isinstance(p, int) and p == 0):
                    dve.wait_ge(mv_kept, p)
                dve.sem_inc(z_seen, 1)
                for j in range(TT):
                    ins = dve.bn_aggr(mvt[:, j, :], bst[:, j, :])
                ins.then_inc(z_steps, 1)
            else:
                dve.wait_ge(z_steps, (p + 1) * 4 + 4)
                dve.tensor_copy(mv1[:, tiles, :], mvt[:, :, :]).then_inc(mv_kept, 1)

        def scan(p, n, par):
            i = p * NS + n
            dve.wait_ge(u_ready, i + 1)
            for c in range(CT):
                for b in range(2):
                    ins = dve.tensor_tensor_scan(
                        out=h[:, n % HRING, c, b * S:(b + 1) * S],
                        data0=alog[:, c, n:n + 1].to_broadcast([P, S]),
                        data1=h[:, n % HRING, c, b * S:(b + 1) * S],
                        initial=0.0, op0=ALU.mult, op1=ALU.add)
            ins.then_inc(h_ready, 1)

        def times_c(p, n):
            i = p * NS + n
            dve.wait_ge(h_ready, i + 1)
            dve.wait_ge(c_kept, i + 1)
            dve.tensor_tensor(out=h[:, n % HRING, :, :], in0=h[:, n % HRING, :, :],
                              in1=cring[:, n % CRING:n % CRING + 1, :].to_broadcast([P, CT, TP]),
                              op=ALU.mult).then_inc(hc_ready, 1)

        def gate(p):
            dve.wait_ge(fb_free, gate_unit(p, CT - 1) + 1)
            for c in range(CT):
                dve.wait_ge(y_done, p * CT + c + 1)
                dve.tensor_tensor(out=gs[:, c, :], in0=y[:, c, :], in1=gs[:, c, :], op=ALU.mult).then_inc(gated, 1)

        def pair(p, par, last, before, after):
            for n in range(NS):
                scan(p, n, par)
                if n == 1 and before:
                    gate(p - 1)
                if n:
                    times_c(p, n - 1)
                if before and 3 <= n < 8:
                    residual(p - 1, n - 3)
                if after and n == 11:
                    split(p + 1, 1 - par, 0)
                if after and n == 12:
                    split(p + 1, 1 - par, 1)
            times_c(p, NS - 1)

        dve.wait_ge(xloaded[1], 16)
        first_norm(range(TT, NT), n)
        dve.wait_ge(adecay, 2)
        split(0, 0, 0)
        split(0, 0, 1)
        pair(0, 0, False, False, True)
        with dve.Fori(0, NPAIR // 2 - 1) as it:
            pair(it * 2 + 1, 1, False, True, True)
            pair(it * 2 + 2, 0, False, True, True)
        pair(NPAIR - 1, 1, True, True, False)
        gate(NPAIR - 1)
        for step in range(5):
            residual(NPAIR - 1, step)

    @block.scalar
    def _(act):
        rstd_scalar(act, tmpv, stats, rooted, 2 * TT, slice(0, TT))
        act.wait_ge(loaded, 16 * N_LOADS)
        act.activation(alog[:, :, :], alog[:, :, :], ACT.Exp).then_inc(adecay, 1)
        act.wait_ge(adecay, 1)
        act.activation(alog[:, :, :], alog[:, :, :], ACT.Exp, scale=-1.0).then_inc(adecay, 1)
        act.wait_ge(stats, 2 * TT + RSTD_STEPS)
        act.wait_ge(made, 3)

        def take(unit, out, fn, rows=P, **kw):
            bank = unit[1]
            act.wait_ge(fb_full, unit[0] + 1)
            act.activation(out, fb[bank][0:rows, :], fn, **kw).then_inc(fb_free, 1)

        def fu(q, par, k):
            return front_unit(q, k), bank_of(q, par, k)

        def normalise(q):
            for j in range(TT):
                tile = bass.ds(q * TT + j, 1)
                ins = act.activation(xn[:, j, :], xs[:, tile, :], ACT.Identity,
                                     scale=rstd[:, tile], bias=nbias[:, tile])
            ins.then_inc(xn_ready, 1)

        def keep_b(p, n):
            i = p * NS + n
            act.wait_ge(b_sent, i + 1)
            if not isinstance(i, int) or i >= BRING:
                act.wait_ge(u_ready, i - BRING + 1)
            act.activation(bring[:, n % BRING, :], bbank[:, :], ACT.Copy).then_inc(b_kept, 1)

        def keep_c(p, n):
            i = p * NS + n
            act.wait_ge(c_sent, i + 1)
            if not isinstance(i, int) or i >= CRING:
                act.wait_ge(hc_ready, i - CRING + 1)
            act.activation(cring[:, n % CRING, :], cbank[:, :], ACT.Copy).then_inc(c_kept, 1)

        def front(q, par, step):
            if step == 0:
                normalise(q)
                for k in range(DK):
                    take(fu(q, par, U_XT + k), xnT[:, k, :], ACT.Identity, scale=lnw[:, k:k + 1], bias=lnb[:, k:k + 1])
            elif step <= 2:
                for m in (2 * step - 2, 2 * step - 1):
                    act.wait_ge(fb_full, front_unit(q, U_WIN + m) + 1)
                    act.activation(xm[:, m, :, TAPS - 1:PADW], fb[bank_of(q, par, U_WIN + m)][:, :].rearrange("p (b s) -> p b s", b=2),
                                   ACT.Identity, bias=bin_[:, m:m + 1]).then_inc(fb_free, 1)
            elif step <= 6:
                if step == 3 and not (isinstance(q, int) and q < 2):
                    act.wait_ge(gated, (q - 1) * CT)
                c = step - 3
                take(fu(q, par, U_CONV + c), xc[:, par, c, :], ACT.Silu, bias=cb[:, c:c + 1])
            elif step == 7:
                if not (isinstance(q, int) and q == 0):
                    act.wait_ge(split2, q * 4)
                act.wait_ge(fb_full, front_unit(q, U_WX) + 1)
                act.activation(rest[:, :], fb[bank_of(q, par, U_WX)][0:3 * NBC, :], ACT.Identity,
                               bias=bx3[:, :]).then_inc(split2, 1)
                act.activation(parts[:, par, :], fb[bank_of(q, par, U_WX)][0:3 * NBC, :], ACT.Identity,
                               bias=bx3[:, :]).then_inc(split2, 1)
                act.wait_ge(split2, q * 4 + 2)
                act.sem_inc(fb_free, 1)
            elif step == 8:
                act.wait_ge(split1, q * 2 + 1)
                mid, lo = slice(NBC, 2 * NBC), slice(2 * NBC, 3 * NBC)
                act.activation(parts[mid, par, :], rest[mid, :], ACT.Copy)
                act.activation(parts[lo, par, :], rest[lo, :], ACT.Copy).then_inc(split2, 1)
            else:
                lo = slice(2 * NBC, 3 * NBC)
                act.wait_ge(split1, q * 2 + 2)
                act.activation(parts[lo, par, :], rest[lo, :], ACT.Copy).then_inc(split2, 1)

        def gate(p, par, half):
            for m in (2 * half, 2 * half + 1):
                take((gate_unit(p, m), gate_bank(p, par, m)), gs[:, m, :], ACT.Silu, bias=bin_[:, CT + m:CT + m + 1])

        def project_out(p, par):
            act.wait_ge(z_steps, p * 4 + 1)
            for k in range(U_OUT):
                act.wait_ge(fb_full, out_unit(p, k) + 1)
                act.activation(otmp[:, 2 * k:2 * k + 2, :],
                               fb[out_bank(p, par, k)][:, :].rearrange("p (a n) -> p a n", a=2),
                               ACT.Copy).then_inc(fb_free, 1)

        def pair(p, par, before, after):
            for n in range(NS):
                if n + BLEAD < NS:
                    keep_b(p, n + BLEAD)
                elif after:
                    keep_b(p + 1, n + BLEAD - NS)
                if n + CLEAD < NS:
                    keep_c(p, n + CLEAD)
                elif after:
                    keep_c(p + 1, n + CLEAD - NS)
                if before and n == 0:
                    project_out(p - 1, 1 - par)
                if 1 <= n < 3:
                    gate(p, par, n - 1)
                if after and 2 <= n < 12:
                    front(p + 1, 1 - par, n - 2)

        for step in range(7):
            front(0, 0, step)
        rstd_scalar(act, tmpv, stats, rooted, 2 * NT + RSTD_STEPS, slice(TT, NT))
        act.wait_ge(stats, 2 * NT + 2 * RSTD_STEPS)
        for step in range(7, 10):
            front(0, 0, step)
        for n in range(BLEAD):
            keep_b(0, n)
        for n in range(CLEAD):
            keep_c(0, n)
        pair(0, 0, False, True)
        with act.Fori(0, NPAIR // 2 - 1) as it:
            pair(it * 2 + 1, 1, True, True)
            pair(it * 2 + 2, 0, True, True)
        pair(NPAIR - 1, 1, True, False)
        project_out(NPAIR - 1, 1)

    @block.tensor
    def _(pe):
        pe.wait_ge(made, 7)

        def free_bank(unit):
            if not isinstance(unit, int) or unit >= 2:
                pe.wait_ge(fb_free, unit - 1)

        def front(q, par, step):
            if step == 0:
                pe.wait_ge(xn_ready, q + 1)
                for k in range(DK):
                    free_bank(front_unit(q, U_XT + k))
                    bank = fb[bank_of(q, par, U_XT + k)]
                    for j in range(TT):
                        ins = pe.transpose(bank[:, j * P:(j + 1) * P], xn[:, j, k * P:(k + 1) * P], ident[:, :])
                    ins.then_inc(fb_full, 1)
            elif step <= 2:
                pe.wait_ge(fb_free, front_unit(q, U_XT + DK - 1) + 1)
                for m in (2 * step - 2, 2 * step - 1):
                    free_bank(front_unit(q, U_WIN + m))
                    for k in range(DK):
                        ins = pe.matmul(fb[bank_of(q, par, U_WIN + m)][:, :], win[:, k, m * P:(m + 1) * P],
                                        xnT[:, k, :], start=(k == 0), stop=(k == DK - 1))
                    ins.then_inc(fb_full, 1)
            elif step <= 6:
                c = step - 3
                free_bank(front_unit(q, U_CONV + c))
                for k in range(TAPS):
                    ins = pe.matmul(fb[bank_of(q, par, U_CONV + c)][:, :].rearrange("p (b s) -> p b s", b=2),
                                    cdiag[:, c, k, :], xm[:, c, :, k:k + S],
                                    start=(k == 0), stop=(k == TAPS - 1))
                ins.then_inc(fb_full, 1)
            elif step == 7:
                pe.wait_ge(fb_free, front_unit(q, U_CONV + CT - 1) + 1)
                for c in range(CT):
                    ins = pe.matmul(fb[bank_of(q, par, U_WX)][0:3 * NBC, :], wx3[:, c, :], xc[:, par, c, :],
                                    start=(c == 0), stop=(c == CT - 1))
                ins.then_inc(fb_full, 1)

        def gate(p, par, half):
            for m in (2 * half, 2 * half + 1):
                free_bank(gate_unit(p, m))
                for k in range(DK):
                    ins = pe.matmul(fb[gate_bank(p, par, m)][:, :], win[:, k, (CT + m) * P:(CT + m + 1) * P],
                                    xnT[:, k, :], start=(k == 0), stop=(k == DK - 1))
                ins.then_inc(fb_full, 1)

        def project_out(p, par):
            pe.wait_ge(gated, (p + 1) * CT)
            for k in range(U_OUT):
                free_bank(out_unit(p, k))
                for a in range(2):
                    j = 2 * k + a
                    for c in range(CT):
                        ins = pe.matmul(fb[out_bank(p, par, k)][:, a * D:(a + 1) * D], gs[:, c, j * P:(j + 1) * P],
                                        wout[:, c, :], start=(c == 0), stop=(c == CT - 1))
                ins.then_inc(fb_full, 1)

        def send_b(p, par, n):
            i = p * NS + n
            if n == 0:
                pe.wait_ge(split2, p * 4 + 4)
            if not isinstance(i, int) or i >= 1:
                pe.wait_ge(b_kept, i)
            pe.matmul(bbank[:, :], sel[:, n, :], parts[:, par, :], start=True, stop=True).then_inc(b_sent, 1)

        def send_c(p, par, n):
            i = p * NS + n
            if not isinstance(i, int) or i >= 1:
                pe.wait_ge(c_kept, i)
            pe.matmul(cbank[:, :], sel[:, NS + n, :], parts[:, par, :], start=True, stop=True).then_inc(c_sent, 1)

        def add_up(p, n):
            if n - 1 in ADDED:
                return
            if n in ADDED:
                pe.wait_ge(added, p * len(ADDED) + ADDED.index(n) + 1)
            else:
                pe.wait_ge(hc_ready, p * NS + n + 1)
            for c in range(CT):
                ins = pe.matmul(y[:, c, :], ident[:, :], h[:, n % HRING, c, :], start=False, stop=(n == NS - 1))
                if n == NS - 1:
                    ins.then_inc(y_done, 1)
            if n == NS - 1:
                pe.wait_ge(y_done, (p + 1) * CT)
                pe.sem_inc(summed, 1)
            else:
                ins.then_inc(summed, 2 if n in ADDED else 1)

        def skip(p, par):
            for c in range(CT):
                if not (isinstance(p, int) and p == 0):
                    pe.wait_ge(gated, (p - 1) * CT + c + 1)
                pe.matmul(y[:, c, :], ddiag[:, c, :], xc[:, par, c, :], start=True, stop=False)

        def pair(p, par, before, after):
            for n in range(NS):
                if n + BLEAD < NS:
                    send_b(p, par, n + BLEAD)
                elif after:
                    send_b(p + 1, 1 - par, n + BLEAD - NS)
                if n + CLEAD < NS:
                    send_c(p, par, n + CLEAD)
                elif after:
                    send_c(p + 1, 1 - par, n + CLEAD - NS)
                if n == 0:
                    skip(p, par)
                for m in range(NS):
                    if SUM_STEP[m] == n:
                        add_up(p, m)
                if before and n == 0:
                    project_out(p - 1, 1 - par)
                if 1 <= n < 3:
                    gate(p, par, n - 1)
                if after and 2 <= n < 10:
                    front(p + 1, 1 - par, n - 2)
            for m in range(NS):
                if SUM_STEP[m] >= NS:
                    add_up(p, m)

        for step in range(8):
            if step == 1:
                pe.wait_ge(loaded, 16 * N_LOADS)
            if step == 3:
                pe.wait_ge(tables, 1)
            front(0, 0, step)
        for n in range(BLEAD):
            send_b(0, 0, n)
        for n in range(CLEAD):
            send_c(0, 0, n)
        pair(0, 0, False, True)
        with pe.Fori(0, NPAIR // 2 - 1) as it:
            pair(it * 2 + 1, 1, True, True)
            pair(it * 2 + 2, 0, True, True)
        pair(NPAIR - 1, 1, True, False)
        project_out(NPAIR - 1, 1)

def bank_of(q, par, k):
    return front_unit(q if isinstance(q, int) else par + 2, k) % 2

def gate_bank(p, par, k):
    return gate_unit(p if isinstance(p, int) else par, k) % 2

def out_bank(p, par, k):
    return out_unit(p if isinstance(p, int) else par, k) % 2

RSTD_STEPS = 7

def rstd_scalar(act, tmpv, stats, rooted, n, cols=slice(0, NT)):
    act.wait_ge(stats, n + 1)
    act.activation(tmpv[:, 1, cols], tmpv[:, 0, cols], ACT.Sqrt).then_inc(rooted, 1)

def rstd_vector(dve, mv, rstd, nbias, tmpv, stats, rooted, n, cols=slice(0, NT), turn=1):
    var, root, a, b = (tmpv[:, k, cols] for k in range(4))
    at = n

    def link(ins):
        nonlocal at
        at += 1
        ins.then_inc(stats, 1)
        dve.wait_ge(stats, at)

    link(dve.tensor_scalar(var, mv[:, cols, 1], EPS, None, ALU.add))
    dve.wait_ge(rooted, turn)
    link(dve.reciprocal(a, root))
    link(dve.tensor_tensor(out=b, in0=a, in1=a, op=ALU.mult))
    link(dve.tensor_tensor(out=b, in0=b, in1=var, op=ALU.mult))
    link(dve.tensor_scalar(b, b, -0.5, 1.5, ALU.mult, ALU.add))
    link(dve.tensor_tensor(out=rstd[:, cols], in0=a, in1=b, op=ALU.mult))
    link(dve.scalar_tensor_tensor(out=nbias[:, cols], in0=mv[:, cols, 0], scalar=-1.0, in1=rstd[:, cols],
                                  op0=ALU.mult, op1=ALU.mult))
    return at

HEADS, DH, KEYS = 16, 64, 77
INNER = HEADS * DH
MT = INNER // P
JT = S // P
SBANKS = [(0, 6), (6, 11), (11, 16)]
NSB = len(SBANKS)
KCHUNK = 6
TH = 4
NTB = HEADS // TH
GB = 3
G_O, G_OUT, G_V, G_Q = MT // 2, JT, INNER // 512, MT // 2
G_BACK, G_FRONT = G_O + G_OUT, G_V + G_Q
G_ALL = G_BACK + G_FRONT
T_ALL = 1 + JT * NTB
T_BEFORE = 2
MASKED = -1e30
fp16 = mybir.dt.float16
WSCALE = 16.0

def gfront(b, k):
    if isinstance(b, int) and b == 0:
        return k
    return b * G_ALL - G_BACK + k

def gback(b, k):
    last = isinstance(b, int) and b == B - 1
    return (b + 1) * G_ALL + k - (G_FRONT if last else 0)

def gbank(k):
    return k % GB

def txunit(b):
    return 0 if isinstance(b, int) and b == 0 else (b - 1) * T_ALL + 1 + T_BEFORE

def tpunit(b, k):
    last = isinstance(b, int) and b == B - 1
    return b * T_ALL + 1 + k + (0 if last or k < T_BEFORE else 1)

def tx_bank(b, par):
    return txunit(b if isinstance(b, int) else par + 2) % 2

def tp_bank(b, par, k):
    return tpunit(b if isinstance(b, int) else par, k) % 2

def all_but_low(pe, out, pairs):
    n, of = 0, 3 * len(pairs)
    for left, right in pairs:
        for a, b in ((0, 0), (0, 1), (1, 0)):
            ins = pe.matmul(out, left(a), right(b), start=(n == 0), stop=(n == of - 1))
            n += 1
    return ins

assert G_FRONT % GB == 0 and G_BACK % GB == 0 and T_ALL % 2 == 1 and B % 2 == 0

def attention(nc, ctx, t):
    def sb(name, shape, dt=fp32):
        return ctx.enter_context(nc.sbuf_tensor(name, shape, dt))

    def sem(name):
        return ctx.enter_context(nc.semaphore(name))

    xs, ident, mv0, mv1, rstd, nbias, tmpv = t["xs"], t["ident"], t["mv0"], t["mv1"], t["rstd"], t["nbias"], t["tmpv"]
    wqh, wql = sb("wqh", [P, DK, INNER], fp16), sb("wql", [P, DK, INNER], fp16)
    wvh, wvl = sb("wvh", [P, DK, INNER], fp16), sb("wvl", [P, DK, INNER], fp16)
    woh, wol = sb("woh", [P, MT, D], fp16), sb("wol", [P, MT, D], fp16)
    bo = sb("bo", [P, D])
    cxTh, cxTl = sb("cxTh", [P, DK, B * KEYS], fp16), sb("cxTl", [P, DK, B * KEYS], fp16)
    kT = sb("kT", [P, MT, B * KEYS])
    v = sb("v", [KEYS, 2, INNER])
    x1 = sb("x1", [P, 2, JT, D])
    xTh, xTl = sb("xTh", [P, DK, S], fp16), sb("xTl", [P, DK, S], fp16)
    q = sb("q", [P, 2, 2, MT, S])
    mrow8 = sb("mrow8", [1, B * KEYS // 4], u32)
    mrow = sb("mrow", [P, B * KEYS], bf16)
    first = sb("first", [P, P], bf16)
    nmax = sb("nmax", [P, JT, HEADS])
    rsum = sb("rsum", [P, JT, HEADS])
    rinv = sb("rinv", [P, JT, HEADS])
    pr = sb("pr", [P, JT, HEADS, KEYS])
    pn = sb("pn", [P, JT, HEADS, KEYS])
    pT = sb("pT", [KEYS, HEADS, S])
    oT = sb("oT", [P, 2, MT, S], fp16)
    bst = sb("bst2", [P, JT, 6])
    mvt = sb("mvt2", [P, JT, 2])
    assert (B, D) == (HEADS, S) and MT * S == DK * INNER
    cx = pT[:, :, :]
    wkh, wkl = (oT[:, i, :, :].rearrange("p (k m) s -> p k (m s)", k=DK) for i in range(2))
    wk32, wv32 = (q[:, 0, i, :, :].rearrange("p (k m) s -> p k (m s)", k=DK) for i in range(2))
    wq32 = pr[:, :, :, :].rearrange("p j h k -> p (j h k)")[:, 0:DK * INNER].rearrange("p (k n) -> p k n", k=DK)
    wo32 = pn[:, :, :, :].rearrange("p j h k -> p (j h k)")[:, 0:MT * D].rearrange("p (m d) -> p m d", m=MT)
    sc = ctx.enter_context(nc.psum_tensor("sc", [P, NSB, 512], fp32))
    tb = [ctx.enter_context(nc.psum_tensor(f"tb{i}", [P, TH * P], fp32)) for i in range(2)]
    g = [ctx.enter_context(nc.psum_tensor(f"g{i}", [P, 512], fp32)) for i in range(GB)]

    loaded = [sem(f"a_loaded{i}") for i in range(4)]
    stats = sem("a_stats")
    rooted = sem("a_rooted")
    const = sem("a_const")
    maskrow = sem("a_maskrow")
    high = sem("a_high")
    low = sem("a_low")
    xl_ready = sem("a_xl")
    halves = sem("a_halves")
    p_full = sem("a_p_full")
    p_free = sem("a_p_free")
    p_low = sem("a_p_low")
    x1_ready = sem("a_x1")
    g_full = sem("a_g_full")
    g_free = sem("a_g_free")
    s_full = sem("a_s_full")
    maxed = sem("a_maxed")
    exped = sem("a_exped")
    inverted = sem("a_inverted")
    pn_ready = sem("a_pn")
    t_full = sem("a_t_full")
    t_free = sem("a_t_free")
    z_steps = sem("a_z")
    z_seen = sem("a_z_seen")
    mv_kept = sem("a_mv_kept")

    zero_made = sem("a_zero_made")
    zero_sent = sem("a_zero_sent")
    zero = sb("zero", [P, D])

    KB = [(a, min(a + KCHUNK, B)) for a in range(0, B, KCHUNK)]
    XPB = 3
    XB = [(a, min(a + XPB, B)) for a in range(0, B, XPB)]
    NX = len(XB)
    WK_AFTER = 8

    weights = [((loaded[1], 16), wk32, wkh, wkl), ((loaded[2], 32), wq32, wqh, wql),
               ((loaded[3], 48), wv32, wvh, wvl), ((loaded[3], 48), wo32, woh, wol)]

    def high_half(act, i):
        (arrived, n), w32, hi, _ = weights[i]
        act.wait_ge(arrived, n)
        act.activation(hi[:, :, :], w32, ACT.Copy, scale=WSCALE).then_inc(high, 1)

    def low_half(dve, i):
        _, w32, hi, lo = weights[i]
        dve.wait_ge(high, i + 1)
        dve.scalar_tensor_tensor(out=lo[:, :, :], in0=w32, scalar=WSCALE, in1=hi[:, :, :],
                                 op0=ALU.mult, op1=ALU.subtract).then_inc(low, 1)

    with nc.Block() as block:
        @block.sync
        def _(sp):
            sp.dma_start(cx, t["ctx"].rearrange("b k d -> k b d")).then_inc(loaded[0], 16)
            wkv = t["Wkv"].rearrange("(k p) n -> p k n", p=P)
            sp.dma_start(wk32, wkv[:, :, 0:INNER]).then_inc(loaded[1], 16)
            sp.dma_start(wv32, wkv[:, :, INNER:2 * INNER]).then_inc(loaded[3], 16)
            sp.dma_start(wq32, t["Wq"].rearrange("(k p) n -> p k n", p=P)).then_inc(loaded[2], 16)
            sp.dma_start(mrow8[:, :], t["mask"].rearrange("(a n) -> a n", a=1)).then_inc(loaded[2], 16)
            sp.dma_start(wo32, t["Wout"].rearrange("(k p) n -> p k n", p=P)).then_inc(loaded[3], 16)
            sp.dma_start(bo[:, :], t["b_out"].rearrange("(a n) -> a n", a=1).to_broadcast([P, D])).then_inc(loaded[3], 16)

        @block.gpsimd
        def _(pool):
            pool.memset(zero[:, :], 0.0).then_inc(zero_made, 1)
            pool.memset(first[:, :], 0.0).then_inc(const, 1)
            pool.memset(mrow[:, :], 0.0).then_inc(const, 1)
            pool.wait_ge(const, 1)
            pool.memset(first[0:1, :], 1.0).then_inc(const, 1)
            pool.wait_ge(low, 4)
            pool.memset(q[:, :, :, :, :], 0.0).then_inc(const, 1)

        @block.vector
        def _(dve):
            rstd_vector(dve, mv1, rstd, nbias, tmpv, stats, rooted, 0)
            unit = 0
            for a, e in XB:
                if unit == WK_AFTER:
                    low_half(dve, 0)
                for k in range(DK):
                    dve.wait_ge(p_free, unit + 1)
                    dve.tensor_tensor(out=cxTl[:, k, a * KEYS:e * KEYS], in0=g[unit % 2][:, 0:(e - a) * KEYS],
                                      in1=cxTh[:, k, a * KEYS:e * KEYS], op=ALU.subtract).then_inc(p_low, 1)
                    unit += 1
            dve.wait_ge(loaded[2], 32)
            dve.wait_ge(const, 2)
            dve.tensor_scalar(mrow[0:1, :], mrow8[:, :].bitcast(mybir.dt.uint8), MASKED, None, ALU.mult).then_inc(maskrow, 1)
            for i in range(1, len(weights)):
                low_half(dve, i)

        @block.scalar
        def _(act):
            rstd_scalar(act, tmpv, stats, rooted, 0)
            unit = 0
            for a, e in XB:
                if unit == WK_AFTER:
                    high_half(act, 0)
                for k in range(DK):
                    act.wait_ge(p_full, unit + 1)
                    act.activation(cxTh[:, k, a * KEYS:e * KEYS], g[unit % 2][:, 0:(e - a) * KEYS], ACT.Copy).then_inc(p_free, 1)
                    unit += 1
            for m in range(MT):
                if m in (1, 3, 5):
                    high_half(act, (m + 1) // 2)
                for a, e in KB:
                    act.wait_ge(p_full, unit + 1)
                    act.activation(kT[:, m, a * KEYS:e * KEYS], g[unit % 2][:, 0:(e - a) * KEYS], ACT.Copy,
                                   scale=1 / WSCALE).then_inc(p_free, 1)
                    unit += 1

        @block.tensor
        def _(pe):
            pe.wait_ge(loaded[0], 16)
            unit = 0
            for a, e in XB:
                for k in range(DK):
                    if unit >= 2:
                        pe.wait_ge(p_low, unit - 1)
                    for b in range(a, e):
                        ins = pe.transpose(g[unit % 2][:, (b - a) * KEYS:(b - a + 1) * KEYS],
                                           cx[:, b, k * P:(k + 1) * P], ident[0:KEYS, 0:KEYS])
                    ins.then_inc(p_full, 1)
                    unit += 1
            pe.wait_ge(low, 1)
            pe.wait_ge(p_low, NX * DK)
            for m in range(MT):
                for a, e in KB:
                    if unit >= NX * DK + 2:
                        pe.wait_ge(p_free, unit - 1)
                    ins = all_but_low(pe, g[unit % 2][:, 0:(e - a) * KEYS],
                                      [(lambda half, k=k: (wkh, wkl)[half][:, k, m * P:(m + 1) * P],
                                        lambda half, k=k: (cxTh, cxTl)[half][:, k, a * KEYS:e * KEYS]) for k in range(DK)])
                    ins.then_inc(p_full, 1)
                    unit += 1

    block = ctx.enter_context(nc.Block())

    def batches(eng, body):
        body(0, 0, False, True)
        with eng.Fori(0, B // 2 - 1) as it:
            body(it * 2 + 1, 1, True, True)
            body(it * 2 + 2, 0, True, True)
        body(B - 1, 1, True, False)

    @block.sync
    def _(sp):
        sp.wait_ge(zero_made, 1)
        zeroed = t["ysum"].rearrange("(n p) d -> p n d", p=P)
        sp.dma_start(zeroed, zero[:, :].rearrange("p (a d) -> p a d", a=1).to_broadcast([P, zeroed.shape[1], D])).then_inc(zero_sent, 16)
        sp.wait_ge(zero_sent, 16)

    @block.gpsimd
    def _(pool):
        def norm_p(b, j):
            pool.wait_ge(inverted, 2 * b + j + 1)
            if not (isinstance(b, int) and b == 0):
                pool.wait_ge(t_full, tpunit(b - 1, (j + 1) * NTB - 1) + 1)
            pool.tensor_tensor(out=pn[:, j, :, :], in0=pr[:, j, :, :],
                               in1=rinv[:, j, :].rearrange("p (h a) -> p h a", a=1).to_broadcast([P, HEADS, KEYS]),
                               op=ALU.mult).then_inc(pn_ready, 1)

        def batch(b, par, before, after):
            norm_p(b, 0)
            norm_p(b, 1)

        batches(pool, batch)

    @block.vector
    def _(dve):
        def maxima(b, j):
            for i, (a, e) in enumerate(SBANKS):
                dve.wait_ge(s_full, (2 * b + j) * NSB + i + 1)
                dve.tensor_reduce(nmax[:, j, a:e], sc[:, i, 0:(e - a) * KEYS].rearrange("p (h k) -> p h k", k=KEYS),
                                  axis=AX.X, op=ALU.max, negate=True).then_inc(maxed, 1)

        def invert(b, j):
            dve.wait_ge(exped, (2 * b + j + 1) * NSB)
            dve.reciprocal(rinv[:, j, :], rsum[:, j, :]).then_inc(inverted, 1)

        def front_v(b, par, i):
            dve.wait_ge(g_full, gfront(b, i) + 1)
            dve.tensor_scalar(v[:, par, i * 512:(i + 1) * 512], g[gbank(i)][0:KEYS, :], 1 / WSCALE, None, ALU.mult).then_inc(g_free, 1)

        def front_q(b, par):
            for i in range(G_Q):
                bank = g[gbank(G_V + i)]
                dve.wait_ge(g_full, gfront(b, G_V + i) + 1)
                for o in range(2):
                    rows = slice(o * DH, (o + 1) * DH)
                    ins = dve.tensor_scalar(q[rows, par, o, 2 * i:2 * i + 2, :], bank[rows, :].rearrange("p (m s) -> p m s", m=2),
                                            DH ** -0.5 / WSCALE, None, ALU.mult)
                ins.then_inc(g_free, 1)

        def front_x(b, par):
            dve.wait_ge(t_free, txunit(b) + 1)
            dve.tensor_tensor(out=xTl[:, :, :], in0=tb[tx_bank(b, par)][:, :].rearrange("p (k s) -> p k s", k=DK),
                              in1=xTh[:, :, :], op=ALU.subtract).then_inc(xl_ready, 1)

        def outputs(b):
            for i in range(G_O):
                dve.wait_ge(g_full, gback(b, i) + 1)
                bank = g[gbank(i)][:, :].rearrange("p (m s) -> p m s", m=2)
                dve.tensor_copy(oT[:, 0, 2 * i:2 * i + 2, :], bank).then_inc(halves, 1)
                dve.wait_ge(halves, b * G_O + i + 1)
                dve.tensor_tensor(out=oT[:, 1, 2 * i:2 * i + 2, :], in0=bank, in1=oT[:, 0, 2 * i:2 * i + 2, :],
                                  op=ALU.subtract).then_inc(g_free, 1)

        def residual(b, par, j):
            dve.wait_ge(g_full, gback(b, G_O + j) + 1)
            dve.scalar_tensor_tensor(out=xs[:, bass.ds(b * JT + j, 1), :], in0=g[gbank(G_O + j)][:, 0:D].rearrange("p (a d) -> p a d", a=1),
                                     scalar=1 / WSCALE, in1=x1[:, par, j:j + 1, :], op0=ALU.mult, op1=ALU.add).then_inc(g_free, 1)

        def statistics(b):
            tiles = bass.ds(b * JT, JT)
            dve.wait_ge(g_free, gback(b, G_BACK - 1) + 1)
            dve.tensor_tensor(out=xs[:, tiles, :], in0=xs[:, tiles, :],
                              in1=bo[:, :].rearrange("p (a n) -> p a n", a=1).to_broadcast([P, JT, D]),
                              op=ALU.add).then_inc(z_steps, 1)
            dve.wait_ge(z_steps, 3 * b + 1)
            dve.sem_inc(z_seen, 1)
            for j in range(JT):
                ins = dve.bn_stats(bst[:, j, :], xs[:, bass.ds(b * JT + j, 1), :])
            ins.then_inc(z_steps, 1)
            dve.wait_ge(z_steps, 3 * b + 2)
            if not (isinstance(b, int) and b == 0):
                dve.wait_ge(mv_kept, b)
            dve.sem_inc(z_seen, 1)
            for j in range(JT):
                ins = dve.bn_aggr(mvt[:, j, :], bst[:, j, :])
            ins.then_inc(z_steps, 1)
            dve.wait_ge(z_steps, 3 * b + 3)
            dve.tensor_copy(mv0[:, tiles, :], mvt[:, :, :]).then_inc(mv_kept, 1)

        def batch(b, par, before, after):
            maxima(b, 0)
            if before:
                outputs(b - 1)
            invert(b, 0)
            maxima(b, 1)
            if before:
                residual(b - 1, 1 - par, 0)
            invert(b, 1)
            if before:
                residual(b - 1, 1 - par, 1)
                statistics(b - 1)
            if after:
                front_v(b + 1, 1 - par, 0)
                front_x(b + 1, 1 - par)
                front_v(b + 1, 1 - par, 1)
                front_q(b + 1, 1 - par)

        dve.wait_ge(loaded[3], 48)
        front_v(0, 0, 0)
        front_x(0, 0)
        front_v(0, 0, 1)
        front_q(0, 0)
        batches(dve, batch)
        outputs(B - 1)
        for j in range(JT):
            residual(B - 1, 1, j)
        statistics(B - 1)

    @block.scalar
    def _(act):
        def exps(b, j):
            if not (isinstance(b, int) and b == 0):
                act.wait_ge(pn_ready, 2 * (b - 1) + j + 1)
            for i, (a, e) in enumerate(SBANKS):
                act.wait_ge(maxed, (2 * b + j) * NSB + i + 1)
                for hd in range(a, e):
                    ins = act.activation(pr[:, j, hd, :], sc[:, i, (hd - a) * KEYS:(hd - a + 1) * KEYS], ACT.Exp,
                                         bias=nmax[:, j, hd:hd + 1], accum_out=rsum[:, j, hd:hd + 1])
                ins.then_inc(exped, 1)

        def probabilities(b, par, units):
            for k in units:
                j, kk = divmod(k, NTB)
                act.wait_ge(t_full, tpunit(b, k) + 1)
                act.activation(pT[:, kk * TH:(kk + 1) * TH, j * P:(j + 1) * P],
                               tb[tp_bank(b, par, k)][0:KEYS, :].rearrange("p (h s) -> p h s", h=TH), ACT.Copy).then_inc(t_free, 1)

        def norm_x(b, par):
            if not (isinstance(b, int) and b < 2):
                act.wait_ge(g_free, gback(b - 2, G_BACK - 1) + 1)
            for j in range(JT):
                tile = bass.ds(b * JT + j, 1)
                ins = act.activation(x1[:, par, j, :], xs[:, tile, :], ACT.Identity, scale=rstd[:, tile], bias=nbias[:, tile])
            ins.then_inc(x1_ready, 1)

        def front_x(b, par):
            act.wait_ge(t_full, txunit(b) + 1)
            act.activation(xTh[:, :, :], tb[tx_bank(b, par)][:, :].rearrange("p (k s) -> p k s", k=DK), ACT.Copy).then_inc(t_free, 1)

        def batch(b, par, before, after):
            exps(b, 0)
            exps(b, 1)
            if after:
                norm_x(b + 1, 1 - par)
            probabilities(b, par, range(T_BEFORE))
            if after:
                front_x(b + 1, 1 - par)
            probabilities(b, par, range(T_BEFORE, JT * NTB))

        norm_x(0, 0)
        front_x(0, 0)
        batches(act, batch)

    @block.tensor
    def _(pe):
        def free_bank(unit):
            if not isinstance(unit, int) or unit >= GB:
                pe.wait_ge(g_free, unit - GB + 1)

        def free_tbank(unit):
            if not isinstance(unit, int) or unit >= 2:
                pe.wait_ge(t_free, unit - 1)

        def scores(b, j, par):
            keys = bass.ds(b * KEYS, KEYS)
            for i, (a, e) in enumerate(SBANKS):
                if j == 0:
                    pe.wait_ge(g_free, gfront(b, G_V + (e - 1) // 4) + 1)
                if not (isinstance(b, int) and b == 0 and j == 0):
                    pe.wait_ge(exped, (2 * b + j - 1) * NSB + i + 1)
                mask = mrow[:, keys].rearrange("p (a k) -> p a k", a=1).to_broadcast([P, e - a, KEYS])
                pe.matmul(sc[:, i, 0:(e - a) * KEYS].rearrange("p (h k) -> p h k", k=KEYS), first[:, :], mask, start=True, stop=False)
                for hd in range(a, e):
                    ins = pe.matmul(sc[:, i, (hd - a) * KEYS:(hd - a + 1) * KEYS], q[:, par, hd % 2, hd // 2, j * P:(j + 1) * P],
                                    kT[:, hd // 2, keys], start=False, stop=(hd == e - 1))
                ins.then_inc(s_full, 1)

        def transposes(b, par, k):
            j, kk = divmod(k, NTB)
            if kk == 0:
                pe.wait_ge(pn_ready, 2 * b + j + 1)
            free_tbank(tpunit(b, k))
            if k == T_BEFORE + 1 and not (isinstance(b, int) and b == B - 1):
                pe.wait_ge(xl_ready, b + 2)
            for hd in range(TH):
                ins = pe.transpose(tb[tp_bank(b, par, k)][0:KEYS, hd * P:(hd + 1) * P], pn[:, j, kk * TH + hd, :], ident[:, :])
            ins.then_inc(t_full, 1)

        def front_v(b, par, i):
            free_bank(gfront(b, i))
            keys = bass.ds(b * KEYS, KEYS)
            ins = all_but_low(pe, g[gbank(i)][0:KEYS, :],
                              [(lambda half, k=k: (cxTh, cxTl)[half][:, k, keys],
                                lambda half, k=k: (wvh, wvl)[half][:, k, i * 512:(i + 1) * 512]) for k in range(DK)])
            ins.then_inc(g_full, 1)

        def front_x(b, par):
            pe.wait_ge(x1_ready, b + 1)
            free_tbank(txunit(b))
            for k in range(DK):
                for j in range(JT):
                    ins = pe.transpose(tb[tx_bank(b, par)][:, k * S + j * P:k * S + (j + 1) * P],
                                       x1[:, par, j, k * P:(k + 1) * P], ident[:, :])
            ins.then_inc(t_full, 1)

        def front_q(b, i):
            free_bank(gfront(b, G_V + i))
            if i == 0:
                pe.wait_ge(xl_ready, b + 1)
            for a in range(2):
                m = 2 * i + a
                ins = all_but_low(pe, g[gbank(G_V + i)][:, a * S:(a + 1) * S],
                                  [(lambda half, k=k: (wqh, wql)[half][:, k, m * P:(m + 1) * P],
                                    lambda half, k=k: (xTh, xTl)[half][:, k, :]) for k in range(DK)])
            ins.then_inc(g_full, 1)

        def outputs(b, par):
            pe.wait_ge(t_free, tpunit(b, JT * NTB - 1) + 1)
            for i in range(G_O):
                free_bank(gback(b, i))
                for hd in range(4 * i, 4 * i + 4):
                    m, o = hd // 2 - 2 * i, hd % 2
                    ins = pe.matmul(g[gbank(i)][o * DH:(o + 1) * DH, m * S:(m + 1) * S],
                                    v[:, par, hd * DH:(hd + 1) * DH], pT[:, hd, :], start=True, stop=True)
                ins.then_inc(g_full, 1)

        def project_out(b):
            pe.wait_ge(g_free, gback(b, G_O - 1) + 1)
            for j in range(JT):
                free_bank(gback(b, G_O + j))
                ins = all_but_low(pe, g[gbank(G_O + j)][:, 0:D],
                                  [(lambda half, m=m: oT[:, half, m, j * P:(j + 1) * P],
                                    lambda half, m=m: (woh, wol)[half][:, m, :]) for m in range(MT)])
                ins.then_inc(g_full, 1)

        def batch(b, par, before, after):
            scores(b, 0, par)
            if before:
                outputs(b - 1, 1 - par)
            scores(b, 1, par)
            if before:
                project_out(b - 1)
            if after:
                front_v(b + 1, 1 - par, 0)
            for k in range(T_BEFORE):
                transposes(b, par, k)
            if after:
                front_x(b + 1, 1 - par)
                front_v(b + 1, 1 - par, 1)
            k = T_BEFORE
            for i in range(G_Q):
                for _ in range(2 if i < 2 else 1):
                    transposes(b, par, k)
                    k += 1
                if after:
                    front_q(b + 1, i)

        assert (JT * NTB, T_BEFORE, G_Q) == (8, 2, 4)
        pe.wait_ge(loaded[3], 48)
        pe.wait_ge(low, 4)
        front_v(0, 0, 0)
        front_x(0, 0)
        front_v(0, 0, 1)
        for i in range(G_Q):
            front_q(0, i)
        batches(pe, batch)
        outputs(B - 1, 1)
        project_out(B - 1)

i32 = mybir.dt.int32

E, TOPK, H = 8, 2, 1024
HM = H // P
TS_LOG = 8
P_LOG = 7
TS = 1 << TS_LOG
SJ = TS // P
NTILES = (TOPK * B * S + E * (TS - 1)) // TS
NSLOT = NTILES * TS
POOL_LOW = 8
RG = 4
NCOL = NSLOT // P
NU = TOPK * NT
UG = 4
NTOK = B * S
HU = 2

def router(nc, ctx, t):
    def sb(name, shape, dt=fp32):
        return ctx.enter_context(nc.sbuf_tensor(name, shape, dt))

    def sem(name):
        return ctx.enter_context(nc.semaphore(name))

    xs, ident, mv0, rstd, nbias, tmpv = (t[k] for k in ("xs", "ident", "mv0", "rstd", "nbias", "tmpv"))
    w1h, w1l, w2h, w2l, b1s, b2s = (t[k] for k in ("w1h", "w1l", "w2h", "w2l", "b1s", "b2s"))
    x_row, y_row, gate_of, expert_of = t["x_row"], t["y_row"], t["gate_of"], t["expert_of"]
    stage = sb("stage", [P, 2, 2 * H])
    b2f, b2r = (w[0:1, E - 2:E].rearrange("p e k n -> p (e k n)").bitcast(fp32).rearrange("p (e d) -> p e d", e=E)
                for w in (w1l, w2l))
    wr = sb("wr", [P, DK, E])
    x2 = sb("x2", [P, 2, RG, D])
    x2T = sb("x2T", [P, DK, RG * P])
    lg = sb("lg", [P, NT, E])
    rev = sb("rev", [P, NT, E])
    tid = sb("tid", [1, NTILES, E])
    ones = sb("ones", [P, NT])
    lower = sb("lower", [P, P], bf16)
    allone = sb("allone", [P, P], bf16)
    hit = sb("hit", [P, TOPK, NT, E])
    w = [sb(f"w{i}", [P, NT, E]) for i in range(3)]
    chosen = sb("chosen", [P, NT, E], bf16)
    best = sb("best", [P, TOPK, NT])
    at = sb("at", [P, NT])
    small = sb("small", [P, 4, E])
    cnt = sb("cnt", [P, E], i32)
    fexp = sb("fexp", [1, NTILES])
    place = sb("place", [P, TOPK, NT], i32)
    part = sb("part", [P, 2, NU], i32)
    values = sb("values", [P, NU, 2])
    gates = values[:, :, 1].rearrange("p (k j) -> p k j", k=TOPK)
    lanes = sb("lanes", [P, P])
    spare = sb("spare", [P, NCOL])
    room = x2[:, :, :, :].rearrange("p a j d -> p (a j d)")
    used = 0

    def take(rows, n):
        nonlocal used
        used += n
        assert used <= 2 * RG * D
        return room[0:rows, used - n:used]

    chot = take(P, 4 * UG * NCOL).rearrange("p (a u k n) -> p a u k n", a=2, u=UG, k=2)
    partf = take(P, 2 * NU).rearrange("p (a n) -> p a n", a=2)
    rowf = take(P, NCOL)
    over = take(1, NTILES * E).rearrange("p (t e) -> p t e", e=E)
    assert 2 * UG * P == DK * RG * P
    rhot = x2T[:, :, :].rearrange("p k (u s) -> p k u s", u=UG)
    tp = [ctx.enter_context(nc.psum_tensor(f"tp{i}", [P, RG * P], fp32)) for i in range(2)]
    lp = [ctx.enter_context(nc.psum_tensor(f"lp{i}", [P, RG, E], fp32)) for i in range(2)]
    ranks = ctx.enter_context(nc.psum_tensor("ranks", [P, NT, E], fp32))
    totals = ctx.enter_context(nc.psum_tensor("totals", [P, NT, E], fp32))
    table = ctx.enter_context(nc.psum_tensor("table", [P, 2, NCOL], fp32))

    loaded = sem("r_loaded")
    b1_in, b2_in = sem("r_b1_in"), sem("r_b2_in")
    wstage = [sem(f"r_wstage{i}") for i in range(2)]
    whi = sem("r_whi")
    wlo = sem("r_wlo")
    wlo2 = sem("r_wlo2")
    stats = sem("r_stats")
    rooted = sem("r_rooted")
    const = sem("r_const")
    x2_ready = sem("r_x2")
    x2_out = [sem(f"r_x2_out{i}") for i in range(2)]
    t_full, t_free = sem("r_t_full"), sem("r_t_free")
    l_full, l_free = sem("r_l_full"), sem("r_l_free")
    steps = sem("r_steps")
    ranked = sem("r_ranked")
    chosen_ready = sem("r_chosen")
    gap = sem("r_gap")
    egap = sem("r_egap")
    hot = sem("r_hot")
    scaled = sem("r_scaled")
    hot_used = sem("r_hot_used")
    b2_zero = sem("r_b2_zero")
    b2_steps = sem("r_b2")

    NG = NT // RG
    x2d = t["x2d"].rearrange("(p j) d -> p j d", p=P)
    assert NG == E and TOPK * E == 2 * NG
    wviews = []
    for e in range(E):
        wviews.append((t["W1"][e].rearrange("(k p) n -> p k n", p=P), w1h[:, e, :, :], w1l[:, e, :, :], DK))
        wviews.append((t["W2"][e].rearrange("(m p) n -> p m n", p=P), w2h[:, e, :, :], w2l[:, e, :, :], HM))

    block = ctx.enter_context(nc.Block())

    @block.sync
    def _(sp):
        with nc.allow_non_contiguous_dma(reason="biases"):
            sp.dma_start(b2f, t["b2"].rearrange("(a e) n -> a e n", a=1)).then_inc(b2_in, 16)
            sp.dma_start(wr[:, :, :], t["Wr"].rearrange("(k p) n -> p k n", p=P)).then_inc(loaded, 16)
        for i, (src, _, _, k) in enumerate(wviews):
            if i >= 2:
                sp.wait_ge(whi, i - 1)
                if NG <= i - 2 < NG + POOL_LOW:
                    sp.wait_ge(wlo2, i - 1 - NG)
                else:
                    sp.wait_ge(wlo, i - 1 - (0 if i - 2 < NG else POOL_LOW))
            sp.dma_start(stage[:, i % 2, :].rearrange("p (k n) -> p k n", k=k), src).then_inc(wstage[i % 2], 16)
            if i == 1:
                with nc.allow_non_contiguous_dma(reason="biases"):
                    sp.dma_start(b1s[:, :, :], t["b1"].rearrange("e (m p) -> p e m", p=P)).then_inc(b1_in, 16)
        sp.wait_ge(b1_in, 16)

    @block.gpsimd
    def _(pool):
        pool.memset(b2s[:, :, :], 0.0).then_inc(b2_zero, 1)
        pool.iota(rev[:, :, :], pattern=[[0, NT], [-1, E]], base=E, channel_multiplier=0,
                  allow_small_or_imprecise_dtypes=True).then_inc(const, 1)
        pool.iota(tid[:, :, :], pattern=[[1, NTILES], [0, E]], base=0, channel_multiplier=0,
                  allow_small_or_imprecise_dtypes=True).then_inc(const, 1)
        pool.memset(ones[:, :], 1.0).then_inc(const, 1)
        pool.memset(lower[:, :], 0.0).then_inc(const, 1)
        pool.memset(allone[:, :], 1.0).then_inc(const, 1)
        pool.wait_ge(const, 5)
        pool.iota(values[:, :, 0].rearrange("p (k j) -> p k j", k=TOPK), pattern=[[0, TOPK], [1, NT]], base=1, channel_multiplier=NT,
                  allow_small_or_imprecise_dtypes=True).then_inc(const, 1)
        pool.iota(lanes[:, :], pattern=[[1, P]], base=0, channel_multiplier=0,
                  allow_small_or_imprecise_dtypes=True).then_inc(const, 1)
        pool.iota(spare[:, :].rearrange("p (t j) -> p t j", j=SJ), pattern=[[0, NTILES], [P, SJ]], base=NTOK, channel_multiplier=1,
                  allow_small_or_imprecise_dtypes=True).then_inc(const, 1)
        pool.affine_select(out=lower[:, :], in_=lower[:, :], compare_op=ALU.is_ge, fill=1.0,
                           base=0, pattern=[[-1, P]], channel_multiplier=1).then_inc(const, 1)

        def keep_x2(g, par, uses):
            pool.wait_ge(x2_ready, g + 1)
            pool.dma_start(x2d[:, bass.ds(g * RG, RG), :], x2[:, par, :, :]).then_inc(x2_out[par], 16)

        with pool.Fori(0, NG // 2) as it:
            keep_x2(it * 2, 0, it)
            keep_x2(it * 2 + 1, 1, it)
        pool.wait_ge(b2_steps, 3)
        for i, (src, hi, lo, k) in enumerate(wviews[NG:NG + POOL_LOW]):
            pool.wait_ge(whi, NG + i + 1)
            pool.tensor_tensor(out=lo, in0=stage[:, i % 2, :].rearrange("p (k n) -> p k n", k=k), in1=hi,
                               op=ALU.subtract).then_inc(wlo2, 1)
        pool.wait_ge(wlo2, POOL_LOW)
        for par in range(2):
            pool.wait_ge(x2_out[par], 16 * (NG // 2))

    @block.scalar
    def _(act):
        rstd_scalar(act, tmpv, stats, rooted, 0)
        act.wait_ge(stats, RSTD_STEPS)

        def normalise(g, par, uses):
            if not (isinstance(g, int) and g < 2):
                act.wait_ge(x2_out[par], uses * 16)
                act.wait_ge(t_full, 2 * (g - 1))
            for j in range(RG):
                tile = bass.ds(g * RG + j, 1)
                ins = act.activation(x2[:, par, j, :], xs[:, tile, :], ACT.Identity, scale=rstd[:, tile], bias=nbias[:, tile])
            ins.then_inc(x2_ready, 1)

        def high(par, e, uses):
            act.wait_ge(wstage[par], uses * 16 + 16)
            hi, k = ((w1h, DK), (w2h, HM))[par]
            act.activation(hi[:, bass.ds(e, 1), :, :].rearrange("p a k n -> p (a k) n"),
                           stage[:, par, :].rearrange("p (k n) -> p k n", k=k), ACT.Copy, scale=WSCALE).then_inc(whi, 1)

        def scaled_high(i):
            src, hi, lo, k = wviews[NG + i]
            w32 = stage[:, i % 2, :]
            act.wait_ge(wstage[i % 2], ((NG + i) // 2 + 1) * 16)
            act.activation(w32, w32, ACT.Copy, scale=WSCALE).then_inc(scaled, 1)
            act.wait_ge(scaled, i + 1)
            act.activation(hi, w32.rearrange("p (k n) -> p k n", k=k), ACT.Copy).then_inc(whi, 1)

        normalise(0, 0, 0)
        high(0, 0, 0)
        normalise(1, 1, 0)
        high(1, 0, 0)
        with act.Fori(1, NG // 2) as it:
            normalise(it * 2, 0, it)
            high(0, it, it)
            normalise(it * 2 + 1, 1, it)
            high(1, it, it)
        for i in range(2):
            scaled_high(i)
        act.wait_ge(gap, 1)
        act.activation(at[:, :], best[:, 0, :], ACT.Exp).then_inc(egap, 1)
        for i in range(2, POOL_LOW):
            scaled_high(i)
        for e in range((NG + POOL_LOW) // 2, E):
            for par in range(2):
                high(par, e, e)

    @block.tensor
    def _(pe):
        pe.wait_ge(loaded, 16)

        def group(g, par):
            pe.wait_ge(x2_ready, g + 1)
            for k in range(DK):
                if not (isinstance(g, int) and g == 0):
                    pe.wait_ge(t_free, 2 * g + k - 1)
                for j in range(RG):
                    ins = pe.transpose(tp[k][:, j * P:(j + 1) * P], x2[:, par, j, k * P:(k + 1) * P], ident[:, :])
                ins.then_inc(t_full, 1)
            pe.wait_ge(t_free, 2 * g + 2)
            if not (isinstance(g, int) and g < 2):
                pe.wait_ge(l_free, g - 1)
            for j in range(RG):
                for k in range(DK):
                    ins = pe.matmul(lp[par][:, j, :], x2T[:, k, j * P:(j + 1) * P], wr[:, k, :],
                                    start=(k == 0), stop=(k == DK - 1))
            ins.then_inc(l_full, 1)

        group(0, 0)
        group(1, 1)
        with pe.Fori(1, NG // 2) as it:
            group(it * 2, 0)
            group(it * 2 + 1, 1)
        pe.wait_ge(const, 9)
        pe.wait_ge(chosen_ready, 1)
        pe.matmul(ranks[:, :, :], lower[:, :], chosen[:, :, :], start=True, stop=True)
        pe.matmul(totals[:, :, :], allone[:, :], chosen[:, :, :], start=True, stop=True).then_inc(ranked, 1)

        def fill(n, par, start=False, stop=False):
            pe.wait_ge(hot, n + 1)
            for i in range(UG):
                ins = pe.matmul(table[:, :, :], rhot[:, par, i, :], chot[:, par, i, :, :],
                                start=(start and i == 0), stop=(stop and i == UG - 1))
            ins.then_inc(hot_used, 1)

        last = NU // UG
        fill(0, 0, start=True)
        fill(1, 1)
        with pe.Fori(1, last // 2 - 1) as it:
            fill(it * 2, 0)
            fill(it * 2 + 1, 1)
        fill(last - 2, 0)
        fill(last - 1, 1, stop=True)

    @block.vector
    def _(dve):
        rstd_vector(dve, mv0, rstd, nbias, tmpv, stats, rooted, 0)
        dve.wait_ge(b2_in, 16)
        dve.wait_ge(b2_zero, 1)
        dve.tensor_scalar(b2s[0:1, :, :], b2f, WSCALE, None, ALU.mult).then_inc(b2_steps, 1)
        dve.wait_ge(b2_steps, 1)
        dve.scalar_tensor_tensor(out=b2r, in0=b2f, scalar=WSCALE, in1=b2s[0:1, :, :],
                                 op0=ALU.mult, op1=ALU.subtract).then_inc(b2_steps, 1)
        dve.wait_ge(b2_steps, 2)
        dve.tensor_copy(b2s[32:33, :, :], b2r).then_inc(b2_steps, 1)

        def group(g, par):
            for k in range(DK):
                dve.wait_ge(t_full, 2 * g + k + 1)
                dve.tensor_copy(x2T[:, k, :], tp[k][:, :]).then_inc(t_free, 1)
            dve.wait_ge(l_full, g + 1)
            dve.tensor_copy(lg[:, bass.ds(g * RG, RG), :], lp[par][:, :, :]).then_inc(l_free, 1)

        def low(i, par, e):
            dve.wait_ge(whi, i + 1)
            hi, lo, k = ((w1h, w1l, DK), (w2h, w2l, HM))[par]
            dve.scalar_tensor_tensor(out=lo[:, bass.ds(e, 1), :, :].rearrange("p a k n -> p (a k) n"),
                                     in0=stage[:, par, :].rearrange("p (k n) -> p k n", k=k), scalar=WSCALE,
                                     in1=hi[:, bass.ds(e, 1), :, :].rearrange("p a k n -> p (a k) n"),
                                     op0=ALU.mult, op1=ALU.subtract).then_inc(wlo, 1)

        with dve.Fori(0, NG // 2) as it:
            group(it * 2, 0)
            low(it * 2, 0, it)
            group(it * 2 + 1, 1)
            low(it * 2 + 1, 1, it)
        dve.wait_ge(const, 9)
        dve.wait_ge(l_free, NG)
        for par in range(2):
            dve.wait_ge(x2_out[par], 16 * (NG // 2))
        n = 0

        def link(ins):
            nonlocal n
            n += 1
            ins.then_inc(steps, 1)
            dve.wait_ge(steps, n)

        def over_experts(v):
            return v.rearrange("p (j a) -> p j a", a=1).to_broadcast([P, NT, E])

        logits = lg
        for k in range(TOPK):
            link(dve.tensor_reduce(best[:, k, :], logits[:, :, :], axis=AX.X, op=ALU.max))
            link(dve.tensor_tensor(out=w[1][:, :, :], in0=logits[:, :, :], in1=over_experts(best[:, k, :]), op=ALU.is_equal))
            link(dve.tensor_tensor(out=w[1][:, :, :], in0=w[1][:, :, :], in1=rev[:, :, :], op=ALU.mult))
            link(dve.tensor_reduce(at[:, :], w[1][:, :, :], axis=AX.X, op=ALU.max))
            link(dve.tensor_tensor(out=hit[:, k, :, :], in0=rev[:, :, :], in1=over_experts(at[:, :]), op=ALU.is_equal))
            if k == 0:
                link(dve.scalar_tensor_tensor(out=w[0][:, :, :], in0=hit[:, 0, :, :], scalar=-3e38, in1=lg[:, :, :],
                                              op0=ALU.mult, op1=ALU.add))
                logits = w[0]
        dve.tensor_tensor(out=chosen[:, :, :], in0=hit[:, 0, :, :], in1=hit[:, 1, :, :], op=ALU.add).then_inc(chosen_ready, 1)
        link(dve.tensor_tensor(out=best[:, 0, :], in0=best[:, 1, :], in1=best[:, 0, :], op=ALU.subtract))
        dve.sem_inc(gap, 1)
        dve.wait_ge(egap, 1)
        link(dve.tensor_scalar(best[:, 1, :], at[:, :], 1.0, None, ALU.add))
        link(dve.reciprocal(gates[:, 0, :], best[:, 1, :]))
        link(dve.tensor_tensor(out=gates[:, 1, :], in0=gates[:, 0, :], in1=at[:, :], op=ALU.mult))
        dve.wait_ge(ranked, 1)
        upto = w[0][:, :, :].rearrange("p j e -> p (j e)").rearrange("p (e j) -> p e j", e=E)
        for e in range(E):
            ins = dve.tensor_tensor_scan(out=upto[:, e, :], data0=ones[:, :], data1=totals[:, :, e], initial=0.0,
                                         op0=ALU.mult, op1=ALU.add)
        link(ins)
        count, tiles, ends, base = (small[:, i, :] for i in range(4))
        link(dve.tensor_scalar(cnt[:, :], upto[:, :, NT - 1], float(TS - 1), None, ALU.add))
        link(dve.tensor_scalar(cnt[:, :], cnt[:, :], TS_LOG, None, ALU.logical_shift_right))
        link(dve.tensor_copy(tiles, cnt[:, :]))
        link(dve.tensor_tensor_scan(out=ends, data0=ones[:, 0:E], data1=tiles, initial=0.0, op0=ALU.mult, op1=ALU.add))
        link(dve.tensor_tensor(out=base, in0=ends, in1=tiles, op=ALU.subtract))
        link(dve.tensor_scalar(base, base, float(TS), None, ALU.mult))
        link(dve.tensor_tensor(out=w[1][:, :, :], in0=upto.rearrange("p e j -> p j e"), in1=totals[:, :, :], op=ALU.subtract))
        link(dve.tensor_tensor(out=w[2][:, :, :], in0=w[1][:, :, :], in1=ranks[:, :, :], op=ALU.add))
        link(dve.tensor_tensor(out=w[1][:, :, :], in0=w[2][:, :, :],
                               in1=base.rearrange("p (a e) -> p a e", a=1).to_broadcast([P, NT, E]), op=ALU.add))
        for k in range(TOPK):
            link(dve.tensor_tensor(out=w[2][:, :, :], in0=w[1][:, :, :], in1=hit[:, k, :, :], op=ALU.mult))
            link(dve.tensor_reduce(best[:, k, :], w[2][:, :, :], axis=AX.X, op=ALU.add))
            link(dve.tensor_copy(place[:, k, :], best[:, k, :]))
        slot = place[:, :, :].rearrange("p k j -> p (k j)")
        dve.tensor_scalar(part[:, 0, :], slot, P_LOG, None, ALU.logical_shift_right)
        link(dve.tensor_scalar(part[:, 1, :], slot, P - 1, None, ALU.bitwise_and))
        link(dve.tensor_copy(partf[:, :, :], part[:, :, :]))

        def one_hots(n, par):
            if not (isinstance(n, int) and n < 2):
                dve.wait_ge(hot_used, n - 1)
            rows = partf[:, 1, bass.ds(n * UG, UG)].rearrange("p (u a) -> p u a", a=1).to_broadcast([P, UG, P])
            dve.tensor_tensor(out=rhot[:, par, :, :], in0=lanes[:, :].rearrange("p (a s) -> p a s", a=1).to_broadcast([P, UG, P]),
                              in1=rows, op=ALU.is_equal)
            for i in range(UG):
                u = bass.ds(n * UG + i, 1)
                ins = dve.scalar_tensor_tensor(
                    out=chot[:, par, i, :, :], in0=lanes[:, 0:NCOL].rearrange("p (a c) -> p a c", a=1).to_broadcast([P, 2, NCOL]),
                    scalar=partf[:, 0, u], in1=values[:, u, :].rearrange("p a (k c) -> p (a k) c", c=1).to_broadcast([P, 2, NCOL]),
                    op0=ALU.is_equal, op1=ALU.mult)
            ins.then_inc(hot, 1)

        one_hots(0, 0)
        one_hots(1, 1)
        with dve.Fori(1, NU // UG // 2) as it:
            one_hots(it * 2, 0)
            one_hots(it * 2 + 1, 1)
        dve.wait_ge(hot_used, NU // UG)
        link(dve.tensor_copy(gate_of[:, :], table[:, 1, :]))
        link(dve.scalar_tensor_tensor(out=rowf[:, :], in0=table[:, 0, :], scalar=0.0, in1=spare[:, :], op0=ALU.is_equal, op1=ALU.mult))
        link(dve.tensor_scalar(x_row[:, :], table[:, 0, :], -1.0, 0.0, ALU.add, ALU.max))
        link(dve.scalar_tensor_tensor(out=y_row[:, :], in0=x_row[:, :], scalar=1.0, in1=rowf[:, :], op0=ALU.mult, op1=ALU.add))
        link(dve.tensor_tensor(out=over[:, :, :], in0=tid[:, :, :],
                               in1=ends[0:1, :].rearrange("p (a e) -> p a e", a=1).to_broadcast([1, NTILES, E]), op=ALU.is_ge))
        link(dve.tensor_reduce(fexp[:, :], over[:, :, :], axis=AX.X, op=ALU.add))
        link(dve.tensor_scalar(expert_of[:, :], fexp[:, :], float(E - 1), None, ALU.min))
        for e in range((NG + POOL_LOW) // 2, E):
            for par in range(2):
                low(2 * e + par, par, e)
        dve.wait_ge(wlo, 2 * E - POOL_LOW)

def experts(nc, ctx, t):
    def sb(name, shape, dt=fp32):
        return ctx.enter_context(nc.sbuf_tensor(name, shape, dt))

    def sem(name):
        return ctx.enter_context(nc.semaphore(name))

    ident, w1h, w1l, w2h, w2l, b1s, b2s, expert_of = (t[k] for k in ("ident", "w1h", "w1l", "w2h", "w2l", "b1s", "b2s", "expert_of"))
    NHU = HM // HU
    STORE_LAG = 4
    xs, x_row, y_row, gate_of = (t[k] for k in ("xs", "x_row", "y_row", "gate_of"))
    x_at = sb("x_at", [P, 2, SJ], i32)
    y_at = sb("y_at", [P, 2, SJ], i32)
    xt = sb("xt", [P, 2, SJ, D])
    xh = sb("xh", [P, 2, DK, TS], fp16)
    xl = sb("xl", [P, 2, DK, TS], fp16)
    act32 = sb("act32", [P, 2, HU, TS])
    hh = sb("hh", [P, 2, HM, TS], fp16)
    hl = sb("hl", [P, 2, HM, TS], fp16)
    ys = sb("ys", [P, 2, SJ, D])
    brow = sb("brow", [P, P], fp16)
    hp = [ctx.enter_context(nc.psum_tensor(f"hp{i}", [P, HU * TS], fp32)) for i in range(4)]
    xp = ctx.enter_context(nc.psum_tensor("xp", [P, DK * TS], fp32))
    yp = [ctx.enter_context(nc.psum_tensor(f"yp{i}", [P, SJ * D], fp32)) for i in range(2)]

    x_in = [sem(f"e_x_in{i}") for i in range(2)]
    const = sem("e_const")
    xp_full = sem("e_xp_full")
    xh_ready, xl_ready = sem("e_xh"), sem("e_xl")
    h_full = sem("e_h_full")
    g_ready = sem("e_g")
    hh_ready = sem("e_hh")
    hl_ready = sem("e_hl")
    y_full = sem("e_y_full")
    y_ready = sem("e_y")
    y_out = sem("e_y_out")
    x_found, y_found = sem("e_x_found"), sem("e_y_found")
    seen = sem("e_seen")
    x2_back = sem("e_x2_back")
    block = ctx.enter_context(nc.Block())

    def tiles(eng, body, apart=2):
        for t in range(apart):
            body(t, t % 2, t // 2)
        with eng.Fori(apart // 2, NTILES // 2) as it:
            body(it * 2, 0, it)
            body(it * 2 + 1, 1, it)
        if NTILES % 2:
            body(NTILES - 1, 0, NTILES // 2)

    t_x2d, t_sum = t["x2d"], t["ysum"]

    def late(t, n=1):
        return not isinstance(t, int) or t >= n

    @block.sync
    def _(sp):
        sp.wait_ge(xp_full, 4)
        sp.dma_start(xs[:, :, :], t["x2d"].rearrange("(p j) d -> p j d", p=P)).then_inc(x2_back, 16)
        sp.wait_ge(x2_back, 16)

    @block.gpsimd
    def _(pool):
        pool.memset(brow[:, :], 0.0).then_inc(const, 1)
        pool.wait_ge(const, 1)
        pool.memset(brow[0:1, :], 1.0).then_inc(const, 1)
        pool.memset(brow[32:33, :], 1.0).then_inc(const, 1)

        pool.wait_ge(const, 3)

        def load(t, par):
            if late(t, 2):
                pool.wait_ge(xp_full, t - 1)
                pool.sem_inc(seen, 1)
            pool.tensor_copy(x_at[:, par, :], x_row[:, bass.ds(t * SJ, SJ)]).then_inc(x_found, 1)
            pool.wait_ge(x_found, t + 1)
            pool.sem_inc(seen, 1)
            for j in range(SJ):
                pool.indirect_dma_start(xt[:, par, j, :], None, t_x2d,
                                        bass.IndirectOffsetOnAxis(ap=x_at[:, par, j:j + 1], axis=0)).then_inc(x_in[par], 16)

        def add(t, par):
            pool.wait_ge(y_ready, t + 1)
            if late(t):
                pool.wait_ge(y_out, t * SJ * 16)
            pool.sem_inc(seen, 1)
            pool.tensor_copy(y_at[:, par, :], y_row[:, bass.ds(t * SJ, SJ)]).then_inc(y_found, 1)
            pool.wait_ge(y_found, t + 1)
            pool.sem_inc(seen, 1)
            for j in range(SJ):
                pool.indirect_dma_start(t_sum, bass.IndirectOffsetOnAxis(ap=y_at[:, par, j:j + 1], axis=0),
                                        ys[:, par, j, :], None, compute_op=ALU.add).then_inc(y_out, 16)

        def tile(t, par, uses):
            load(t, par)
            if late(t, STORE_LAG):
                add(t - STORE_LAG, par)

        tiles(pool, tile, STORE_LAG)
        for t in range(NTILES - STORE_LAG, NTILES):
            add(t, t % 2)
        pool.wait_ge(y_out, 16 * SJ * NTILES)

    @block.scalar
    def _(act):
        def take_x(t, par):
            act.wait_ge(xp_full, t + 1)
            if late(t, 2):
                act.wait_ge(h_full, (t - 1) * NHU)
            act.activation(xh[:, par, :, :], xp[:, :].rearrange("p (k s) -> p k s", k=DK), ACT.Copy).then_inc(xh_ready, 1)

        def hidden(t, par):
            e = act.value_load(expert_of[0:1, bass.ds(t, 1)] , min_val=0, max_val=E - 1)
            for i in range(NHU):
                act.wait_ge(h_full, t * NHU + i + 1)
                if late(t * NHU + i, 2) if isinstance(t, int) else True:
                    act.wait_ge(hl_ready, t * NHU + i - 1)
                if late(t, 2):
                    act.wait_ge(y_full, t - 1)
                for a in range(HU):
                    m = i * HU + a
                    bias = b1s[:, bass.ds(e, 1), m]
                    pre = hp[i % 4][:, a * TS:(a + 1) * TS]
                    ins = act.activation(act32[:, i % 2, a, :], pre, ACT.Gelu, bias=bias, scale=1 / WSCALE)
                ins.then_inc(g_ready, 1)
                for a in range(HU):
                    m = i * HU + a
                    bias = b1s[:, bass.ds(e, 1), m]
                    pre = hp[i % 4][:, a * TS:(a + 1) * TS]
                    ins = act.activation(hh[:, par, m, :], pre, ACT.Gelu, bias=bias, scale=1 / WSCALE)
                ins.then_inc(hh_ready, 1)

        def tile(t, par, uses):
            hidden(t, par)
            if not (isinstance(t, int) and t == NTILES - 1):
                take_x(t + 1, 1 - par)

        take_x(0, 0)
        tiles(act, tile)

    @block.vector
    def _(dve):
        def take_x(t, par):
            dve.wait_ge(xh_ready, t + 1)
            if late(t, 2):
                dve.wait_ge(h_full, (t - 1) * NHU)
            dve.tensor_tensor(out=xl[:, par, :, :], in0=xp[:, :].rearrange("p (k s) -> p k s", k=DK),
                              in1=xh[:, par, :, :], op=ALU.subtract).then_inc(xl_ready, 1)

        def hidden(t, par):
            for i in range(NHU):
                dve.wait_ge(hh_ready, t * NHU + i + 1)
                if late(t, 2):
                    dve.wait_ge(y_full, t - 1)
                dve.tensor_tensor(out=hl[:, par, i * HU:(i + 1) * HU, :], in0=act32[:, i % 2, :, :],
                                  in1=hh[:, par, i * HU:(i + 1) * HU, :], op=ALU.subtract).then_inc(hl_ready, 1)

        def output(t, par, uses):
            dve.wait_ge(y_full, t + 1)
            if late(t, 2):
                dve.wait_ge(y_out, (t - 1) * SJ * 16)
            for j in range(SJ):
                ins = dve.tensor_scalar(ys[:, par, j, :], yp[par][:, j * D:(j + 1) * D], gate_of[:, bass.ds(t * SJ + j, 1)],
                                        1 / WSCALE, ALU.mult, ALU.mult)
            ins.then_inc(y_ready, 1)

        def tile(t, par, uses):
            hidden(t, par)
            if not (isinstance(t, int) and t == NTILES - 1):
                take_x(t + 1, 1 - par)
            if late(t):
                output(t - 1, 1 - par, uses - 1 + par)

        take_x(0, 0)
        tiles(dve, tile)
        output(NTILES - 1, (NTILES - 1) % 2, (NTILES - 1) // 2)

    @block.tensor
    def _(pe):
        def transpose(t, par, uses):
            pe.wait_ge(x_in[par], (uses + 1) * SJ * 16)
            if late(t):
                pe.wait_ge(xl_ready, t)
            for k in range(DK):
                for j in range(SJ):
                    ins = pe.transpose(xp[:, k * TS + j * P:k * TS + (j + 1) * P], xt[:, par, j, k * P:(k + 1) * P], ident[:, :])
            ins.then_inc(xp_full, 1)

        def hidden(t, par):
            e = pe.value_load(expert_of[0:1, bass.ds(t, 1)], min_val=0, max_val=E - 1)
            pe.wait_ge(xl_ready, t + 1)
            for i in range(NHU):
                if late(t * NHU + i, 4) if isinstance(t, int) else True:
                    pe.wait_ge(hh_ready, t * NHU + i - 3)
                for a in range(HU):
                    m = i * HU + a
                    n = 0
                    for k in range(DK):
                        for wt, xx in ((w1h, xh), (w1h, xl), (w1l, xh)):
                            ins = pe.matmul(hp[i % 4][:, a * TS:(a + 1) * TS],
                                            wt[:, bass.ds(e, 1), k, m * P:(m + 1) * P], xx[:, par, k, :],
                                            start=(n == 0), stop=(n == 3 * DK - 1))
                            n += 1
                ins.then_inc(h_full, 1)

        def output(t, par):
            e = pe.value_load(expert_of[0:1, bass.ds(t, 1)], min_val=0, max_val=E - 1)
            pe.wait_ge(hl_ready, (t + 1) * NHU)
            if late(t, 2):
                pe.wait_ge(y_ready, t - 1)
            for j in range(SJ):
                out = yp[par][:, j * D:(j + 1) * D]
                pe.matmul(out, brow[:, :], b2s[:, bass.ds(e, 1), :], start=True, stop=False)
                for m in range(HM):
                    for hx, wt in ((hh, w2h), (hh, w2l), (hl, w2h)):
                        ins = pe.matmul(out, hx[:, par, m, j * P:(j + 1) * P], wt[:, bass.ds(e, 1), m, :], start=False,
                                        stop=(m == HM - 1 and hx is hl))
            ins.then_inc(y_full, 1)

        def tile(t, par, uses):
            hidden(t, par)
            if not (isinstance(t, int) and t == NTILES - 1):
                transpose(t + 1, 1 - par, uses + par)
            if late(t):
                output(t - 1, 1 - par)

        pe.wait_ge(const, 3)
        transpose(0, 0, 0)
        tiles(pe, tile)
        output(NTILES - 1, (NTILES - 1) % 2)

CG = 8

def combine(nc, ctx, t):
    def sb(name, shape, dt=fp32):
        return ctx.enter_context(nc.sbuf_tensor(name, shape, dt))

    def sem(name):
        return ctx.enter_context(nc.semaphore(name))

    xs, mv, rstd, nbias, tmpv = (t[k] for k in ("xs", "mv0", "rstd", "nbias", "tmpv"))
    NG = NT // CG
    yk = sb("yk", [P, NT, D])
    res = sb("res", [P, NT, D])
    bst = sb("bst3", [P, NT, 6])
    got = [sem(f"c_got{i}") for i in range(NG)]
    steps = sem("c_steps")
    rooted = sem("c_rooted")
    done = sem("c_done")
    out_sent = sem("c_out_sent")
    added = sem("c_added")
    PER = 2 + RSTD_STEPS
    block = ctx.enter_context(nc.Block())

    @block.gpsimd
    def _(pool):
        for g in range(NG):
            cols = slice(g * CG, (g + 1) * CG)
            pool.wait_ge(got[g], 16)
            pool.tensor_tensor(out=xs[:, cols, :], in0=xs[:, cols, :], in1=yk[:, cols, :], op=ALU.add).then_inc(added, 1)

    @block.vector
    def _(dve):
        for g in range(NG):
            cols = slice(g * CG, (g + 1) * CG)
            dve.wait_ge(added, g + 1)
            for j in range(g * CG, (g + 1) * CG):
                ins = dve.bn_stats(bst[:, j, :], xs[:, j, :])
            ins.then_inc(steps, 1)
            dve.wait_ge(steps, g * PER + 1)
            for j in range(g * CG, (g + 1) * CG):
                ins = dve.bn_aggr(mv[:, j, :], bst[:, j, :])
            ins.then_inc(steps, 1)
            dve.wait_ge(steps, g * PER + 2)
            rstd_vector(dve, mv, rstd, nbias, tmpv, steps, rooted, g * PER + 2, cols, g + 1)

    @block.scalar
    def _(act):
        for g in range(NG):
            rstd_scalar(act, tmpv, steps, rooted, g * PER + 2, slice(g * CG, (g + 1) * CG))
            act.wait_ge(steps, (g + 1) * PER)
            for j in range(g * CG, (g + 1) * CG):
                ins = act.activation(res[:, j, :], xs[:, j, :], ACT.Identity, scale=rstd[:, j:j + 1], bias=nbias[:, j:j + 1])
            ins.then_inc(done, 1)

    @block.sync
    def _(sp):
        sums = t["ysum"][0:NTOK, :].rearrange("(p j) d -> p j d", p=P)
        for g in range(NG):
            sp.dma_start(yk[:, g * CG:(g + 1) * CG, :], sums[:, g * CG:(g + 1) * CG, :]).then_inc(got[g], 16)
        ov = t["out"].rearrange("b (h p) d -> p (b h) d", p=P)
        for g in range(NG):
            sp.wait_ge(done, g + 1)
            sp.dma_start(ov[:, g * CG:(g + 1) * CG, :], res[:, g * CG:(g + 1) * CG, :]).then_inc(out_sent, 16)
        sp.wait_ge(out_sent, 16 * NG)

def decoder_layer(nc, a, out):
    def part(prefix):
        return {k[len(prefix):]: v for k, v in a.items() if k.startswith(prefix)}

    with ExitStack() as ctx:
        def sb(name, shape, dt=fp32):
            return ctx.enter_context(nc.sbuf_tensor(name, shape, dt))

        t = {
            "xs": sb("xs", [P, NT, D]),
            "ident": sb("ident", [P, P]),
            "mv0": sb("mv0", [P, NT, 2]),
            "mv1": sb("mv1", [P, NT, 2]),
            "rstd": sb("rstd", [P, NT]),
            "nbias": sb("nbias", [P, NT]),
            "tmpv": sb("tmpv", [P, 4, NT]),
            "x_row": sb("x_row", [P, NCOL], i32),
            "y_row": sb("y_row", [P, NCOL], i32),
            "gate_of": sb("gate_of", [P, NCOL]),
            "expert_of": sb("expert_of", [1, NTILES], i32),
            "x2d": nc.dram_tensor("x2d", [NTOK, D], fp32, kind="Internal").ap(),
            "ysum": nc.dram_tensor("ysum", [NTOK + SJ * P, D], fp32, kind="Internal").ap(),
            "out": out,
        }
        with ExitStack() as stage:
            mixer(nc, stage, t | part("L0_attn_") | {"x": a["x"]})
        with ExitStack() as stage:
            attention(nc, stage, t | part("L0_xattn_") | {"ctx": a["ctx_1024"], "mask": a["mask_BxS2_bk0"]})
        with ExitStack() as weights:
            def wsb(name, shape, dt=fp16):
                return weights.enter_context(nc.sbuf_tensor(name, shape, dt))

            tw = t | part("L0_ffn_") | {
                "w1h": wsb("w1h", [P, E, DK, H]), "w1l": wsb("w1l", [P, E, DK, H]),
                "w2h": wsb("w2h", [P, E, HM, D]), "w2l": wsb("w2l", [P, E, HM, D]),
                "b1s": wsb("b1s", [P, E, HM], fp32), "b2s": wsb("b2s", [P, E, D]),
            }
            with ExitStack() as stage:
                router(nc, stage, tw)
            with ExitStack() as stage:
                experts(nc, stage, tw)
        with ExitStack() as stage:
            combine(nc, stage, t)

_INS = ["x", "ctx_1024", "mask_BxS2_bk0"] + [
    "L0_attn_" + n for n in ("ln_w", "ln_b", "W_in", "b_in", "conv_w", "conv_b", "A_log", "D", "W_x", "b_x", "W_out", "b_out")
] + ["L0_xattn_" + n for n in ("Wq", "Wkv", "Wout", "b_out")] + ["L0_ffn_" + n for n in ("Wr", "W1", "b1", "W2", "b2")]

def kernel(**inputs):
    import numpy as _np
    import concourse.bacc as _bacc
    from concourse import mybir as _mybir
    from concourse.bass_utils import run_bass_kernel_spmd as _run

    nc = _bacc.Bacc("TRN2", target_bir_lowering=False, num_devices=1)
    arrays, aps = {}, {}
    for name in _INS:
        a = _np.ascontiguousarray(inputs[name])
        if a.dtype.kind == "b":
            a = a.reshape(-1).view(_np.uint32)
        arrays[f"in_{name}"] = a
        aps[name] = nc.dram_tensor(f"in_{name}", a.shape, _mybir.dt.from_np(a.dtype), kind="ExternalInput").ap()
    out = nc.dram_tensor("out_0", (B, S, D), fp32, kind="ExternalOutput").ap()
    decoder_layer(nc, aps, out)
    r = _run(nc, [arrays], core_ids=[0])
    return _np.asarray(r.results[0]["out_0"])
```
